# Optimizing a Trainium2 kernel written in Bass

```python
import numpy as np
import jax
import jax.numpy as jnp

def _softmax(x, axis=-1):
    return jax.nn.softmax(x, axis=axis)

def _gelu(x):
    return jax.nn.gelu(x, approximate=True)

def _silu(x):
    return jax.nn.silu(x)

def _sigmoid(x):
    return jax.nn.sigmoid(x)

def _layernorm(x, axis=-1, eps=1e-05):
    m = jnp.mean(x, axis=axis, keepdims=True)
    v = jnp.var(x, axis=axis, keepdims=True)
    return (x - m) / jnp.sqrt(v + eps)

def _scatter_add(tgt, idx, src, axis=0):
    return tgt.at[idx].add(src)

def _segment_sum(src, seg, n):
    return jax.ops.segment_sum(src, seg, n)
kernel_name = 'mk_xattn_ffn_d4_seqx_r8_c1802b'

def setup_inputs(seed: int=0):
    np.random.seed(seed)
    _w = jnp.asarray

    def _rec_inputs():
        import jax
        import jax.numpy as jnp
        _rk = jax.random.key(seed)
        x = -0.000125 + 0.9999 * jax.random.normal(jax.random.fold_in(_rk, 1), (8, 128, 256), jnp.float32)
        _lenS = 128 - jax.random.randint(jax.random.fold_in(_rk, 7), (8,), 0, max(1, 128 // 4) + 1, jnp.int32)
        _lenS2 = 128 - jax.random.randint(jax.random.fold_in(_rk, 8), (8,), 0, max(1, 128 // 4) + 1, jnp.int32)
        _ctx_2048P = jax.random.normal(jax.random.fold_in(_rk, 11), (8, 16, 256), jnp.float32)
        _ctx_2048c = jax.random.dirichlet(jax.random.fold_in(_rk, 511), 0.3 * jnp.ones((16,), jnp.float32), (8, 128))
        _ctx_2048t = jnp.einsum('bsk,bkd->bsd', _ctx_2048c, _ctx_2048P)
        _ctx_2048t = _ctx_2048t * jax.lax.rsqrt(jnp.mean(jnp.square(_ctx_2048t)) + 1e-12) * 0.953939
        ctx_2048 = 0.00139358 + 0.999369 * (_ctx_2048t + 0.3 * jax.random.normal(jax.random.fold_in(_rk, 611), (8, 128, 256), jnp.float32))
        _validS = jnp.arange(128)[None, :] < _lenS[:, None]
        _validS2 = jnp.arange(128)[None, :] < _lenS2[:, None]
        _causal = jnp.tril(jnp.ones((128, 128), dtype=bool))
        mask_BxS2_bk0 = jnp.logical_not(jnp.broadcast_to(_validS2[:, :], (8, 128)))
        return (x, ctx_2048, mask_BxS2_bk0)
    x, ctx_2048, mask_BxS2_bk0 = _rec_inputs()

    def _L0_xattn_setup():
        import jax, jax.numpy as jnp
        import numpy as np
        key = jax.random.key(seed)
        k = jax.random.split(key, 6)
        B, S, D, NKV = (4, 512, 256, 64)
        inv = D ** (-0.5)
        return {'x': jax.random.normal(k[0], (B, S, D), jnp.float32), 'W_qkv': jax.random.normal(k[1], (3 * D, D), jnp.float32) * inv, 'W_o': jax.random.normal(k[2], (D, D), jnp.float32) * inv, 'beta_q': jnp.array(1.0, jnp.float32), 'beta_k': jnp.array(1.0, jnp.float32), 'gate': jnp.array(0.0, jnp.float32), 'log_tau': jnp.array(0.0, jnp.float32), 'K_mem': jax.random.normal(k[3], (B, NKV, D), jnp.float32), 'V_mem': jax.random.normal(k[4], (B, NKV, D), jnp.float32), 'clip_k': 54}
    _L0_xattn_all = _L0_xattn_setup()
    _L0_xattn_in = {k: v for k, v in _L0_xattn_all.items() if k in ('W_qkv', 'W_o', 'beta_q', 'beta_k', 'gate', 'log_tau')}
    del _L0_xattn_all

    def _L0_ffn_setup():
        import jax, jax.numpy as jnp
        import numpy as np
        K = 2

        def gelu(v):
            return jax.nn.gelu(v, approximate=False)
        key = jax.random.key(seed)
        ks = jax.random.split(key, 10)
        B, S, D, H, E = (4, 256, 256, 128, 8)
        SH = 2 * H
        u = lambda k_, shape, b: jax.random.uniform(k_, shape, jnp.float32, -b, b)
        return {'x': jax.random.normal(ks[0], (B, S, D), jnp.float32), 'gate_w': u(ks[1], (D, E), 1.0 / D), 'w1': u(ks[2], (E, D, H), 1.0 / D), 'b1': u(ks[3], (E, H), 1.0 / np.sqrt(D)), 'w2': u(ks[4], (E, H, D), 1.0 / H), 'b2': u(ks[5], (E, D), 1.0 / np.sqrt(H)), 'shared_w1': u(ks[6], (D, SH), 1.0 / D), 'shared_b1': u(ks[7], (SH,), 1.0 / np.sqrt(D)), 'shared_w2': u(ks[8], (SH, D), 1.0 / SH), 'shared_b2': u(ks[9], (D,), 1.0 / np.sqrt(SH))}
    _L0_ffn_all = _L0_ffn_setup()
    _L0_ffn_in = {k: v for k, v in _L0_ffn_all.items() if k in ('gate_w', 'w1', 'b1', 'w2', 'b2', 'shared_w1', 'shared_b1', 'shared_w2', 'shared_b2')}
    del _L0_ffn_all

    def _L1_xattn_setup():
        import jax, jax.numpy as jnp
        import numpy as np
        DIM = 256
        NHEADS = 32
        HEAD_DIM = DIM // NHEADS
        EPS = 1e-06

        def _rmsnorm(t):
            return t * jax.lax.rsqrt(jnp.mean(t * t, axis=-1, keepdims=True) + EPS)
        key = jax.random.key(seed)
        kx, kc, kq, kk, kv = jax.random.split(key, 5)
        x = jax.random.normal(kx, (2, 512, DIM), dtype=jnp.float32)
        context = jax.random.normal(kc, (2, 64, DIM), dtype=jnp.float32)
        std = 0.02
        Wq = jax.random.normal(kq, (DIM, DIM), dtype=jnp.float32) * std
        Wk = jax.random.normal(kk, (DIM, DIM), dtype=jnp.float32) * std
        Wv = jax.random.normal(kv, (DIM, DIM), dtype=jnp.float32) * std
        return {'x': x, 'context': context, 'Wq': Wq, 'Wk': Wk, 'Wv': Wv}
    _L1_xattn_all = _L1_xattn_setup()
    _L1_xattn_in = {k: v for k, v in _L1_xattn_all.items() if k in ('Wq', 'Wk', 'Wv')}
    del _L1_xattn_all

    def _L1_ffn_setup():
        import jax, jax.numpy as jnp
        import numpy as np
        B, S, H = (2, 256, 256)
        E, I, K = (8, 176, 2)
        SHARED_I = 176 * 2

        def _moe_forward(hidden_states, gate_w, w1, w3, w2, sw1, sw3, sw2):
            x = hidden_states.reshape(-1, H)
            T = x.shape[0]
            logits = x @ gate_w.T
            scores = jax.nn.softmax(logits, axis=-1)
            topk_w, topk_idx = jax.lax.top_k(scores, K)
            topk_w = topk_w / jnp.sum(topk_w, axis=-1, keepdims=True)
            h = jnp.einsum('th,ehi->eti', x, w1)
            g = jnp.einsum('th,ehi->eti', x, w3)
            y_all = jnp.einsum('eti,eih->eth', jax.nn.silu(h) * g, w2)
            tok = jnp.arange(T)[:, None]
            y_sel = y_all[topk_idx, tok]
            y = jnp.sum(y_sel * topk_w[..., None], axis=1)
            shared = jax.nn.silu(x @ sw1) * (x @ sw3) @ sw2
            return (y + shared).reshape(hidden_states.shape)
        key = jax.random.key(seed)
        ks = jax.random.split(key, 8)
        s = 0.02
        return {'hidden_states': jax.random.normal(ks[0], (B, S, H), jnp.float32), 'gate_w': jax.random.normal(ks[1], (E, H), jnp.float32) * s, 'w1': jax.random.normal(ks[2], (E, H, I), jnp.float32) * s, 'w3': jax.random.normal(ks[3], (E, H, I), jnp.float32) * s, 'w2': jax.random.normal(ks[4], (E, I, H), jnp.float32) * s, 'sw1': jax.random.normal(ks[5], (H, SHARED_I), jnp.float32) * s, 'sw3': jax.random.normal(ks[6], (H, SHARED_I), jnp.float32) * s, 'sw2': jax.random.normal(ks[7], (SHARED_I, H), jnp.float32) * s}
    _L1_ffn_all = _L1_ffn_setup()
    _L1_ffn_in = {k: v for k, v in _L1_ffn_all.items() if k in ('gate_w', 'w1', 'w3', 'w2', 'sw1', 'sw3', 'sw2')}
    del _L1_ffn_all

    def _L2_xattn_setup():
        import jax, jax.numpy as jnp
        import numpy as np
        key = jax.random.key(seed)
        k1, k2, k3 = jax.random.split(key, 3)
        B, S, D, M = (8, 256, 256, 128)
        hidden_states = jax.random.normal(k1, (B, S, D), dtype=jnp.float32)
        memory_tokens = jax.random.normal(k2, (B, M, D), dtype=jnp.float32)
        memory_mask = jax.random.randint(k3, (B, M), 0, 2).astype(jnp.bool_)
        return {'hidden_states': hidden_states, 'memory_tokens': memory_tokens, 'memory_mask': memory_mask}
    _L2_xattn_all = _L2_xattn_setup()
    _L2_xattn_in = {k: v for k, v in _L2_xattn_all.items() if k in ()}
    del _L2_xattn_all

    def _L2_ffn_setup():
        import jax, jax.numpy as jnp
        import numpy as np
        from jax import lax
        B, S, H = (1, 256, 256)
        E, I, TOP_K = (64, 64, 8)
        SHARED_I = 64
        key = jax.random.key(seed)
        ks = jax.random.split(key, 8)
        sc = 0.02
        return {'hidden_states': jax.random.normal(ks[0], (B, S, H), jnp.float32), 'router_w': jax.random.normal(ks[1], (E, H), jnp.float32) * sc, 'gate_up_proj': jax.random.normal(ks[2], (E, 2 * I, H), jnp.float32) * sc, 'down_proj': jax.random.normal(ks[3], (E, H, I), jnp.float32) * sc, 'shared_gate_w': jax.random.normal(ks[4], (SHARED_I, H), jnp.float32) * sc, 'shared_up_w': jax.random.normal(ks[5], (SHARED_I, H), jnp.float32) * sc, 'shared_down_w': jax.random.normal(ks[6], (H, SHARED_I), jnp.float32) * sc, 'shared_expert_gate_w': jax.random.normal(ks[7], (1, H), jnp.float32) * sc}
    _L2_ffn_all = _L2_ffn_setup()
    _L2_ffn_in = {k: v for k, v in _L2_ffn_all.items() if k in ('router_w', 'gate_up_proj', 'down_proj', 'shared_gate_w', 'shared_up_w', 'shared_down_w', 'shared_expert_gate_w')}
    del _L2_ffn_all

    def _L3_xattn_setup():
        import jax, jax.numpy as jnp
        import numpy as np
        B, S, DIM, HD = (4, 128, 256, 128)
        H = DIM // HD
        GN_EPS = 0.001

        def _decay_masks(n_heads, seq_len):
            gam = 1.0 - 2.0 ** (-5.0 - jnp.arange(n_heads, dtype=jnp.float32))
            idx = jnp.arange(seq_len, dtype=jnp.float32)
            expo = idx[None, :] - idx[:, None]
            D = jnp.where(expo[None, :, :] <= 0, gam[:, None, None] ** expo[None, :, :], 0.0)
            return D / jnp.sqrt(D.sum(axis=-1))[:, None, :]
        key = jax.random.key(seed)
        ks = jax.random.split(key, 8)
        x = jax.random.normal(ks[0], (B, S, DIM), dtype=jnp.float32)
        k = jax.random.normal(ks[1], (B, S, DIM), dtype=jnp.float32)
        v = jax.random.normal(ks[2], (B, S, DIM), dtype=jnp.float32)
        Wh = jax.random.normal(ks[3], (H, HD, HD), dtype=jnp.float32) / np.sqrt(HD)
        wg_w = jax.random.normal(ks[4], (DIM, DIM), dtype=jnp.float32) / np.sqrt(DIM)
        wo_w = jax.random.normal(ks[5], (DIM, DIM), dtype=jnp.float32) / np.sqrt(DIM)
        gn_gamma = jnp.ones((DIM,), dtype=jnp.float32)
        gn_beta = jnp.zeros((DIM,), dtype=jnp.float32)
        return {'x': x, 'k': k, 'v': v, 'Wh': Wh, 'wg_w': wg_w, 'wo_w': wo_w, 'gn_gamma': gn_gamma, 'gn_beta': gn_beta}
    _L3_xattn_all = _L3_xattn_setup()
    _L3_xattn_in = {k: v for k, v in _L3_xattn_all.items() if k in ('Wh', 'wg_w', 'wo_w', 'gn_gamma', 'gn_beta')}
    del _L3_xattn_all

    def _L3_ffn_setup():
        import jax, jax.numpy as jnp
        import numpy as np
        H = 256
        E = 8
        TOPK = 2
        I_MOE = 128
        I_SH = 512

        def _silu_and_mul(gu):
            g, u = jnp.split(gu, 2, axis=-1)
            return jax.nn.silu(g) * u
        key = jax.random.key(seed)
        ks = jax.random.split(key, 6)
        s = lambda *sh: 1.0 / np.sqrt(sh[-2])
        hidden_states = jax.random.normal(ks[0], (2, 128, H), dtype=jnp.float32)
        w_gate = jax.random.normal(ks[1], (H, E), dtype=jnp.float32) * (1.0 / np.sqrt(H))
        w_gate_up = jax.random.normal(ks[2], (E, H, 2 * I_MOE), dtype=jnp.float32) * (1.0 / np.sqrt(H))
        w_down = jax.random.normal(ks[3], (E, I_MOE, H), dtype=jnp.float32) * (1.0 / np.sqrt(I_MOE))
        w_sh_gate_up = jax.random.normal(ks[4], (H, 2 * I_SH), dtype=jnp.float32) * (1.0 / np.sqrt(H))
        w_sh_down = jax.random.normal(ks[5], (I_SH, H), dtype=jnp.float32) * (1.0 / np.sqrt(I_SH))
        return {'hidden_states': hidden_states, 'w_gate': w_gate, 'w_gate_up': w_gate_up, 'w_down': w_down, 'w_sh_gate_up': w_sh_gate_up, 'w_sh_down': w_sh_down}
    _L3_ffn_all = _L3_ffn_setup()
    _L3_ffn_in = {k: v for k, v in _L3_ffn_all.items() if k in ('w_gate', 'w_gate_up', 'w_down', 'w_sh_gate_up', 'w_sh_down')}
    del _L3_ffn_all
    return {'x': x, 'ctx_2048': ctx_2048, 'mask_BxS2_bk0': mask_BxS2_bk0, 'L0_xattn_W_qkv': _L0_xattn_in['W_qkv'], 'L0_xattn_W_o': _L0_xattn_in['W_o'], 'L0_xattn_beta_q': _L0_xattn_in['beta_q'], 'L0_xattn_beta_k': _L0_xattn_in['beta_k'], 'L0_xattn_gate': _L0_xattn_in['gate'], 'L0_xattn_log_tau': _L0_xattn_in['log_tau'], 'L0_ffn_gate_w': _L0_ffn_in['gate_w'], 'L0_ffn_w1': _L0_ffn_in['w1'], 'L0_ffn_b1': _L0_ffn_in['b1'], 'L0_ffn_w2': _L0_ffn_in['w2'], 'L0_ffn_b2': _L0_ffn_in['b2'], 'L0_ffn_shared_w1': _L0_ffn_in['shared_w1'], 'L0_ffn_shared_b1': _L0_ffn_in['shared_b1'], 'L0_ffn_shared_w2': _L0_ffn_in['shared_w2'], 'L0_ffn_shared_b2': _L0_ffn_in['shared_b2'], 'L1_xattn_Wq': _L1_xattn_in['Wq'], 'L1_xattn_Wk': _L1_xattn_in['Wk'], 'L1_xattn_Wv': _L1_xattn_in['Wv'], 'L1_ffn_gate_w': _L1_ffn_in['gate_w'], 'L1_ffn_w1': _L1_ffn_in['w1'], 'L1_ffn_w3': _L1_ffn_in['w3'], 'L1_ffn_w2': _L1_ffn_in['w2'], 'L1_ffn_sw1': _L1_ffn_in['sw1'], 'L1_ffn_sw3': _L1_ffn_in['sw3'], 'L1_ffn_sw2': _L1_ffn_in['sw2'], 'L2_ffn_router_w': _L2_ffn_in['router_w'], 'L2_ffn_gate_up_proj': _L2_ffn_in['gate_up_proj'], 'L2_ffn_down_proj': _L2_ffn_in['down_proj'], 'L2_ffn_shared_gate_w': _L2_ffn_in['shared_gate_w'], 'L2_ffn_shared_up_w': _L2_ffn_in['shared_up_w'], 'L2_ffn_shared_down_w': _L2_ffn_in['shared_down_w'], 'L2_ffn_shared_expert_gate_w': _L2_ffn_in['shared_expert_gate_w'], 'L3_xattn_Wh': _L3_xattn_in['Wh'], 'L3_xattn_wg_w': _L3_xattn_in['wg_w'], 'L3_xattn_wo_w': _L3_xattn_in['wo_w'], 'L3_xattn_gn_gamma': _L3_xattn_in['gn_gamma'], 'L3_xattn_gn_beta': _L3_xattn_in['gn_beta'], 'L3_ffn_w_gate': _L3_ffn_in['w_gate'], 'L3_ffn_w_gate_up': _L3_ffn_in['w_gate_up'], 'L3_ffn_w_down': _L3_ffn_in['w_down'], 'L3_ffn_w_sh_gate_up': _L3_ffn_in['w_sh_gate_up'], 'L3_ffn_w_sh_down': _L3_ffn_in['w_sh_down']}

def reference(x, ctx_2048, mask_BxS2_bk0, L0_xattn_W_qkv, L0_xattn_W_o, L0_xattn_beta_q, L0_xattn_beta_k, L0_xattn_gate, L0_xattn_log_tau, L0_ffn_gate_w, L0_ffn_w1, L0_ffn_b1, L0_ffn_w2, L0_ffn_b2, L0_ffn_shared_w1, L0_ffn_shared_b1, L0_ffn_shared_w2, L0_ffn_shared_b2, L1_xattn_Wq, L1_xattn_Wk, L1_xattn_Wv, L1_ffn_gate_w, L1_ffn_w1, L1_ffn_w3, L1_ffn_w2, L1_ffn_sw1, L1_ffn_sw3, L1_ffn_sw2, L2_ffn_router_w, L2_ffn_gate_up_proj, L2_ffn_down_proj, L2_ffn_shared_gate_w, L2_ffn_shared_up_w, L2_ffn_shared_down_w, L2_ffn_shared_expert_gate_w, L3_xattn_Wh, L3_xattn_wg_w, L3_xattn_wo_w, L3_xattn_gn_gamma, L3_xattn_gn_beta, L3_ffn_w_gate, L3_ffn_w_gate_up, L3_ffn_w_down, L3_ffn_w_sh_gate_up, L3_ffn_w_sh_down):
    import jax
    import jax.numpy as jnp

    def _L0_xattn_ref(x, W_qkv, W_o, beta_q, beta_k, gate, log_tau, K_mem, V_mem, clip_k):
        import jax, jax.numpy as jnp
        import numpy as np
        D = x.shape[-1]
        scale = D ** (-0.5)
        qkv = x @ W_qkv.T
        Q = qkv[..., :D]
        alpha = jax.nn.sigmoid(gate)
        tau = jnp.exp(log_tau)
        coef = (alpha * beta_q + (1.0 - alpha) * beta_k) * scale * tau
        scores = coef * jnp.einsum('bsd,bnd->bsn', Q, K_mem)
        scores = scores - jnp.max(scores, axis=-1, keepdims=True)
        thr = jax.lax.top_k(scores, clip_k)[0][..., -1:]
        scores = jnp.where(scores < thr, -jnp.inf, scores)
        att = jax.nn.softmax(scores, axis=-1)
        out = jnp.einsum('bsn,bnd->bsd', att, V_mem)
        return out @ W_o.T

    def _L0_ffn_ref(x, gate_w, w1, b1, w2, b2, shared_w1, shared_b1, shared_w2, shared_b2):
        import jax, jax.numpy as jnp
        import numpy as np
        K = 2

        def gelu(v):
            return jax.nn.gelu(v, approximate=False)
        B, S, D = x.shape
        E = gate_w.shape[1]
        xf = x.reshape(-1, D)
        logits = xf @ gate_w
        top_logits, top_idx = jax.lax.top_k(logits, K)
        top_gates = jax.nn.softmax(top_logits, axis=-1)
        gates = jnp.sum(jax.nn.one_hot(top_idx, E, dtype=xf.dtype) * top_gates[..., None], axis=1)
        h = gelu(jnp.einsum('nd,edh->neh', xf, w1) + b1)
        out_e = jnp.einsum('neh,ehd->ned', h, w2) + b2
        routed = jnp.einsum('ne,ned->nd', gates, out_e)
        shared = gelu(xf @ shared_w1 + shared_b1) @ shared_w2 + shared_b2
        return (routed + shared).reshape(B, S, D)

    def _L1_xattn_ref(x, context, Wq, Wk, Wv):
        import jax, jax.numpy as jnp
        import numpy as np
        DIM = 256
        NHEADS = 32
        HEAD_DIM = DIM // NHEADS
        EPS = 1e-06

        def _rmsnorm(t):
            return t * jax.lax.rsqrt(jnp.mean(t * t, axis=-1, keepdims=True) + EPS)
        b, n, _ = x.shape
        m = context.shape[1]
        q = x @ Wq.T
        k_raw = context @ Wk.T
        v_raw = context @ Wv.T
        q = q.reshape(b, n, NHEADS, HEAD_DIM).transpose(0, 2, 1, 3)
        kv = jnp.concatenate([k_raw, v_raw], axis=-1)
        kv = kv.reshape(b, m, NHEADS, HEAD_DIM, 2)
        k = kv[..., 0].transpose(0, 2, 1, 3)
        v = kv[..., 1].transpose(0, 2, 1, 3)
        q = _rmsnorm(q)
        k = _rmsnorm(k)
        scale = HEAD_DIM ** (-0.5)
        scores = jnp.einsum('bhnd,bhmd->bhnm', q, k) * scale
        attn = jax.nn.softmax(scores, axis=-1)
        out = jnp.einsum('bhnm,bhmd->bhnd', attn, v)
        return out.transpose(0, 2, 1, 3).reshape(b, n, NHEADS * HEAD_DIM)

    def _L1_ffn_ref(hidden_states, gate_w, w1, w3, w2, sw1, sw3, sw2):
        import jax, jax.numpy as jnp
        import numpy as np
        B, S, H = (2, 256, 256)
        E, I, K = (8, 176, 2)
        SHARED_I = 176 * 2

        def _moe_forward(hidden_states, gate_w, w1, w3, w2, sw1, sw3, sw2):
            x = hidden_states.reshape(-1, H)
            T = x.shape[0]
            logits = x @ gate_w.T
            scores = jax.nn.softmax(logits, axis=-1)
            topk_w, topk_idx = jax.lax.top_k(scores, K)
            topk_w = topk_w / jnp.sum(topk_w, axis=-1, keepdims=True)
            h = jnp.einsum('th,ehi->eti', x, w1)
            g = jnp.einsum('th,ehi->eti', x, w3)
            y_all = jnp.einsum('eti,eih->eth', jax.nn.silu(h) * g, w2)
            tok = jnp.arange(T)[:, None]
            y_sel = y_all[topk_idx, tok]
            y = jnp.sum(y_sel * topk_w[..., None], axis=1)
            shared = jax.nn.silu(x @ sw1) * (x @ sw3) @ sw2
            return (y + shared).reshape(hidden_states.shape)
        return _moe_forward(hidden_states, gate_w, w1, w3, w2, sw1, sw3, sw2)

    def _L2_xattn_ref(hidden_states, memory_tokens, memory_mask):
        import jax, jax.numpy as jnp
        import numpy as np
        B, S, D = hidden_states.shape
        scale = 1.0 / jnp.sqrt(jnp.asarray(D, hidden_states.dtype))
        scores = jnp.einsum('bsd,bmd->bsm', hidden_states, memory_tokens) * scale
        neg_inf = jnp.asarray(-1e+30, scores.dtype)
        scores = jnp.where(memory_mask[:, None, :], scores, neg_inf)
        attn = jax.nn.softmax(scores, axis=-1)
        readout = jnp.einsum('bsm,bmd->bsd', attn, memory_tokens)
        valid_b = jnp.any(memory_mask, axis=-1)
        out = jnp.where(valid_b[:, None, None], readout, jnp.zeros_like(readout))
        return out

    def _L2_ffn_ref(hidden_states, router_w, gate_up_proj, down_proj, shared_gate_w, shared_up_w, shared_down_w, shared_expert_gate_w):
        import jax, jax.numpy as jnp
        import numpy as np
        from jax import lax
        B, S, H = (1, 256, 256)
        E, I, TOP_K = (64, 64, 8)
        SHARED_I = 64
        b, s, h_dim = hidden_states.shape
        h = hidden_states.reshape(-1, h_dim)
        T = h.shape[0]
        shared = jnp.dot(jax.nn.silu(jnp.dot(h, shared_gate_w.T)) * jnp.dot(h, shared_up_w.T), shared_down_w.T)
        shared = jax.nn.sigmoid(jnp.dot(h, shared_expert_gate_w.T)) * shared
        logits = jnp.dot(h, router_w.T)
        probs = jax.nn.softmax(logits.astype(jnp.float32), axis=-1)
        top_vals, top_idx = lax.top_k(probs, TOP_K)
        top_vals = top_vals / jnp.sum(top_vals, axis=-1, keepdims=True)
        top_vals = top_vals.astype(h.dtype)
        comb = jnp.zeros((T, E), h.dtype).at[jnp.arange(T)[:, None], top_idx].add(top_vals)

        def body(acc, xs):
            wgu, wd, w_e = xs
            g, u = jnp.split(jnp.dot(h, wgu.T), 2, axis=-1)
            eo = jnp.dot(jax.nn.silu(g) * u, wd.T)
            return (acc + eo * w_e[:, None], None)
        expert_out, _ = lax.scan(body, jnp.zeros_like(h), (gate_up_proj, down_proj, comb.T))
        return (expert_out + shared).reshape(b, s, h_dim)

    def _L3_xattn_ref(x, k, v, Wh, wg_w, wo_w, gn_gamma, gn_beta):
        import jax, jax.numpy as jnp
        import numpy as np
        B, S, DIM, HD = (4, 128, 256, 128)
        H = DIM // HD
        GN_EPS = 0.001

        def _decay_masks(n_heads, seq_len):
            gam = 1.0 - 2.0 ** (-5.0 - jnp.arange(n_heads, dtype=jnp.float32))
            idx = jnp.arange(seq_len, dtype=jnp.float32)
            expo = idx[None, :] - idx[:, None]
            D = jnp.where(expo[None, :, :] <= 0, gam[:, None, None] ** expo[None, :, :], 0.0)
            return D / jnp.sqrt(D.sum(axis=-1))[:, None, :]
        b, s, dim = x.shape
        h, hd, _ = Wh.shape
        xh = x.reshape(b, s, h, hd)
        kh = k.reshape(b, s, h, hd)
        vh = v.reshape(b, s, h, hd)
        Q = jnp.einsum('bshd,hde->bshe', xh, Wh)
        K = jnp.einsum('bshd,hde->bshe', kh, Wh)
        V = jnp.einsum('bshd,hde->bshe', vh, Wh)
        scores = jnp.einsum('bshe,bthe->bhst', Q, K) / jnp.sqrt(jnp.float32(hd))
        Dn = _decay_masks(h, s)
        masked = scores * Dn[None, :, :, :]
        A = jnp.maximum(jnp.abs(masked.sum(axis=0)), 1.0)
        O = jnp.einsum('hst,bthe->bshe', A, V).reshape(b, s, dim)
        mu = O.mean(axis=-1, keepdims=True)
        var = O.var(axis=-1, keepdims=True)
        Y = (O - mu) / jnp.sqrt(var + GN_EPS) * gn_gamma + gn_beta
        W = jax.nn.relu(x @ wg_w)
        return W * Y @ wo_w

    def _L3_ffn_ref(hidden_states, w_gate, w_gate_up, w_down, w_sh_gate_up, w_sh_down):
        import jax, jax.numpy as jnp
        import numpy as np
        H = 256
        E = 8
        TOPK = 2
        I_MOE = 128
        I_SH = 512

        def _silu_and_mul(gu):
            g, u = jnp.split(gu, 2, axis=-1)
            return jax.nn.silu(g) * u
        orig_shape = hidden_states.shape
        x = hidden_states.reshape(-1, orig_shape[-1])
        router_logits = x @ w_gate
        probs = jax.nn.softmax(router_logits, axis=-1)
        topk_w, topk_ids = jax.lax.top_k(probs, TOPK)
        topk_w = topk_w / jnp.sum(topk_w, axis=-1, keepdims=True)
        combine = jnp.sum(topk_w[..., None] * jax.nn.one_hot(topk_ids, E, dtype=x.dtype), axis=1)
        gu = jnp.einsum('th,ehf->etf', x, w_gate_up)
        act = _silu_and_mul(gu)
        eo = jnp.einsum('eti,eih->eth', act, w_down)
        routed = jnp.einsum('te,eth->th', combine, eo)
        shared = _silu_and_mul(x @ w_sh_gate_up) @ w_sh_down
        return (routed + shared).reshape(orig_shape)
    x = x + _L0_xattn_ref(_layernorm(x, axis=-1), L0_xattn_W_qkv, L0_xattn_W_o, L0_xattn_beta_q, L0_xattn_beta_k, L0_xattn_gate, L0_xattn_log_tau, ctx_2048, ctx_2048, 54)
    x = x + _L0_ffn_ref(_layernorm(x, axis=-1), L0_ffn_gate_w, L0_ffn_w1, L0_ffn_b1, L0_ffn_w2, L0_ffn_b2, L0_ffn_shared_w1, L0_ffn_shared_b1, L0_ffn_shared_w2, L0_ffn_shared_b2)
    x = x + _L1_xattn_ref(_layernorm(x, axis=-1), ctx_2048, L1_xattn_Wq, L1_xattn_Wk, L1_xattn_Wv)
    x = x + _L1_ffn_ref(_layernorm(x, axis=-1), L1_ffn_gate_w, L1_ffn_w1, L1_ffn_w3, L1_ffn_w2, L1_ffn_sw1, L1_ffn_sw3, L1_ffn_sw2)
    x = x + _L2_xattn_ref(_layernorm(x, axis=-1), ctx_2048, mask_BxS2_bk0)
    x = x + _L2_ffn_ref(_layernorm(x, axis=-1), L2_ffn_router_w, L2_ffn_gate_up_proj, L2_ffn_down_proj, L2_ffn_shared_gate_w, L2_ffn_shared_up_w, L2_ffn_shared_down_w, L2_ffn_shared_expert_gate_w)
    x = x + _L3_xattn_ref(_layernorm(x, axis=-1), ctx_2048, ctx_2048, L3_xattn_Wh, L3_xattn_wg_w, L3_xattn_wo_w, L3_xattn_gn_gamma, L3_xattn_gn_beta)
    x = x + _L3_ffn_ref(_layernorm(x, axis=-1), L3_ffn_w_gate, L3_ffn_w_gate_up, L3_ffn_w_down, L3_ffn_w_sh_gate_up, L3_ffn_w_sh_down)
    return x

_drawn_inputs = setup_inputs


def setup_inputs(seed=0):
    import zlib

    import numpy as np

    out = dict(_drawn_inputs(seed))
    spreads = {'L3_xattn_gn_gamma': (1.0, 0.2), 'L3_xattn_gn_beta': (0.0, 0.1)}
    factors = {'L0_ffn_w1': 8.0,
     'L0_ffn_b1': 8.0,
     'L0_ffn_w2': 8.0,
     'L0_ffn_shared_w1': 8.0,
     'L0_ffn_shared_b1': 8.0,
     'L0_ffn_shared_w2': 8.0,
     'L1_ffn_gate_w': 3.388,
     'L1_ffn_w1': 3.193,
     'L1_ffn_w2': 3.354,
     'L2_ffn_router_w': 5.903,
     'L2_ffn_gate_up_proj': 4.802,
     'L2_ffn_down_proj': 5.678,
     'L2_ffn_shared_gate_w': 7.013,
     'L2_ffn_shared_up_w': 5.294,
     'L2_ffn_shared_down_w': 5.221,
     'L2_ffn_shared_expert_gate_w': 8.0}
    for name, (base, spread) in spreads.items():
        noise = np.random.default_rng([zlib.crc32(name.encode()), seed]).standard_normal(out[name].shape)
        drawn = base * np.exp(spread * noise) if base else spread * noise
        out[name] = jnp.asarray(drawn.astype(out[name].dtype))
    for name, factor in factors.items():
        out[name] = (out[name] * factor).astype(out[name].dtype)
    return out
```

```python
from contextlib import ExitStack

import concourse.bass as bass
from concourse import mybir

F32 = mybir.dt.float32
F32R = mybir.dt.float32r
F16 = mybir.dt.float16
BF16 = mybir.dt.bfloat16
I32 = mybir.dt.int32
U8 = mybir.dt.uint8
ALU = mybir.AluOpType
ACT = mybir.ActivationFunctionType
AX = mybir.AxisListType

P = 128
D = 256
K = D // P
B = 8
T = B * P
PAIRS = B // 2
HALF = T // 2
BLOCKS = 8
LN_EPS = 1e-5
RMS_EPS = 1e-6
GN_EPS = 1e-3
HEADS1 = 32
HD1 = D // HEADS1
GROUPS1 = HEADS1 // 4
VW = 3 * HD1 + 1
CLIP = 54
NEG = -3.0e38


TAIL = 2


class Ffn:

    def __init__(self, base, chunks, peeled, plain, experts, gate_rows, top, up, act):
        self.base, self.chunks, self.peeled, self.plain = base, chunks, peeled, plain
        self.experts, self.gate_rows, self.top, self.up, self.act = experts, gate_rows, top, up, act
        self.steps = (chunks - peeled - TAIL) // 2
        self.width = (K * P * (2 if up else 1)) + D
        self.bias = not up
        assert (chunks - peeled - TAIL) % 2 == 0


FFN = [
    Ffn(0, 10, 2, 2, 8, 8, 2, False, ACT.Gelu),
    Ffn(10, 14, 6, 3, 8, 8, 2, True, ACT.Silu),
    Ffn(24, 33, 3, 0, 64, 65, 8, True, ACT.Silu),
    Ffn(57, 12, 4, 4, 8, 8, 2, True, ACT.Silu),
]
I1 = 176
R1 = I1 - P
GATED = [sum(f.chunks - f.plain for f in FFN[:n]) for n in range(len(FFN))]

SMALL = ["wq0", "wo0", "wk1", "wv1", "wq1", "wg3", "wo3"]
GATE_AT = []
_at = len(SMALL) * K * D
for _f in FFN:
    GATE_AT.append(_at)
    _at += K * _f.gate_rows
WH_AT = _at
LP = 66
LD_M = 16 * 7
SCHEDULE1 = [("tile", 0), ("raw", 4), ("raw", 5), ("tile", 1), ("raw", 6), ("raw", 7), ("scale", 7),
             ("tile", 2), ("stack", 4), ("stack", 5), ("tile", 3), ("stack", 6), ("stack", 7),
             ("tile", 4), ("tile", 5), ("tile", 6), ("tile", 7)]
WHT_AT = WH_AT + D
SMALL_W = WHT_AT + D


def SPLITS(ld_c, ld_s, craw, sraw, c_part, s_part):
    first = K * D
    return [(ld_s, s_part[:, 0:first], sraw[:, 0:first]),
            (ld_c, c_part[:, 0, :], craw[:, 0, :]), (ld_c, c_part[:, 1, :], craw[:, 1, :]),
            (ld_s, s_part[:, first:WHT_AT], sraw[:, first:WHT_AT])]


def program(nc, x_in, ctx_t, ctx_n, mask_in, small_in, coef_in, b2_in, gamma_in, beta_in,
            decay_in, ident_in, w_in, gates, out, blocks=8):
    with ExitStack() as ctx:
        def sb(name, shape, dt=F32):
            return ctx.enter_context(nc.sbuf_tensor(name, shape, dt))

        def sem(name):
            return ctx.enter_context(nc.semaphore(name))

        x = sb("x", [P, B, D])
        xs = sb("xs", [P, K, B, 2, P], F32R)
        xn = sb("xn", [P, 4, D])
        ch = sb("ch", [P, K, T], F32R)
        cl = sb("cl", [P, K, T], F32R)
        mk_h = sb("mk_h", [P, 2, T], F32R)
        mk_l = sb("mk_l", [P, 2, T], F32R)
        vw = sb("vw", [P, 2, B, P])
        vw0 = vw[:, :, :, :].rearrange("p h b e -> p (h b e)").rearrange("p (b d) -> p b d", b=B)
        two = ExitStack()
        cn = two.enter_context(nc.sbuf_tensor("cn", [P, B, D], F32))
        two.close()
        kst = sb("kst", [P, B, GROUPS1, P], F16)
        vp = sb("vp", [P, B, HEADS1, VW], BF16)
        sw_h = sb("sw_h", [P, WHT_AT], F32R)
        sw_l = sb("sw_l", [P, WHT_AT], F32R)
        g_h = sb("g_h", [P, 2, P], F32R)
        g_l = sb("g_l", [P, 2, P], F32R)
        ident = sb("ident", [P, P])
        ident16 = sb("ident16", [P, P], F16)
        wraw = sb("wraw", [P, 2, 3 * D])
        wup_h = sb("wup_h", [P, 2, 2 * D], F32R)
        wup_l = sb("wup_l", [P, 2, 2 * D], F32R)
        wdn_h = sb("wdn_h", [P, 2, D], F32R)
        wdn_l = sb("wdn_l", [P, 2, D], F32R)
        b2 = sb("b2", [FFN[0].experts + 1, D])
        gam = sb("gam", [P, D])
        bet = sb("bet", [P, D])
        dec = sb("dec", [P, 2, P])
        masku = sb("masku", [P, B, P], U8)
        stat = sb("stat", [P, 2, 2, 6])
        mv = sb("mv", [P, 2, 2, 2])
        var_eps = sb("var_eps", [P, 2, 2])
        rstd = sb("rstd", [P, 2, 2])
        mhalf = sb("mhalf", [P, 8])
        cvec = sb("cvec", [P, 4])
        cwork = sb("cwork", [P, 8])
        negm = sb("negm", [P, 2])
        esum = sb("esum", [P, B])
        rsum = sb("rsum", [P, B])
        valid = sb("valid", [P, B])
        sc = sb("sc", [P, 2, P])
        work = sb("work", [P, 2, P])
        ex = sb("ex", [P, 2, P])
        ep = sb("ep", [P, 2, P])
        ept = sb("ept", [P, 2, P])
        top = sb("top", [P, 2, 56])

        early = ExitStack()
        craw = early.enter_context(nc.sbuf_tensor("craw", [P, K, T], F32))
        sraw = early.enter_context(nc.sbuf_tensor("sraw", [P, SMALL_W], F32))
        early.close()

        mid = ExitStack()

        def sbm(name, shape, dt=F32):
            return mid.enter_context(nc.sbuf_tensor(name, shape, dt))
        s_act = sbm("s_act", [P, 2, HALF])
        sg = sbm("sg", [P, 2, HALF])
        tt = sbm("tt", [P, 2, HALF])
        gb = sbm("gb", [P, 2, T])
        gt = sbm("gt", [P, T])
        routing = ExitStack()

        def sbr(name, shape, dt=F32):
            return routing.enter_context(nc.sbuf_tensor(name, shape, dt))
        lgt = sbr("lgt", [P, 2, HALF])
        lg = sbr("lg", [P, 2, 4, 65])
        le = sbr("le", [P, 2, 4, 65])
        lm = sbr("lm", [P, 2, 4, 65])
        m8 = sbr("m8", [P, 2, 4, 8])
        gsum = sbr("gsum", [P, 2, 16])
        routing.close()
        th = sbm("th", [P, 2, T], F32R)
        tl = sbm("tl", [P, 2, T], F32R)
        mid.close()

        att = ExitStack()

        def sba(name, shape, dt=F32):
            return att.enter_context(nc.sbuf_tensor(name, shape, dt))
        maskf = sba("maskf", [P, B, P])
        maskb = sba("maskb", [P, B, P])
        at = sba("at", [P, 2, P])
        a1 = sba("a1", [P, 2, P])
        wr = sba("wr", [P, B, D])
        ya = sba("ya", [P, 2, D])
        yb = sba("yb", [P, 2, D])
        yc = sba("yc", [P, 2, D])
        st3 = sba("st3", [P, B, 2, 6])
        mv3 = sba("mv3", [P, B, 2])
        ve3 = sba("ve3", [P, B])
        rs3 = sba("rs3", [P, B])
        att.close()

        one = ExitStack()

        def sb1(name, shape, dt=F32):
            return one.enter_context(nc.sbuf_tensor(name, shape, dt))
        qf = sb1("qf", [P, 4, D])
        sq = sb1("sq", [P, 2, D])
        ss = sb1("ss", [P, 4, HEADS1])
        nw_y = sb1("nw_y", [P, 4, HEADS1])
        nw_a = sb1("nw_a", [P, 4, HEADS1])
        nw_b = sb1("nw_b", [P, 4, HEADS1])
        qn = sb1("qn", [P, 2, D])
        stk = sb1("stk", [P, 2, HEADS1, 4, HD1], F16)
        vres = sb1("vres", [P, 2, 2, D])
        qst = sb1("qst", [P, 4, GROUPS1, P], F16)
        e1 = sb1("e1", [P, 4, HALF])
        eh = sb1("eh", [P, 4, HALF], F16)
        el = sb1("el", [P, 4, HALF], F16)
        o3 = sb1("o3", [P, 2, 16, HD1])
        oy = sb1("oy", [P, 2, 16, HD1])
        r3 = sb1("r3", [P, 2, 16])
        one.close()

        ps = ctx.enter_context(nc.psum_tensor("ps", [P, 8, 512], F32))
        ps16 = ps[:, :, :].bitcast(F16)

        ld_x, ld_c, ld_s, ld_m, ld_n = sem("ld_x"), sem("ld_c"), sem("ld_s"), sem("ld_m"), sem("ld_n")
        w_loaded = [sem("w_loaded0"), sem("w_loaded1")]
        g_loaded = [sem("g_loaded0"), sem("g_loaded1")]
        g_stored, stored = sem("g_stored"), sem("stored")
        const_ready = sem("const_ready")
        dve_step = sem("dve_step")
        split_hi, split_lo = sem("split_hi"), sem("split_lo")
        pre_ps, pre_hi, pre_lo = sem("pre_ps"), sem("pre_hi"), sem("pre_lo")
        mv_ready, rstd_ready = sem("mv_ready"), sem("rstd_ready")
        xn_ready, xt_ps, xh_ready, xl_ready = sem("xn_ready"), sem("xt_ps"), sem("xh_ready"), sem("xl_ready")
        coef_exp = sem("coef_exp")
        sc_ps, sc_read, negm_ready, ex_ready = sem("sc_ps"), sem("sc_read"), sem("negm_ready"), sem("ex_ready")
        ep_ready, ept_ps, ept_ready = sem("ep_ready"), sem("ept_ps"), sem("ept_ready")
        y_ps, x_added = sem("y_ps"), sem("x_added")
        up_ps, s_ready, sg_ready, t_ready = sem("up_ps"), sem("s_ready"), sem("sg_ready"), sem("t_ready")
        th_ready, tl_ready, dn_ps = sem("th_ready"), sem("tl_ready"), sem("dn_ps")
        wup_hi, wup_lo, wdn_hi, wdn_lo = sem("wup_hi"), sem("wup_lo"), sem("wdn_hi"), sem("wdn_lo")
        lt_ps, lt_ready, lg_ps = sem("lt_ps"), sem("lt_ready"), sem("lg_ps")
        ld_ready, le_ready, gw_ready = sem("ld_ready"), sem("le_ready"), sem("gw_ready")
        gt_ps, gt_ready = sem("gt_ps"), sem("gt_ready")
        qk_ps, qk_sq, ss_read = sem("qk_ps"), sem("qk_sq"), sem("ss_read")
        qn_ready, st_hi, st_lo = sem("qn_ready"), sem("st_hi"), sem("st_lo")
        qt_ps, qt_ready = sem("qt_ps"), sem("qt_ready")
        v_ps, v1_ready, v2_ready, v3_ready, r1_ready = (
            sem("v_ps"), sem("v1_ready"), sem("v2_ready"), sem("v3_ready"), sem("r1_ready"))
        s1_ps, e1_ready, eh_ready, el_ready = sem("s1_ps"), sem("e1_ready"), sem("eh_ready"), sem("el_ready")
        o1_ps, o1_read = sem("o1_ps"), sem("o1_read")
        a_ps, a_ready, o_ps, wg_ps, wr_ready = sem("a_ps"), sem("a_ready"), sem("o_ps"), sem("wg_ps"), sem("wr_ready")
        mv3_ready, rs3_ready, ya_ready, yb_ready = sem("mv3_ready"), sem("rs3_ready"), sem("ya_ready"), sem("yb_ready")
        yc_ready, mask_ready, av_ps = sem("yc_ready"), sem("mask_ready"), sem("av_ps")

        def small(n, k):
            return slice((n * K + k) * D, (n * K + k + 1) * D)

        def gate_cols(n, k):
            return slice(GATE_AT[n] + k * FFN[n].gate_rows, GATE_AT[n] + (k + 1) * FFN[n].gate_rows)

        LAYERS = [n for n in range(4) if 2 * n + 1 < blocks]
        CHUNKS = sum(FFN[n].chunks for n in LAYERS)

        def norms_before(block):
            return PAIRS * (block + (1 if block > 6 else 0))

        def after(i, count, rate):
            return count if i is None else rate * i + count

        def every_chunk(eng, n, do):
            f = FFN[n]
            for c in range(f.peeled):
                do(n, c, None)
            with eng.Fori(0, f.steps) as i:
                for u in range(2):
                    do(n, f.peeled + u, i)
            for c in range(f.chunks - TAIL, f.chunks):
                do(n, c, None)

        def gated(n, c):
            return GATED[n] + c - FFN[n].plain

        def segments(n, c):
            f = FFN[n]
            if n == 2:
                return [(0, P, 64)] if c == 0 else [(0, 64, 2 * (c - 1)), (64, 64, 2 * (c - 1) + 1)]
            if n == 1 and c < f.peeled:
                found, r = [], 0
                while r < P:
                    unit = (c - f.plain) * P + r
                    e = unit // R1
                    size = min(P - r, (e + 1) * R1 - unit)
                    found.append((r, size, e))
                    r += size
                return found
            return [(0, P, c - (f.peeled if n == 1 else f.plain))]

        def g_loads(n, c):
            return sum(len(segments(m, d)) for m in range(n + 1) for d in range(FFN[m].plain, FFN[m].chunks)
                       if gated(m, d) % 2 == gated(n, c) % 2 and (m < n or d <= c))

        block_ = ctx.enter_context(nc.Block())

        @block_.sync
        def _(sp):
            sp.dma_start(x[:, :, :], x_in.rearrange("b p d -> p b d")).then_inc(ld_x, 16)
            sp.dma_start(craw[:, :, :], ctx_t.rearrange("(k p) t -> p k t", p=P)).then_inc(ld_c, 16)
            sp.dma_start(sraw[:, :], small_in).then_inc(ld_s, 16)
            sp.dma_start(ident[:, :], ident_in).then_inc(ld_m, 16)
            sp.dma_start(cvec[:, :], coef_in.rearrange("(o c) -> o c", o=1).broadcast_to([P, 4])).then_inc(ld_m, 16)
            sp.dma_start(b2[:, :], b2_in).then_inc(ld_m, 16)
            sp.dma_start(gam[:, :], gamma_in.rearrange("(o c) -> o c", o=1).broadcast_to([P, D])).then_inc(ld_m, 16)
            sp.dma_start(bet[:, :], beta_in.rearrange("(o c) -> o c", o=1).broadcast_to([P, D])).then_inc(ld_m, 16)
            sp.dma_start(dec[:, :, :], decay_in).then_inc(ld_m, 16)
            sp.dma_start(masku[:, :, :], mask_in.rearrange("(o b) m -> o b m", o=1).broadcast_to([P, B, P])).then_inc(ld_m, 16)

            def load(n, c, i):
                f, g = FFN[n], FFN[n].base + c
                if g >= 2:
                    sp.wait_ge(t_ready, after(i, 2 * (g - 1), 4))
                if i is None:
                    src = w_in[n][c]
                else:
                    src = w_in[n][bass.ds(2 * i + c, 1), :, :].rearrange("o p c -> (o p) c")
                sp.dma_start(wraw[:, g % 2, 0:f.width + f.bias], src).then_inc(w_loaded[g % 2], 16)

            for n in LAYERS:
                every_chunk(sp, n, load)

            for p in range(PAIRS):
                sp.wait_ge(x_added, PAIRS * (blocks - 1) + p + 1)
                sp.dma_start(out[2 * p:2 * p + 2].rearrange("b p d -> p b d"),
                             x[:, 2 * p:2 * p + 2, :]).then_inc(stored, 16)
            sp.wait_ge(stored, 16 * PAIRS)

        @block_.gpsimd
        def _(pool):
            pool.memset(mhalf[:, :], -0.5).then_inc(const_ready, 1)
            pool.memset(vp[:, :, :, VW - 1:VW], 1.0).then_inc(const_ready, 1)
            pool.wait_ge(ld_m, LD_M)
            pool.tensor_copy(ident16[:, :], ident[:, :]).then_inc(const_ready, 1)
            pool.wait_ge(const_ready, 3)

            def norm(block):
                for p in range(PAIRS):
                    r = PAIRS * block + p
                    pool.wait_ge(mv_ready, r + 1)
                    pool.tensor_tensor(rstd[:, r % 2, :], var_eps[:, r % 2, :], mhalf[:, 0:2],
                                       ALU.pow).then_inc(rstd_ready, 1)

            def gate(n, c, i):
                f, g = FFN[n], FFN[n].base + c
                if c < f.plain or not f.up:
                    return
                slot = gated(n, c) % 2
                pool.wait_ge(g_loaded[slot], after(i, 16 * g_loads(n, c), 16 * len(segments(n, f.peeled))))
                for h in range(2):
                    pool.wait_ge(s_ready, after(i, 2 * g + h + 1, 4))
                    pool.wait_ge(t_ready, after(i, 2 * (g - 1) + h + 1, 4))
                    pool.tensor_tensor(sg[:, h, :], s_act[:, h, :], gb[:, slot, h * HALF:(h + 1) * HALF],
                                       ALU.mult).then_inc(sg_ready, 1)

            norm(0)
            if blocks > 1:
                norm(1)
            if blocks > 2:
                norm(2)
                for u in range(8 * B):
                    pool.wait_ge(e1_ready, u + 1)
                    if u >= 4:
                        pool.wait_ge(o1_ps, u - 3)
                    pool.tensor_scalar(eh[:, u % 4, :], e1[:, u % 4, :], 1.0, 0.0,
                                       ALU.mult, ALU.add).then_inc(eh_ready, 1)
            if blocks > 3:
                norm(3)
                every_chunk(pool, 1, gate)
            if blocks > 4:
                norm(4)
            if blocks > 5:
                norm(5)
                every_chunk(pool, 2, gate)
            if blocks > 6:
                norm(6)
                pool.wait_ge(mv3_ready, 1)
                pool.tensor_tensor(rs3[:, :], ve3[:, :], mhalf[:, :], ALU.pow).then_inc(rs3_ready, 1)
                for b in range(B):
                    pool.wait_ge(ya_ready, b + 1)
                    if b >= 2:
                        pool.wait_ge(yc_ready, b - 1)
                    pool.tensor_tensor(yb[:, b % 2, :], ya[:, b % 2, :], gam[:, :], ALU.mult).then_inc(yb_ready, 1)
            if blocks > 7:
                norm(7)
                every_chunk(pool, 3, gate)

        @block_.tensor
        def _(pe):
            def product(dst, lhs, rhs, start=True, stop=True):
                last = None
                for k in range(K):
                    (ah, al), (bh, bl) = lhs(k), rhs(k)
                    for m, (a, b_) in enumerate(((ah, bh), (ah, bl), (al, bh))):
                        last = pe.matmul(dst, a, b_, start=start and k == 0 and m == 0,
                                         stop=stop and k == K - 1 and m == 2, skip_group_check=True)
                return last

            def x_tile(b):
                return lambda k: (xs[:, k, b, 0, :], xs[:, k, b, 1, :])

            def x_half(h):
                return lambda k: (xs[:, k, 4 * h:4 * h + 4, 0, :], xs[:, k, 4 * h:4 * h + 4, 1, :])

            def ctx_tile(b):
                return lambda k: (ch[:, k, b * P:(b + 1) * P], cl[:, k, b * P:(b + 1) * P])

            def ctx_cols(at_, size):
                return lambda k: (ch[:, k, at_:at_ + size], cl[:, k, at_:at_ + size])

            def weight(n, at_=0, size=D):
                def of(k):
                    a = (n * K + k) * D + at_
                    return sw_h[:, a:a + size], sw_l[:, a:a + size]
                return of

            def turn(q, bank):
                pe.wait_ge(xn_ready, q + 1)
                for k in range(K):
                    for t in range(2):
                        at_ = k * D + t * P
                        last = pe.transpose(ps[:, bank, at_:at_ + P], xn[:, (2 * q + t) % 4, k * P:(k + 1) * P], ident[:, :])
                last.then_inc(xt_ps, 1)

            def norm(block):
                for p in range(PAIRS):
                    turn(norms_before(block) + p, 4 + p)

            def prepare():
                for j in range(2):
                    for h in range(2):
                        pe.wait_ge(split_lo, 3)
                        product(ps[:, 2 * j + h, :], weight(0, j * P, P), ctx_cols(h * HALF, HALF)).then_inc(pre_ps, 1)
                for p in range(PAIRS):
                    pe.wait_ge(split_lo, 4)
                    pe.wait_ge(pre_lo, p + 1)
                    for t in range(2):
                        last = product(ps[:, p, t * D:(t + 1) * D], ctx_tile(2 * p + t), weight(1))
                    last.then_inc(pre_ps, 1)
                pe.wait_ge(pre_hi, 5)
                for h in range(2):
                    wt = sraw[:, WHT_AT + h * P:WHT_AT + (h + 1) * P]
                    last = pe.matmul(ps[:, 0, h * P:(h + 1) * P], wt, wt, start=True, stop=True)
                last.then_inc(pre_ps, 1)

            def rows(z, src, n):
                if z:
                    pe.wait_ge(qk_sq, z)
                product(ps[:, 6, 0:D], src, weight(n)).then_inc(qk_ps, 1)

            def stacks(z):
                pe.wait_ge(st_lo, z + 1)
                if z:
                    pe.wait_ge(qt_ready, z)
                for g in range(GROUPS1):
                    part = stk[:, z % 2, 4 * g:4 * g + 4, :, :].rearrange("p j r d -> p (j r d)")
                    last = pe.transpose(ps16[:, 7, g * P:(g + 1) * P], part, ident16[:, :])
                last.then_inc(qt_ps, 1)

            def values(b):
                if b >= 2:
                    pe.wait_ge(r1_ready, b - 1)
                product(ps[:, 4 + b % 2, 0:D], ctx_tile(b), weight(3)).then_inc(v_ps, 1)

            def prepare_last():
                for h in range(2):
                    for s in range(2):
                        parts = ((g_h, ch), (g_h, cl), (g_l, ch))
                        for m, (a, b_) in enumerate(parts):
                            last = pe.matmul(ps[:, 2 * h + s, :], a[:, h, :], b_[:, h, s * HALF:(s + 1) * HALF],
                                             start=m == 0, stop=m == 2)
                        last.then_inc(pre_ps, 1)
                for b in range(B):
                    if b < 4:
                        pe.wait_ge(pre_lo, 6 + b)
                    else:
                        pe.wait_ge(pre_hi, 14 + b - 4)
                    for h in range(2):
                        t = slice(b * P, (b + 1) * P)
                        wh = slice(WH_AT, WH_AT + D)
                        for m, (a, w) in enumerate(((ch, sw_h), (ch, sw_l), (cl, sw_h))):
                            last = pe.matmul(ps[:, b % 4, h * D:(h + 1) * D], a[:, h, t], w[:, wh],
                                             start=m == 0, stop=m == 2)
                    last.then_inc(pre_ps, 1)

            def attend(block):
                o, nb = (0, 0) if block == 0 else (B, norms_before(block))
                keys = (lambda k, a: (mk_h[:, k, a:a + D], mk_l[:, k, a:a + D])) if block == 0 else \
                    (lambda k, a: (ch[:, k, a:a + D], cl[:, k, a:a + D]))
                norm(block)
                if block == 0:
                    pe.wait_ge(pre_lo, 5)
                    pe.wait_ge(pre_hi, 9)
                for i in range(B + 2):
                    if i < B:
                        z = o + i
                        pe.wait_ge(xl_ready, nb + i // 2 + 1)
                        if z >= 2:
                            pe.wait_ge(sc_read, z - 1)
                        product(ps[:, z % 2, 0:D], x_tile(i), lambda k: keys(k, (i // 2) * D)).then_inc(sc_ps, 1)
                    if 1 <= i <= B:
                        z = o + i - 1
                        src = (ep if block == 0 else ex)[:, z % 2, :]
                        pe.wait_ge(ep_ready if block == 0 else ex_ready, z + 1)
                        if z >= 2:
                            pe.wait_ge(ept_ready, z - 1)
                        pe.transpose(ps[:, 2 + z % 2, 0:P], src, ident[:, :]).then_inc(ept_ps, 1)
                    if i >= 2:
                        b, z = i - 2, o + i - 2
                        pe.wait_ge(ept_ready, z + 1)
                        if block == 4:
                            pe.wait_ge(ld_n, 16)
                        if b == 0:
                            pe.wait_ge(xl_ready, nb + PAIRS)
                        vals = vw0[:, b, :] if block == 0 else cn[:, b, :]
                        pe.matmul(ps[:, 4 + b // 2, (b % 2) * D:(b % 2 + 1) * D], ept[:, z % 2, :], vals,
                                  start=True, stop=True).then_inc(av_ps, 1)

            def up(n, c, i, h):
                f, g = FFN[n], FFN[n].base + c
                pe.wait_ge(wup_lo, after(i, g + 1, 2))
                if g:
                    pe.wait_ge(s_ready, after(i, 2 * (g - 1) + h + 1, 4))
                    pe.wait_ge(t_ready, after(i, 2 * (g - 1) + h + 1, 4))
                for m in range(2 if f.up else 1):
                    def w(k):
                        a = m * D + k * P
                        return wup_h[:, g % 2, a:a + P], wup_l[:, g % 2, a:a + P]
                    last = product(ps[:, 2 * h + m, :], w, x_half(h))
                last.then_inc(up_ps, 1)

            def down(n, c, i):
                f, g = FFN[n], FFN[n].base + c
                pe.wait_ge(wdn_lo, after(i, g + 1, 2))
                if c == 0:
                    pe.wait_ge(gt_ready, 2 * n + 2)
                for b in range(B):
                    if b % 4 == 0:
                        pe.wait_ge(tl_ready, after(i, 2 * g + b // 4 + 1, 4))
                    dst = ps[:, 4 + b // 2, (b % 2) * D:(b % 2 + 1) * D]
                    t = slice(b * P, (b + 1) * P)
                    parts = ((th, wdn_h), (th, wdn_l), (tl, wdn_h))
                    for m, (a, w) in enumerate(parts):
                        last = pe.matmul(dst, a[:, g % 2, t], w[:, g % 2, :],
                                         start=c == 0 and i is None and b % 2 == 0 and m == 0,
                                         stop=c == f.chunks - 1 and m == 2, skip_group_check=True)
                    if c == f.chunks - 1 and b in (1, 3, 5):
                        last.then_inc(y_ps, 1)
                last.then_inc(dn_ps, 1)

            def experts(n):
                f, nb = FFN[n], norms_before(2 * n + 1)
                norm(2 * n + 1)

                def logits(h):
                    pe.wait_ge(xl_ready, nb + 2 * h + 2)
                    gate_w = lambda k: (sw_h[:, gate_cols(n, k)], sw_l[:, gate_cols(n, k)])
                    product(ps[0:f.gate_rows, 4 + 2 * h, :], gate_w, x_half(h)).then_inc(lt_ps, 1)

                def logit_rows(h):
                    pe.wait_ge(lt_ready, 2 * n + h + 1)
                    for t in range(4):
                        last = pe.transpose(ps[:, 5 + 2 * h, t * LP:t * LP + f.gate_rows],
                                            lgt[0:f.gate_rows, h, t * P:(t + 1) * P],
                                            ident[0:f.gate_rows, 0:f.gate_rows])
                    last.then_inc(lg_ps, 1)

                def gate_cols_(h):
                    pe.wait_ge(gw_ready, 2 * n + h + 1)
                    for t in range(4):
                        last = pe.transpose(ps[0:f.gate_rows, 4 + 2 * h, t * P:(t + 1) * P],
                                            lm[:, h, t, 0:f.gate_rows], ident[:, :])
                    last.then_inc(gt_ps, 1)

                logits(0)
                up(n, 0, None, 0)
                logits(1)
                logit_rows(0)
                up(n, 0, None, 1)
                logit_rows(1)
                gate_cols_(0)
                gate_cols_(1)

                def chunk(n, c, i):
                    if c:
                        up(n, c, i, 0)
                        up(n, c, i, 1)
                        down(n, c - 1, i)
                every_chunk(pe, n, chunk)
                if n == 0:
                    for b in range(B):
                        pe.matmul(ps[:, 4 + b // 2, (b % 2) * D:(b % 2 + 1) * D], gt[0:f.experts + 1, b * P:(b + 1) * P],
                                  b2[:, :], start=False, stop=False, skip_group_check=True)
                down(n, f.chunks - 1, None)

            def scores1(u):
                b, s, j = u // 8, (u // 4) % 2, u % 4
                if j == 0:
                    pe.wait_ge(qt_ready, B + b + 1)
                if u >= 4:
                    pe.wait_ge(e1_ready, u - 3)
                r = slice(32 * j, 32 * j + 32)
                for g in range(4):
                    last = pe.matmul(ps[:, j, g * P:(g + 1) * P], kst[r, b, 4 * s + g, :], qst[r, b % 4, 4 * s + g, :],
                                     start=True, stop=True)
                last.then_inc(s1_ps, 1)

            def mix1(u):
                b, s, j = u // 8, (u // 4) % 2, u % 4
                pe.wait_ge(el_ready, u + 1)
                if j == 0 and b:
                    pe.wait_ge(o1_read, 2 * b + s - 1)
                for g in range(4):
                    head = 4 * (4 * s + g) + j
                    at_ = (head - 16 * s) * VW
                    for m, e in enumerate((eh, el)):
                        last = pe.matmul(ps[:, 4 + s, at_:at_ + VW], e[:, j, g * P:(g + 1) * P], vp[:, b, head, :],
                                         start=j == 0 and g == 0 and m == 0, stop=True, skip_group_check=True)
                last.then_inc(o1_ps, 1)

            def attend1():
                norm(2)
                prepare_last()
                pe.wait_ge(xl_ready, norms_before(2) + PAIRS)

                def raw(b):
                    rows(B + b, x_tile(b), 4)

                def tile(b):
                    for u in range(8 * b, 8 * b + 8):
                        if u + 4 < 8 * B:
                            scores1(u + 4)
                        mix1(u)
                for b in range(4):
                    raw(b)
                for b in range(4):
                    stacks(B + b)
                pe.wait_ge(pre_hi, 21)
                for u in range(4):
                    scores1(u)
                for what, b in SCHEDULE1:
                    {"raw": raw, "tile": tile, "scale": lambda b: None, "stack": lambda b: stacks(B + b)}[what](b)

            def retain():
                nb = norms_before(6)
                norm(6)
                for b in range(B):
                    pe.wait_ge(xl_ready, nb + b // 2 + 1)
                    for h in range(2):
                        for m, w in enumerate((mk_h, mk_l)):
                            last = pe.matmul(ps[:, h, 0:2 * P], w[:, h, b * P:(b + 1) * P],
                                             xs[:, h, b, :, :].rearrange("p r t -> p (r t)"),
                                             start=b == 0 and m == 0, stop=b == B - 1 and m == 1, skip_group_check=True)
                    if b == B - 1:
                        last.then_inc(a_ps, 1)
                for b in range(B):
                    if b >= 2:
                        pe.wait_ge(wr_ready, b - 1)
                    product(ps[:, 2 + b % 2, 0:D], x_tile(b), weight(5)).then_inc(wg_ps, 1)
                for s in range(2):
                    for h in range(2):
                        pe.wait_ge(a_ready, h + 1)
                        pe.matmul(ps[:, 4 + 2 * s + h, :], at[:, h, :],
                                  vw[:, h, 4 * s:4 * s + 4, :].rearrange("p b e -> p (b e)"),
                                  start=True, stop=True).then_inc(o_ps, 1)
                for p in range(PAIRS):
                    q = nb + PAIRS + p
                    if p >= 2:
                        pe.wait_ge(xl_ready, q - 1)
                    turn(q, p % 2)
                    pe.wait_ge(xl_ready, q + 1)
                    pe.wait_ge(ya_ready, 4 * (p // 2) + 4)
                    for t in range(2):
                        last = product(ps[:, 4 + p, t * D:(t + 1) * D], x_tile(2 * p + t), weight(6))
                    last.then_inc(y_ps, 1)

            prepare()
            pe.wait_ge(const_ready, 3)
            for b in range(B):
                rows(b, ctx_tile(b), 2)
                values(b)
                if b % 4 == 3:
                    for d in range(b - 3, b + 1):
                        stacks(d)
            pe.wait_ge(qt_ready, B)
            pe.wait_ge(r1_ready, B)
            attend(0)
            if blocks > 1:
                experts(0)
            if blocks > 2:
                attend1()
            if blocks > 3:
                experts(1)
            if blocks > 4:
                attend(4)
            if blocks > 5:
                experts(2)
            if blocks > 6:
                retain()
            if blocks > 7:
                experts(3)

        @block_.scalar
        def _(act):
            def high(q, p, bank):
                act.wait_ge(xt_ps, q + 1)
                act.activation(xs[:, :, 2 * p:2 * p + 2, 0, :],
                               ps[:, bank, :].rearrange("p (k t c) -> p k t c", k=K, t=2), ACT.Copy).then_inc(xh_ready, 1)

            def norm(block):
                for p in range(PAIRS):
                    high(norms_before(block) + p, p, 4 + p)

            def split_up(n, c, i):
                f, g = FFN[n], FFN[n].base + c
                act.wait_ge(w_loaded[g % 2], after(i, 16 * (g // 2 + 1), 16))
                if g >= 2:
                    act.wait_ge(up_ps, after(i, 2 * (g - 1), 4))
                act.activation(wup_h[:, g % 2, 0:f.width - D], wraw[:, g % 2, 0:f.width - D], ACT.Copy).then_inc(wup_hi, 1)

            def split_down(n, c, i):
                f, g = FFN[n], FFN[n].base + c
                act.wait_ge(w_loaded[g % 2], after(i, 16 * (g // 2 + 1), 16))
                if g >= 2:
                    act.wait_ge(dn_ps, after(i, g - 1, 2))
                act.activation(wdn_h[:, g % 2, :], wraw[:, g % 2, f.width - D:f.width], ACT.Copy).then_inc(wdn_hi, 1)

            def gate_rows_load(n, c, i):
                f = FFN[n]
                if c < f.plain or c >= f.chunks:
                    return
                slot, j = gated(n, c) % 2, gated(n, c)
                if j >= 2:
                    g0 = f.base + c - 2 if c - 2 >= f.plain else FFN[n - 1].base + FFN[n - 1].chunks - (2 - (c - f.plain))
                    act.wait_ge(t_ready, after(i, 2 * g0 + 2, 4))
                for r, size, e in segments(n, c):
                    if i is None:
                        src = gates[n][e:e + 1, :]
                    else:
                        src = gates[n][bass.ds((4 if n == 2 else 2) * i + e, 1), :]
                    act.dma_start(gb[r:r + size, slot, :], src.broadcast_to([size, T])).then_inc(g_loaded[slot], 16)

            def chunk(n, c, i):
                f, g = FFN[n], FFN[n].base + c
                nxt = (n, c + 1) if c + 1 < f.chunks else (n + 1, 0)
                if g + 1 < CHUNKS:
                    split_up(*nxt, i)
                for h in range(2):
                    act.wait_ge(up_ps, after(i, 2 * g + h + 1, 4))
                    if g:
                        act.wait_ge(t_ready, after(i, 2 * (g - 1) + h + 1, 4))
                    bias = 0.0
                    if f.bias:
                        bias = wraw[:, g % 2, f.width:f.width + 1]
                    act.activation(s_act[:, h, :], ps[:, 2 * h, :], f.act, bias=bias).then_inc(s_ready, 1)
                if c + 1 > 1:
                    gate_rows_load(n, c + 1, i)
                if g + 1 < CHUNKS:
                    split_down(*nxt, i)
                for h in range(2):
                    act.wait_ge(t_ready, after(i, 2 * g + h + 1, 4))
                    act.activation(th[:, g % 2, h * HALF:(h + 1) * HALF], tt[:, h, :], ACT.Copy).then_inc(th_ready, 1)

            def experts(n):
                f = FFN[n]
                norm(2 * n + 1)
                for h in range(2):
                    act.wait_ge(lt_ps, 2 * n + h + 1)
                    act.activation(lgt[0:f.gate_rows, h, :], ps[0:f.gate_rows, 4 + 2 * h, :], ACT.Copy).then_inc(lt_ready, 1)
                for h in range(2):
                    act.wait_ge(ld_ready, 2 * n + h + 1)
                    if f.gate_rows > f.experts:
                        act.activation(le[:, h, :, f.experts:f.gate_rows], lg[:, h, :, f.experts:f.gate_rows], ACT.Exp, scale=-1.0)
                    act.activation(le[:, h, :, 0:f.experts], le[:, h, :, 0:f.experts], ACT.Exp).then_inc(le_ready, 1)
                for h in range(2):
                    act.wait_ge(gt_ps, 2 * n + h + 1)
                    act.activation(gt[0:f.gate_rows, h * HALF:(h + 1) * HALF], ps[0:f.gate_rows, 4 + 2 * h, :],
                                   ACT.Copy).then_inc(gt_ready, 1)
                act.wait_ge(gt_ready, 2 * n + 2)
                act.dma_start(gates[n], gt[0:f.gate_rows, :]).then_inc(g_stored, 16)
                act.wait_ge(g_stored, 16 * (n + 1))
                for c in (0, 1):
                    gate_rows_load(n, c, None)
                every_chunk(act, n, chunk)

            def attend(block):
                o = 0 if block == 0 else B
                norm(block)
                for i in range(B + 1):
                    if i < B:
                        z = o + i
                        act.wait_ge(negm_ready, z + 1)
                        if block == 0:
                            act.activation(ex[:, z % 2, :], sc[:, z % 2, :], ACT.Exp, bias=negm[:, z % 2:z % 2 + 1]).then_inc(ex_ready, 1)
                        else:
                            act.wait_ge(ept_ps, z - 1)
                            act.activation(ex[:, z % 2, :], sc[:, z % 2, :], ACT.Exp, bias=negm[:, z % 2:z % 2 + 1],
                                           accum_out=esum[:, i:i + 1]).then_inc(ex_ready, 1)
                    if i >= 1:
                        z = o + i - 1
                        act.wait_ge(ept_ps, z + 1)
                        if z >= 2:
                            act.wait_ge(av_ps, z - 1)
                        act.activation(ept[:, z % 2, :], ps[:, 2 + z % 2, 0:P], ACT.Copy).then_inc(ept_ready, 1)

            def raw(z):
                act.wait_ge(qk_ps, z + 1)
                if z >= 4:
                    act.wait_ge(qn_ready, z - 3)
                act.activation(qf[:, z % 4, :], ps[:, 6, 0:D], ACT.Copy)
                if z >= 2:
                    act.wait_ge(ss_read, z - 1)
                act.activation(sq[:, z % 2, :], ps[:, 6, 0:D], ACT.Square).then_inc(qk_sq, 1)

            def stack(z, dst):
                act.wait_ge(qn_ready, z + 1)
                if z >= 2:
                    act.wait_ge(qt_ps, z - 1)
                for r in ((0, 2) if z < B else (0, 1)):
                    last = act.activation(stk[:, z % 2, :, r, :], qn[:, z % 2, :].rearrange("p (n d) -> p n d", d=HD1), ACT.Copy)
                last.then_inc(st_hi, 1)
                act.wait_ge(qt_ps, z + 1)
                if z >= B + 4:
                    act.wait_ge(s1_ps, 8 * (z - B - 4) + 8)
                act.activation(dst.rearrange("p g t -> p (g t)"), ps16[:, 7, :], ACT.Copy).then_inc(qt_ready, 1)

            def attend1():
                norm(2)
                for m in range(4):
                    act.wait_ge(pre_ps, 10 + m)
                    act.activation(mk_h[:, m // 2, (m % 2) * HALF:(m % 2 + 1) * HALF], ps[:, m, :], ACT.Copy).then_inc(pre_hi, 1)
                for b in range(B):
                    act.wait_ge(pre_ps, 14 + b)
                    for h in range(2):
                        last = act.activation(vw[:, h, b, :], ps[:, b % 4, h * D + h * P:h * D + (h + 1) * P], ACT.Copy)
                    last.then_inc(pre_hi, 1)

                def tile(b):
                    for u in range(8 * b, 8 * b + 8):
                        act.wait_ge(s1_ps, u + 1)
                        if u >= 4:
                            act.wait_ge(el_ready, u - 3)
                        act.activation(e1[:, u % 4, :], ps[:, u % 4, :], ACT.Exp, scale=HD1 ** -0.5).then_inc(e1_ready, 1)
                for b in range(4):
                    raw(B + b)
                for b in range(4):
                    stack(B + b, qst[:, b % 4, :, :])
                for what, b in SCHEDULE1:
                    {"raw": lambda b: raw(B + b), "tile": tile, "scale": lambda b: None,
                     "stack": lambda b: stack(B + b, qst[:, b % 4, :, :])}[what](b)

            def retain():
                nb = norms_before(6)
                norm(6)
                for b in range(B):
                    act.wait_ge(wg_ps, b + 1)
                    act.activation(wr[:, b, :], ps[:, 2 + b % 2, 0:D], ACT.Relu).then_inc(wr_ready, 1)
                for p in range(PAIRS):
                    high(nb + PAIRS + p, p, p % 2)

            for wait, dst, src in SPLITS(ld_c, ld_s, craw, sraw, ch, sw_h):
                act.wait_ge(wait, 16)
                act.activation(dst, src, ACT.Copy).then_inc(split_hi, 1)
            for m in range(4):
                act.wait_ge(pre_ps, m + 1)
                act.activation(mk_h[:, m // 2, (m % 2) * HALF:(m % 2 + 1) * HALF], ps[:, m, :], ACT.Copy).then_inc(pre_hi, 1)
            for p in range(PAIRS):
                act.wait_ge(pre_ps, 5 + p)
                act.activation(vw0[:, 2 * p:2 * p + 2, :], ps[:, p, :].rearrange("p (t d) -> p t d", t=2), ACT.Copy).then_inc(pre_hi, 1)
            act.wait_ge(pre_ps, 9)
            act.activation(g_h[:, :, :], ps[:, 0, 0:2 * P].rearrange("p (h d) -> p h d", h=2), ACT.Copy).then_inc(pre_hi, 1)
            act.wait_ge(ld_m, LD_M)
            act.activation(cwork[:, 0:1], cvec[:, 2:3], ACT.Exp, scale=-1.0)
            act.activation(cwork[:, 1:2], cvec[:, 3:4], ACT.Exp).then_inc(coef_exp, 1)
            for b in range(B):
                raw(b)
                act.wait_ge(v_ps, b + 1)
                heads = lambda a: a.rearrange("p (n d) -> p n d", d=HD1)
                act.activation(vp[:, b, :, 0:HD1], heads(ps[:, 4 + b % 2, 0:D]), ACT.Copy).then_inc(v1_ready, 1)
                act.wait_ge(r1_ready, b + 1)
                act.activation(vp[:, b, :, HD1:2 * HD1], heads(vres[:, b % 2, 0, :]), ACT.Copy).then_inc(v2_ready, 1)
                if b % 4 == 3:
                    for d in range(b - 3, b + 1):
                        stack(d, kst[:, d, :, :])
            if blocks > 1:
                split_up(0, 0, None)
                split_down(0, 0, None)
            attend(0)
            if blocks > 1:
                experts(0)
            if blocks > 2:
                attend1()
            if blocks > 3:
                act.wait_ge(o1_ps, 8 * B)
                act.dma_start(cn[:, :, :], ctx_n.rearrange("b p d -> p b d")).then_inc(ld_n, 16)
                experts(1)
            if blocks > 4:
                attend(4)
            if blocks > 5:
                experts(2)
            if blocks > 6:
                retain()
            if blocks > 7:
                experts(3)

        @block_.vector
        def _(dve):
            steps = [0]

            def step(instruction):
                instruction.then_inc(dve_step, 1)
                steps[0] += 1
                return steps[0]

            def stats(block, p):
                r = PAIRS * block + p
                if block:
                    dve.wait_ge(x_added, r - PAIRS + 1)
                for t in range(2):
                    n = step(dve.bn_stats(stat[:, r % 2, t, :], x[:, 2 * p + t, :]))
                dve.wait_ge(dve_step, n)
                for t in range(2):
                    n = step(dve.bn_aggr(mv[:, r % 2, t, :], stat[:, r % 2, t, :]))
                dve.wait_ge(dve_step, n)
                dve.tensor_scalar(var_eps[:, r % 2, :], mv[:, r % 2, :, 1], LN_EPS, None, ALU.add).then_inc(mv_ready, 1)

            def normal(block, p):
                r, q = PAIRS * block + p, norms_before(block) + p
                dve.wait_ge(rstd_ready, r + 1)
                if q >= 2:
                    dve.wait_ge(xt_ps, q - 1)
                for t in range(2):
                    last = dve.tensor_scalar(xn[:, (2 * q + t) % 4, :], x[:, 2 * p + t, :], mv[:, r % 2, t, 0:1],
                                             rstd[:, r % 2, t:t + 1], ALU.subtract, ALU.mult)
                last.then_inc(xn_ready, 1)

            def low(q, p, bank):
                dve.wait_ge(xh_ready, q + 1)
                dve.tensor_tensor(xs[:, :, 2 * p:2 * p + 2, 1, :],
                                  ps[:, bank, :].rearrange("p (k t c) -> p k t c", k=K, t=2),
                                  xs[:, :, 2 * p:2 * p + 2, 0, :].bitcast(F32), ALU.subtract).then_inc(xl_ready, 1)

            def add_bank(block, p):
                if block in (1, 3, 5, 7) and p == PAIRS - 1:
                    f = FFN[block // 2]
                    dve.wait_ge(dn_ps, f.base + f.chunks)
                else:
                    dve.wait_ge(y_ps, {1: 0, 3: 3, 5: 6, 6: 9, 7: 13}[block] + p + 1)
                xp = x[:, 2 * p:2 * p + 2, :].rearrange("p t d -> p (t d)")
                dve.tensor_tensor(xp, ps[:, 4 + p, :], xp, ALU.add).then_inc(x_added, 1)

            def add_scaled(block, p):
                o = 0 if block == 0 else B
                dve.wait_ge(av_ps, o + 2 * p + 2)
                for t in range(2):
                    b = 2 * p + t
                    last = dve.scalar_tensor_tensor(x[:, b, :], ps[:, 4 + p, t * D:(t + 1) * D], rsum[:, b:b + 1],
                                                    x[:, b, :], ALU.mult, ALU.add)
                last.then_inc(x_added, 1)

            def boundary(block, add, done=0):
                nb = norms_before(block + 1)
                if block + 1 >= blocks:
                    for p in range(done, PAIRS):
                        add(block, p)
                    return
                for i in range(PAIRS + 2):
                    if i < PAIRS:
                        if i >= done:
                            add(block, i)
                        stats(block + 1, i)
                    if 1 <= i <= PAIRS:
                        normal(block + 1, i - 1)
                    if i >= 2:
                        low(nb + i - 2, i - 2, 4 + i - 2)

            def rsqrt(v, y, a, b_):
                n = step(dve.tensor_scalar(a.bitcast(I32), v.bitcast(I32), 1, None, ALU.logical_shift_right))
                dve.wait_ge(dve_step, n)
                n = step(dve.tensor_scalar(y.bitcast(I32), a.bitcast(I32), -1.0, float(0x5F3759DF), ALU.mult, ALU.add))
                for _ in range(3):
                    dve.wait_ge(dve_step, n)
                    n = step(dve.tensor_tensor(a, y, y, ALU.mult))
                    dve.wait_ge(dve_step, n)
                    n = step(dve.tensor_tensor(b_, a, v, ALU.mult))
                    dve.wait_ge(dve_step, n)
                    n = step(dve.tensor_scalar(a, b_, -0.5, 1.5, ALU.mult, ALU.add))
                    dve.wait_ge(dve_step, n)
                    n = step(dve.tensor_tensor(y, y, a, ALU.mult))
                dve.wait_ge(dve_step, n)

            def front0(b):
                dve.wait_ge(sc_ps, b + 1)
                if b >= 2:
                    dve.wait_ge(ex_ready, b - 1)
                s, w, m = sc[:, b % 2, :], work[:, b % 2, :], top[:, b % 2, :]
                dve.tensor_scalar(s, ps[:, b % 2, (b % 2) * P:(b % 2 + 1) * P], cwork[:, 7:8], None, ALU.mult).then_inc(sc_read, 1)
                dve.wait_ge(sc_read, b + 1)
                n = step(dve.max(m[:, 0:8], s))
                dve.wait_ge(dve_step, n)
                dve.tensor_scalar(negm[:, b % 2:b % 2 + 1], m[:, 0:1], -1.0, None, ALU.mult).then_inc(negm_ready, 1)
                for r in range(1, (CLIP + 7) // 8):
                    n = step(dve.match_replace(w, m[:, 8 * r - 8:8 * r], s if r == 1 else w, NEG))
                    dve.wait_ge(dve_step, n)
                    n = step(dve.max(m[:, 8 * r:8 * r + 8], w))
                    dve.wait_ge(dve_step, n)
                dve.wait_ge(ex_ready, b + 1)
                if b >= 2:
                    dve.wait_ge(ept_ps, b - 1)
                n = step(dve.scalar_tensor_tensor(ep[:, b % 2, :], s, m[:, CLIP - 1:CLIP], ex[:, b % 2, :],
                                                  ALU.is_ge, ALU.mult))
                dve.wait_ge(dve_step, n)
                n = step(dve.tensor_reduce(esum[:, b:b + 1], ep[:, b % 2, :], AX.X, ALU.add))
                dve.wait_ge(dve_step, n)
                dve.reciprocal(rsum[:, b:b + 1], esum[:, b:b + 1]).then_inc(ep_ready, 1)

            def front2(b):
                z = B + b
                dve.wait_ge(sc_ps, z + 1)
                dve.wait_ge(ex_ready, z - 1)
                s, w = sc[:, z % 2, :], work[:, z % 2, :]
                dve.scalar_tensor_tensor(w, ps[:, z % 2, (b % 2) * P:(b % 2 + 1) * P], D ** -0.5,
                                         maskf[:, b, :], ALU.mult, ALU.mult).then_inc(sc_read, 1)
                dve.wait_ge(sc_read, z + 1)
                n = step(dve.tensor_tensor(s, w, maskb[:, b, :], ALU.add))
                dve.wait_ge(dve_step, n)
                dve.tensor_reduce(negm[:, z % 2:z % 2 + 1], s, AX.X, ALU.max, negate=True).then_inc(negm_ready, 1)

            def scale2(p):
                dve.wait_ge(ex_ready, B + 2 * p + 2)
                two = slice(2 * p, 2 * p + 2)
                n = step(dve.reciprocal(rsum[:, two], esum[:, two]))
                dve.wait_ge(dve_step, n)
                n = step(dve.tensor_tensor(rsum[:, two], rsum[:, two], valid[:, two], ALU.mult))
                dve.wait_ge(dve_step, n)

            def low_up(n, c, i):
                f, g = FFN[n], FFN[n].base + c
                dve.wait_ge(wup_hi, after(i, g + 1, 2))
                u = f.width - D
                dve.tensor_tensor(wup_l[:, g % 2, 0:u], wraw[:, g % 2, 0:u], wup_h[:, g % 2, 0:u].bitcast(F32),
                                  ALU.subtract).then_inc(wup_lo, 1)

            def low_down(n, c, i):
                f, g = FFN[n], FFN[n].base + c
                dve.wait_ge(wdn_hi, after(i, g + 1, 2))
                dve.tensor_tensor(wdn_l[:, g % 2, :], wraw[:, g % 2, f.width - D:f.width], wdn_h[:, g % 2, :].bitcast(F32),
                                  ALU.subtract).then_inc(wdn_lo, 1)

            def chunk(n, c, i):
                f, g = FFN[n], FFN[n].base + c
                nxt = (n, c + 1) if c + 1 < f.chunks else (n + 1, 0)
                if g + 1 < CHUNKS:
                    low_up(*nxt, i)
                slot = gated(n, c) % 2
                if not f.up and c >= f.plain:
                    dve.wait_ge(g_loaded[slot], after(i, 16 * g_loads(n, c), 16 * len(segments(n, f.peeled))))
                for h in range(2):
                    if g:
                        dve.wait_ge(tl_ready, after(i, 2 * (g - 1) + h + 1, 4))
                    if not f.up or c < f.plain:
                        dve.wait_ge(s_ready, after(i, 2 * g + h + 1, 4))
                    else:
                        before = sum(2 * (FFN[m].chunks - FFN[m].plain) for m in range(1, n))
                        dve.wait_ge(sg_ready, after(i, before + 2 * (c - f.plain) + h + 1, 4))
                    if not f.up and c < f.plain:
                        dve.tensor_copy(tt[:, h, :], s_act[:, h, :]).then_inc(t_ready, 1)
                    elif not f.up:
                        dve.tensor_tensor(tt[:, h, :], s_act[:, h, :], gb[:, slot, h * HALF:(h + 1) * HALF],
                                          ALU.mult).then_inc(t_ready, 1)
                    else:
                        a = s_act if c < f.plain else sg
                        dve.tensor_tensor(tt[:, h, :], a[:, h, :], ps[:, 2 * h + 1, :], ALU.mult).then_inc(t_ready, 1)
                if g + 1 < CHUNKS:
                    low_down(*nxt, i)
                for h in range(2):
                    dve.wait_ge(th_ready, after(i, 2 * g + h + 1, 4))
                    half = slice(h * HALF, (h + 1) * HALF)
                    dve.tensor_tensor(tl[:, g % 2, half], tt[:, h, :], th[:, g % 2, half].bitcast(F32),
                                      ALU.subtract).then_inc(tl_ready, 1)

            def route(n, h):
                f = FFN[n]
                r = 2 * n + h
                e, rows_ = f.experts, f.gate_rows
                L, E, M, T8, S = lg[:, h], le[:, h], lm[:, h], m8[:, h], gsum[:, h]
                dve.wait_ge(lg_ps, r + 1)
                src = ps[:, 5 + 2 * h, 0:4 * LP].rearrange("p (t e) -> p t e", e=LP)[:, :, 0:rows_]
                k = step(dve.tensor_copy(L[:, :, 0:rows_], src))
                dve.wait_ge(dve_step, k)
                for t in range(4):
                    k = step(dve.max(T8[:, t, :], L[:, t, 0:e]))
                dve.wait_ge(dve_step, k)
                dve.tensor_tensor(E[:, :, 0:e], L[:, :, 0:e], T8[:, :, 0:1].broadcast_to([P, 4, e]), ALU.subtract).then_inc(ld_ready, 1)
                k = step(dve.tensor_tensor(M[:, :, 0:e], L[:, :, 0:e], T8[:, :, f.top - 1:f.top].broadcast_to([P, 4, e]), ALU.is_ge))
                dve.wait_ge(dve_step, k)
                dve.wait_ge(le_ready, r + 1)
                k = step(dve.tensor_tensor(M[:, :, 0:e], M[:, :, 0:e], E[:, :, 0:e], ALU.mult))
                dve.wait_ge(dve_step, k)
                k = step(dve.tensor_reduce(S[:, 0:4], M[:, :, 0:e], AX.X, ALU.add))
                dve.wait_ge(dve_step, k)
                k = step(dve.reciprocal(S[:, 4:8], S[:, 0:4]))
                if rows_ > e:
                    k = step(dve.tensor_scalar(S[:, 8:12], E[:, :, e], 1.0, None, ALU.add))
                    dve.wait_ge(dve_step, k)
                    k = step(dve.reciprocal(M[:, :, e], S[:, 8:12]))
                dve.wait_ge(dve_step, k)
                dve.tensor_tensor(M[:, :, 0:e], M[:, :, 0:e], S[:, 4:8].unsqueeze(2).broadcast_to([P, 4, e]), ALU.mult).then_inc(gw_ready, 1)

            def experts(n):
                if n == 0:
                    k = step(dve.memset(gt[0:FFN[0].experts + 1, :], 1.0))
                for h in range(2):
                    route(n, h)
                every_chunk(dve, n, chunk)
                boundary(2 * n + 1, add_bank)

            def squares(z):
                dve.wait_ge(qk_sq, z + 1)
                dve.tensor_reduce(ss[:, z % 4, :], sq[:, z % 2, :].rearrange("p (n d) -> p n d", d=HD1),
                                  AX.X, ALU.add).then_inc(ss_read, 1)

            def scales(z):
                dve.wait_ge(ss_read, z + 1)
                flat = lambda a: a[:, :, :].rearrange("p t n -> p (t n)")
                n = step(dve.tensor_scalar(flat(ss), flat(ss), 1.0 / HD1, RMS_EPS, ALU.mult, ALU.add))
                dve.wait_ge(dve_step, n)
                rsqrt(flat(ss), flat(nw_y), flat(nw_a), flat(nw_b))

            def stack(z):
                if z >= 2:
                    dve.wait_ge(st_hi, z - 1)
                heads = lambda a: a.rearrange("p (n d) -> p n d", d=HD1)
                dve.tensor_tensor(heads(qn[:, z % 2, :]), heads(qf[:, z % 4, :]),
                                  nw_y[:, z % 4, :].unsqueeze(2).broadcast_to([P, HEADS1, HD1]), ALU.mult).then_inc(qn_ready, 1)
                dve.wait_ge(st_hi, z + 1)
                lows = (1, 3) if z < B else (2, 3)
                for r in lows:
                    last = dve.tensor_tensor(stk[:, z % 2, :, r, :], heads(qn[:, z % 2, :]), stk[:, z % 2, :, 0, :], ALU.subtract)
                last.then_inc(st_lo, 1)

            def mixed(w):
                b, s = w // 2, w % 2
                dve.wait_ge(o1_ps, 4 * w + 4)
                src = ps[:, 4 + s, 0:16 * VW].rearrange("p (n c) -> p n c", c=VW)
                parts = src[:, :, 0:3 * HD1].rearrange("p n (r d) -> p n d r", d=HD1)
                step(dve.tensor_reduce(o3[:, s, :, :], parts, AX.X, ALU.add))
                dve.reciprocal(r3[:, s, :], src[:, :, 3 * HD1]).then_inc(o1_read, 1)
                dve.wait_ge(o1_read, w + 1)
                n = step(dve.tensor_tensor(oy[:, s, :, :], o3[:, s, :, :], r3[:, s, :].unsqueeze(2).broadcast_to([P, 16, HD1]), ALU.mult))
                dve.wait_ge(dve_step, n)
                dst = x[:, b, s * P:(s + 1) * P]
                last = dve.tensor_tensor(dst, dst, oy[:, s, :, :].rearrange("p n d -> p (n d)"), ALU.add)
                if w % 4 == 3:
                    last.then_inc(x_added, 1)

            def attend1():
                nb = norms_before(2)
                for m in range(4):
                    dve.wait_ge(pre_hi, 10 + m)
                    half = slice((m % 2) * HALF, (m % 2 + 1) * HALF)
                    dve.tensor_tensor(mk_l[:, m // 2, half], ps[:, m, :], mk_h[:, m // 2, half].bitcast(F32),
                                      ALU.subtract).then_inc(pre_lo, 1)

                def tile(b):
                    for u in range(8 * b, 8 * b + 8):
                        dve.wait_ge(eh_ready, u + 1)
                        dve.tensor_tensor(el[:, u % 4, :], e1[:, u % 4, :], eh[:, u % 4, :], ALU.subtract).then_inc(el_ready, 1)
                        if u % 4 == 1 and u > 4:
                            mixed(u // 4 - 1)
                for b in range(4):
                    squares(B + b)
                scales(B + 3)
                for b in range(4):
                    stack(B + b)
                for what, b in SCHEDULE1:
                    {"raw": lambda b: squares(B + b), "tile": tile, "scale": lambda b: scales(B + b),
                     "stack": lambda b: stack(B + b)}[what](b)
                mixed(2 * B - 1)
                boundary(2, None, done=PAIRS)

            def retain():
                nb = norms_before(6)
                dve.wait_ge(a_ps, 1)
                for h in range(2):
                    n = step(dve.tensor_copy(a1[:, h, :], ps[:, h, 0:P]))
                    dve.wait_ge(dve_step, n)
                    n = step(dve.tensor_tensor(a1[:, h, :], ps[:, h, P:2 * P], a1[:, h, :], ALU.add))
                    dve.wait_ge(dve_step, n)
                    n = step(dve.tensor_tensor(a1[:, h, :], a1[:, h, :], dec[:, h, :], ALU.mult))
                    dve.wait_ge(dve_step, n)
                    n = step(dve.scalar_tensor_tensor(at[:, h, :], a1[:, h, :], -1.0, a1[:, h, :], ALU.mult, ALU.max))
                    dve.wait_ge(dve_step, n)
                    dve.tensor_scalar(at[:, h, :], at[:, h, :], 1.0, None, ALU.max).then_inc(a_ready, 1)
                for b in range(B):
                    dve.wait_ge(o_ps, 2 * (b // 4) + 2)
                    for h in range(2):
                        n = step(dve.bn_stats(st3[:, b, h, :], ps[:, 4 + 2 * (b // 4) + h, (b % 4) * P:(b % 4 + 1) * P]))
                dve.wait_ge(dve_step, n)
                for b in range(B):
                    n = step(dve.bn_aggr(mv3[:, b, :], st3[:, b, :, :].rearrange("p h s -> p (h s)")))
                dve.wait_ge(dve_step, n)
                dve.tensor_scalar(ve3[:, :], mv3[:, :, 1], GN_EPS, None, ALU.add).then_inc(mv3_ready, 1)
                dve.wait_ge(rs3_ready, 1)

                def finish(b):
                    p, q = b // 2, nb + PAIRS + b // 2
                    dve.wait_ge(yb_ready, b + 1)
                    dve.tensor_tensor(yc[:, b % 2, :], yb[:, b % 2, :], bet[:, :], ALU.add).then_inc(yc_ready, 1)
                    dve.wait_ge(yc_ready, b + 1)
                    dve.wait_ge(wr_ready, b + 1)
                    dve.wait_ge(xt_ps, q - 1)
                    last = dve.tensor_tensor(xn[:, (2 * q + b % 2) % 4, :], yc[:, b % 2, :], wr[:, b, :], ALU.mult)
                    if b % 2:
                        last.then_inc(xn_ready, 1)
                    if b in (5, 7):
                        low(q - 2, p - 2, p % 2)

                for b in range(B):
                    if b >= 2:
                        dve.wait_ge(yb_ready, b - 1)
                    for h in range(2):
                        last = dve.tensor_scalar(ya[:, b % 2, h * P:(h + 1) * P],
                                                 ps[:, 4 + 2 * (b // 4) + h, (b % 4) * P:(b % 4 + 1) * P],
                                                 mv3[:, b, 0:1], rs3[:, b:b + 1], ALU.subtract, ALU.mult)
                    last.then_inc(ya_ready, 1)
                    if b:
                        finish(b - 1)
                finish(B - 1)
                for p in (2, 3):
                    low(nb + PAIRS + p, p, p % 2)
                boundary(6, add_bank)

            dve.wait_ge(ld_x, 16)
            for n, (_, dst, src) in enumerate(SPLITS(ld_c, ld_s, craw, sraw, cl, sw_l)):
                hi = SPLITS(ld_c, ld_s, craw, sraw, ch, sw_h)[n][1]
                dve.wait_ge(split_hi, n + 1)
                dve.tensor_tensor(dst, src, hi.bitcast(F32), ALU.subtract).then_inc(split_lo, 1)
            for m in range(4):
                dve.wait_ge(pre_hi, m + 1)
                half = slice((m % 2) * HALF, (m % 2 + 1) * HALF)
                dve.tensor_tensor(mk_l[:, m // 2, half], ps[:, m, :], mk_h[:, m // 2, half].bitcast(F32),
                                  ALU.subtract).then_inc(pre_lo, 1)
            dve.wait_ge(pre_hi, 9)
            dve.tensor_tensor(g_l[:, :, :], ps[:, 0, 0:2 * P].rearrange("p (h d) -> p h d", h=2), g_h[:, :, :].bitcast(F32),
                              ALU.subtract).then_inc(pre_lo, 1)
            dve.wait_ge(coef_exp, 1)
            n = step(dve.tensor_scalar(cwork[:, 2:3], cwork[:, 0:1], 1.0, None, ALU.add))
            dve.wait_ge(dve_step, n)
            n = step(dve.reciprocal(cwork[:, 3:4], cwork[:, 2:3]))
            n = step(dve.tensor_tensor(cwork[:, 4:5], cvec[:, 0:1], cvec[:, 1:2], ALU.subtract))
            dve.wait_ge(dve_step, n)
            n = step(dve.scalar_tensor_tensor(cwork[:, 5:6], cwork[:, 4:5], cwork[:, 3:4], cvec[:, 1:2], ALU.mult, ALU.add))
            dve.wait_ge(dve_step, n)
            n = step(dve.tensor_scalar(cwork[:, 7:8], cwork[:, 5:6], cwork[:, 1:2], D ** -0.5, ALU.mult, ALU.mult))
            dve.wait_ge(dve_step, n)
            for b in range(B):
                squares(b)
                heads = lambda a: a.rearrange("p (n d) -> p n d", d=HD1)
                dve.wait_ge(v1_ready, b + 1)
                if b >= 2:
                    dve.wait_ge(v2_ready, b - 1)
                dve.tensor_tensor(heads(vres[:, b % 2, 0, :]), heads(ps[:, 4 + b % 2, 0:D]), vp[:, b, :, 0:HD1],
                                  ALU.subtract).then_inc(r1_ready, 1)
                dve.wait_ge(v2_ready, b + 1)
                dve.tensor_tensor(vp[:, b, :, 2 * HD1:3 * HD1], heads(vres[:, b % 2, 0, :]), vp[:, b, :, HD1:2 * HD1],
                                  ALU.subtract).then_inc(v3_ready, 1)
                if b % 4 == 3:
                    scales(b)
                    for d in range(b - 3, b + 1):
                        stack(d)
            if blocks > 1:
                low_up(0, 0, None)
                low_down(0, 0, None)

            for i in range(PAIRS + 2):
                if i < PAIRS:
                    stats(0, i)
                if 1 <= i <= PAIRS:
                    normal(0, i - 1)
                if i >= 2:
                    low(i - 2, i - 2, 4 + i - 2)
            for b in range(B):
                front0(b)
            boundary(0, add_scaled)
            if blocks > 1:
                experts(0)
            if blocks > 2:
                attend1()
            if blocks > 3:
                experts(1)
            if blocks > 4:
                dve.tensor_copy(maskf[:, :, :], masku[:, :, :]).then_inc(mask_ready, 1)
                dve.wait_ge(mask_ready, 1)
                dve.tensor_scalar(maskb[:, :, :], maskf[:, :, :], -1.0, 1e30, ALU.add, ALU.mult).then_inc(mask_ready, 1)
                dve.tensor_reduce(valid[:, :], maskf[:, :, :], AX.X, ALU.max).then_inc(mask_ready, 1)
                dve.wait_ge(mask_ready, 3)
                for b in range(B):
                    front2(b)
                for p in range(PAIRS):
                    scale2(p)
                boundary(4, add_scaled)
            if blocks > 5:
                experts(2)
            if blocks > 6:
                retain()
            if blocks > 7:
                experts(3)

def pack_small(mats, gates, wh):
    import numpy as np
    cols = [m[k * P:(k + 1) * P] for m in mats for k in range(K)]
    cols += [g[k * P:(k + 1) * P] for g in gates for k in range(K)]
    cols += [wh[h] for h in range(2)] + [wh[h].T for h in range(2)]
    return np.ascontiguousarray(np.concatenate(cols, axis=1))


def pack_experts(first, second, bias=None):
    import numpy as np
    chunks = second.shape[0] // P
    out = []
    for c in range(chunks):
        u = slice(c * P, (c + 1) * P)
        cols = [m[k * P:(k + 1) * P, u] for m in first for k in range(K)] + [second[u]]
        if bias is not None:
            cols.append(bias[u, None])
        out.append(np.concatenate(cols, axis=1))
    return np.ascontiguousarray(np.stack(out))


def decay_table():
    import numpy as np
    gam = 1.0 - 2.0 ** (-5.0 - np.arange(2, dtype=np.float64))
    s, t = np.arange(P)[:, None], np.arange(P)[None, :]
    d = np.where(t <= s, gam[:, None, None] ** (t - s), 0.0)
    d = d / np.sqrt(d.sum(axis=-1))[:, None, :] / np.sqrt(float(P))
    return np.ascontiguousarray(d.transpose(2, 0, 1).astype(np.float32))


def kernel(**inputs):
    import numpy as np
    import concourse.bacc as bacc
    from concourse.bass_utils import run_bass_kernel_spmd as run

    a = {k: np.asarray(v) for k, v in inputs.items()}
    cat = np.concatenate

    def units(w):
        return w.transpose(1, 0, 2).reshape(w.shape[1], -1)

    wkv = cat([a["L1_xattn_Wk"], a["L1_xattn_Wv"]], axis=0)
    small = pack_small(
        [a["L0_xattn_W_qkv"][:D], a["L0_xattn_W_o"].T, wkv[0::2].T, wkv[1::2].T, a["L1_xattn_Wq"].T,
         a["L3_xattn_wg_w"], a["L3_xattn_wo_w"]],
        [a["L0_ffn_gate_w"], a["L1_ffn_gate_w"].T,
         cat([a["L2_ffn_router_w"], a["L2_ffn_shared_expert_gate_w"]], axis=0).T, a["L3_ffn_w_gate"]],
        a["L3_xattn_Wh"])

    w0 = pack_experts([cat([a["L0_ffn_shared_w1"], units(a["L0_ffn_w1"])], axis=1)],
                      cat([a["L0_ffn_shared_w2"], a["L0_ffn_w2"].reshape(-1, D)], axis=0),
                      cat([a["L0_ffn_shared_b1"], a["L0_ffn_b1"].reshape(-1)]))
    b2 = cat([a["L0_ffn_b2"], a["L0_ffn_shared_b2"][None]], axis=0)

    def first1(shared, w):
        zero = np.zeros((D, 3 * P - shared.shape[1]), np.float32)
        return cat([shared, zero, units(w[:, :, P:]), units(w[:, :, :P])], axis=1)

    zero = np.zeros((3 * P - 2 * I1, D), np.float32)
    w1 = pack_experts([first1(a["L1_ffn_sw1"], a["L1_ffn_w1"]), first1(a["L1_ffn_sw3"], a["L1_ffn_w3"])],
                      cat([a["L1_ffn_sw2"], zero, a["L1_ffn_w2"][:, P:].reshape(-1, D), a["L1_ffn_w2"][:, :P].reshape(-1, D)], axis=0))

    gu, zero = a["L2_ffn_gate_up_proj"], np.zeros((64, D), np.float32)
    w2 = pack_experts([cat([a["L2_ffn_shared_gate_w"], zero, gu[:, :64].reshape(-1, D)], axis=0).T,
                       cat([a["L2_ffn_shared_up_w"], zero, gu[:, 64:].reshape(-1, D)], axis=0).T],
                      cat([a["L2_ffn_shared_down_w"].T, zero, a["L2_ffn_down_proj"].transpose(0, 2, 1).reshape(-1, D)], axis=0))

    gu, sh = a["L3_ffn_w_gate_up"], a["L3_ffn_w_sh_gate_up"]
    w3 = pack_experts([cat([sh[:, :512], units(gu[:, :, :P])], axis=1), cat([sh[:, 512:], units(gu[:, :, P:])], axis=1)],
                      cat([a["L3_ffn_w_sh_down"], a["L3_ffn_w_down"].reshape(-1, D)], axis=0))

    arrays = {
        "x_in": a["x"], "ctx_t": np.ascontiguousarray(a["ctx_2048"].reshape(T, D).T), "ctx_n": a["ctx_2048"],
        "mask_in": a["mask_BxS2_bk0"], "small_in": small,
        "coef_in": np.stack([a["L0_xattn_beta_q"], a["L0_xattn_beta_k"], a["L0_xattn_gate"], a["L0_xattn_log_tau"]]),
        "b2_in": b2, "gamma_in": a["L3_xattn_gn_gamma"], "beta_in": a["L3_xattn_gn_beta"],
        "decay_in": decay_table(), "ident_in": np.eye(P, dtype=np.float32),
        "w0_in": w0, "w1_in": w1, "w2_in": w2, "w3_in": w3,
    }
    arrays = {k: np.ascontiguousarray(v) for k, v in arrays.items()}
    nc = bacc.Bacc("TRN2", target_bir_lowering=False, num_devices=1)
    ap = {k: nc.dram_tensor(k, v.shape, mybir.dt.from_np(v.dtype), kind="ExternalInput").ap() for k, v in arrays.items()}
    ws = [ap.pop(f"w{n}_in") for n in range(4)]
    gates = [nc.dram_tensor(f"gates{n}", (FFN[n].gate_rows, T), F32, kind="Internal").ap() for n in range(4)]
    out = nc.dram_tensor("y_out", (B, P, D), F32, kind="ExternalOutput").ap()
    program(nc, **ap, w_in=ws, gates=gates, out=out, blocks=BLOCKS)
    r = run(nc, [arrays], core_ids=[0])
    return r.results[0]["y_out"]
```

```python
from contextlib import ExitStack

import concourse.bass as bass
from concourse import mybir

F32 = mybir.dt.float32
F32R = mybir.dt.float32r
F16 = mybir.dt.float16
BF16 = mybir.dt.bfloat16
I32 = mybir.dt.int32
U8 = mybir.dt.uint8
ALU = mybir.AluOpType
ACT = mybir.ActivationFunctionType
AX = mybir.AxisListType

P = 128
D = 256
K = D // P
B = 8
T = B * P
PAIRS = B // 2
HALF = T // 2
BLOCKS = 8
LN_EPS = 1e-5
RMS_EPS = 1e-6
GN_EPS = 1e-3
HEADS1 = 32
HD1 = D // HEADS1
GROUPS1 = HEADS1 // 4
VW = 3 * HD1 + 1
CLIP = 54
NEG = -3.0e38


TAIL = 2


class Ffn:

    def __init__(self, base, chunks, peeled, plain, experts, gate_rows, top, up, act):
        self.base, self.chunks, self.peeled, self.plain = base, chunks, peeled, plain
        self.experts, self.gate_rows, self.top, self.up, self.act = experts, gate_rows, top, up, act
        self.steps = (chunks - peeled - TAIL) // 2
        self.width = (K * P * (2 if up else 1)) + D
        self.bias = not up
        assert (chunks - peeled - TAIL) % 2 == 0


FFN = [
    Ffn(0, 10, 2, 2, 8, 8, 2, False, ACT.Gelu),
    Ffn(10, 14, 6, 3, 8, 8, 2, True, ACT.Silu),
    Ffn(24, 33, 3, 0, 64, 65, 8, True, ACT.Silu),
    Ffn(57, 12, 4, 4, 8, 8, 2, True, ACT.Silu),
]
I1 = 176
R1 = I1 - P
GATED = [sum(f.chunks - f.plain for f in FFN[:n]) for n in range(len(FFN))]

SMALL = ["wq0", "wo0", "wk1", "wv1", "wq1", "wg3", "wo3"]
GATE_AT = []
_at = len(SMALL) * K * D
for _f in FFN:
    GATE_AT.append(_at)
    _at += K * _f.gate_rows
WH_AT = _at
LP = 66
LD_M = 16 * 6
SCHEDULE1 = [("tile", 0), ("raw", 4), ("raw", 5), ("tile", 1), ("raw", 6), ("raw", 7), ("scale", 7),
             ("tile", 2), ("stack", 4), ("stack", 5), ("tile", 3), ("stack", 6), ("stack", 7),
             ("tile", 4), ("tile", 5), ("tile", 6), ("tile", 7)]
WHT_AT = WH_AT + D
SMALL_W = WHT_AT + D


def SPLITS(ld_c, ld_s, craw, sraw, c_part, s_part):
    first, second = K * D, 4 * K * D
    return [(ld_s, s_part[:, 0:first], sraw[:, 0:first]),
            (ld_c, c_part[:, 0, :], craw[:, 0, :]), (ld_c, c_part[:, 1, :], craw[:, 1, :]),
            (ld_s, s_part[:, first:second], sraw[:, first:second]),
            (ld_s, s_part[:, second:WHT_AT], sraw[:, second:WHT_AT])]


def program(nc, x_in, ctx_t, ctx_n, mask_in, small_in, coef_in, b2_in, gamma_in, beta_in,
            decay_in, ident_in, w_in, gates, out, blocks=8):
    with ExitStack() as ctx:
        def sb(name, shape, dt=F32):
            return ctx.enter_context(nc.sbuf_tensor(name, shape, dt))

        def sem(name):
            return ctx.enter_context(nc.semaphore(name))

        x = sb("x", [P, B, D])
        xs = sb("xs", [P, K, B, 2, P], F32R)
        xn = sb("xn", [P, 4, D])
        ch = sb("ch", [P, K, T], F32R)
        cl = sb("cl", [P, K, T], F32R)
        mk_h = sb("mk_h", [P, 2, T], F32R)
        mk_l = sb("mk_l", [P, 2, T], F32R)
        vw = sb("vw", [P, 2, B, P])
        vw0 = vw[:, :, :, :].rearrange("p h b e -> p (h b e)").rearrange("p (b d) -> p b d", b=B)
        two = ExitStack()
        cn = two.enter_context(nc.sbuf_tensor("cn", [P, B, D], F32))
        two.close()
        kst = sb("kst", [P, B, GROUPS1, P], F16)
        vp = sb("vp", [P, B, HEADS1, VW], BF16)
        sw_h = sb("sw_h", [P, WHT_AT], F32R)
        sw_l = sb("sw_l", [P, WHT_AT], F32R)
        g_h = sb("g_h", [P, 2, P], F32R)
        g_l = sb("g_l", [P, 2, P], F32R)
        ident = sb("ident", [P, P])
        ident16 = sb("ident16", [P, P], F16)
        wraw = sb("wraw", [P, 2, 3 * D])
        wup_h = sb("wup_h", [P, 2, 2 * D], F32R)
        wup_l = sb("wup_l", [P, 2, 2 * D], F32R)
        wdn_h = sb("wdn_h", [P, 2, D], F32R)
        wdn_l = sb("wdn_l", [P, 2, D], F32R)
        b2 = sb("b2", [FFN[0].experts + 1, D])
        gam = sb("gam", [P, D])
        bet = sb("bet", [P, D])
        dec = sb("dec", [P, 2, P])
        masku = sb("masku", [P, B, P], U8)
        stat = sb("stat", [P, 2, 2, 6])
        mv = sb("mv", [P, 2, 2, 2])
        var_eps = sb("var_eps", [P, 2, 2])
        rstd = sb("rstd", [P, 2, 2])
        mhalf = sb("mhalf", [P, 8])
        cvec = sb("cvec", [P, 4])
        cwork = sb("cwork", [P, 8])
        negm = sb("negm", [P, 2])
        esum = sb("esum", [P, B])
        rsum = sb("rsum", [P, B])
        valid = sb("valid", [P, B])
        sc = sb("sc", [P, 2, P])
        work = sb("work", [P, 2, P])
        ex = sb("ex", [P, 2, P])
        ep = sb("ep", [P, 2, P])
        ept = sb("ept", [P, 2, P])
        top = sb("top", [P, 2, 56])

        early = ExitStack()
        craw = early.enter_context(nc.sbuf_tensor("craw", [P, K, T], F32))
        sraw = early.enter_context(nc.sbuf_tensor("sraw", [P, SMALL_W], F32))
        early.close()

        mid = ExitStack()

        def sbm(name, shape, dt=F32):
            return mid.enter_context(nc.sbuf_tensor(name, shape, dt))
        s_act = sbm("s_act", [P, 2, HALF])
        sg = sbm("sg", [P, 2, HALF])
        tt = sbm("tt", [P, 2, HALF])
        gb = sbm("gb", [P, 2, T])
        gt = sbm("gt", [P, T])
        routing = ExitStack()

        def sbr(name, shape, dt=F32):
            return routing.enter_context(nc.sbuf_tensor(name, shape, dt))
        lgt = sbr("lgt", [P, 2, HALF])
        lg = sbr("lg", [P, 2, 4, 65])
        le = sbr("le", [P, 2, 4, 65])
        lm = sbr("lm", [P, 2, 4, 65])
        m8 = sbr("m8", [P, 2, 4, 8])
        gsum = sbr("gsum", [P, 2, 16])
        routing.close()
        th = sbm("th", [P, 2, T], F32R)
        tl = sbm("tl", [P, 2, T], F32R)
        mid.close()

        att = ExitStack()

        def sba(name, shape, dt=F32):
            return att.enter_context(nc.sbuf_tensor(name, shape, dt))
        maskf = sba("maskf", [P, B, P])
        maskb = sba("maskb", [P, B, P])
        at = sba("at", [P, 2, P])
        a1 = sba("a1", [P, 2, P])
        wr = sba("wr", [P, B, D])
        ya = sba("ya", [P, 2, D])
        yb = sba("yb", [P, 2, D])
        yc = sba("yc", [P, 2, D])
        st3 = sba("st3", [P, B, 2, 6])
        mv3 = sba("mv3", [P, B, 2])
        ve3 = sba("ve3", [P, B])
        rs3 = sba("rs3", [P, B])
        att.close()

        one = ExitStack()

        def sb1(name, shape, dt=F32):
            return one.enter_context(nc.sbuf_tensor(name, shape, dt))
        sq = sb1("sq", [P, 2, D])
        ss = sb1("ss", [P, 4, HEADS1])
        nw_a = sb1("nw_a", [P, 4, HEADS1])
        nw_b = sb1("nw_b", [P, 4, HEADS1])
        nw_h = sb1("nw_h", [P, 4, HEADS1])
        qf = sb1("qf", [P, 4, D])
        vres = sb1("vres", [P, 2, 2, D])
        stk = sb1("stk", [P, 2, HEADS1, 4, HD1], F16)
        nw_y = sb1("nw_y", [P, 4, HEADS1])
        qst = sb1("qst", [P, 4, GROUPS1, P], F16)
        e1 = sb1("e1", [P, 4, HALF])
        eh = sb1("eh", [P, 4, HALF], F16)
        el = sb1("el", [P, 4, HALF], F16)
        o3 = sb1("o3", [P, 2, 16, HD1])
        oy = sb1("oy", [P, 2, 16, HD1])
        r3 = sb1("r3", [P, 2, 16])
        one.close()

        ps = ctx.enter_context(nc.psum_tensor("ps", [P, 8, 512], F32))
        ps16 = ps[:, :, :].bitcast(F16)

        ld_x, ld_c, ld_s, ld_m, ld_n = sem("ld_x"), sem("ld_c"), sem("ld_s"), sem("ld_m"), sem("ld_n")
        w_loaded = [sem("w_loaded0"), sem("w_loaded1")]
        g_loaded = [sem("g_loaded0"), sem("g_loaded1")]
        g_stored, stored = sem("g_stored"), sem("stored")
        const_ready = sem("const_ready")
        dve_step = sem("dve_step")
        ld_i = sem("ld_i")
        split_hi, split_lo, small_lo = sem("split_hi"), sem("split_lo"), sem("small_lo")
        pre_ps, pre_hi, pre_lo = sem("pre_ps"), sem("pre_hi"), sem("pre_lo")
        mv_ready, rstd_ready = sem("mv_ready"), sem("rstd_ready")
        xn_ready, xt_ps, xh_ready, xl_ready = sem("xn_ready"), sem("xt_ps"), sem("xh_ready"), sem("xl_ready")
        coef_exp = sem("coef_exp")
        sc_ps, sc_read, negm_ready, ex_ready = sem("sc_ps"), sem("sc_read"), sem("negm_ready"), sem("ex_ready")
        ep_ready, ept_ps, ept_ready = sem("ep_ready"), sem("ept_ps"), sem("ept_ready")
        y_ps, x_added = sem("y_ps"), sem("x_added")
        up_ps, s_ready, sg_ready, t_ready = sem("up_ps"), sem("s_ready"), sem("sg_ready"), sem("t_ready")
        th_ready, tl_ready, dn_ps = sem("th_ready"), sem("tl_ready"), sem("dn_ps")
        wup_hi, wup_lo, wdn_hi, wdn_lo = sem("wup_hi"), sem("wup_lo"), sem("wdn_hi"), sem("wdn_lo")
        lt_ps, lt_ready, lg_ps = sem("lt_ps"), sem("lt_ready"), sem("lg_ps")
        ld_ready, le_ready, gw_ready = sem("ld_ready"), sem("le_ready"), sem("gw_ready")
        gt_ps, gt_ready = sem("gt_ps"), sem("gt_ready")
        qk_ps, qk_sq, ss_read = sem("qk_ps"), sem("qk_sq"), sem("ss_read")
        qn_ready, st_hi, st_lo = sem("qn_ready"), sem("st_hi"), sem("st_lo")
        qt_ps, qt_ready = sem("qt_ps"), sem("qt_ready")
        v_ps, v1_ready, v2_ready, v3_ready, r1_ready = (
            sem("v_ps"), sem("v1_ready"), sem("v2_ready"), sem("v3_ready"), sem("r1_ready"))
        s1_ps, e1_ready, eh_ready, el_ready = sem("s1_ps"), sem("e1_ready"), sem("eh_ready"), sem("el_ready")
        o1_ps, o1_read = sem("o1_ps"), sem("o1_read")
        a_ps, a_ready, o_ps, wg_ps, wr_ready = sem("a_ps"), sem("a_ready"), sem("o_ps"), sem("wg_ps"), sem("wr_ready")
        mv3_ready, rs3_ready, ya_ready, yb_ready = sem("mv3_ready"), sem("rs3_ready"), sem("ya_ready"), sem("yb_ready")
        yc_ready, mask_ready, av_ps = sem("yc_ready"), sem("mask_ready"), sem("av_ps")

        def small(n, k):
            return slice((n * K + k) * D, (n * K + k + 1) * D)

        def key_bank(z):
            return (2, 3)[z % 2] if z < 4 else (1, 3)[z % 2]

        def gate_cols(n, k):
            return slice(GATE_AT[n] + k * FFN[n].gate_rows, GATE_AT[n] + (k + 1) * FFN[n].gate_rows)

        LAYERS = [n for n in range(4) if 2 * n + 1 < blocks]
        CHUNKS = sum(FFN[n].chunks for n in LAYERS)

        def norms_before(block):
            return PAIRS * (block + (1 if block > 6 else 0))

        def after(i, count, rate):
            return count if i is None else rate * i + count

        def every_chunk(eng, n, do):
            f = FFN[n]
            for c in range(f.peeled):
                do(n, c, None)
            with eng.Fori(0, f.steps) as i:
                for u in range(2):
                    do(n, f.peeled + u, i)
            for c in range(f.chunks - TAIL, f.chunks):
                do(n, c, None)

        def gated(n, c):
            return GATED[n] + c - FFN[n].plain

        def segments(n, c):
            f = FFN[n]
            if n == 2:
                return [(0, P, 64)] if c == 0 else [(0, 64, 2 * (c - 1)), (64, 64, 2 * (c - 1) + 1)]
            if n == 1 and c < f.peeled:
                found, r = [], 0
                while r < P:
                    unit = (c - f.plain) * P + r
                    e = unit // R1
                    size = min(P - r, (e + 1) * R1 - unit)
                    found.append((r, size, e))
                    r += size
                return found
            return [(0, P, c - (f.peeled if n == 1 else f.plain))]

        def g_loads(n, c):
            return sum(len(segments(m, d)) for m in range(n + 1) for d in range(FFN[m].plain, FFN[m].chunks)
                       if gated(m, d) % 2 == gated(n, c) % 2 and (m < n or d <= c))

        block_ = ctx.enter_context(nc.Block())

        @block_.sync
        def _(sp):
            sp.dma_start(x[:, :, :], x_in.rearrange("b p d -> p b d")).then_inc(ld_x, 16)
            sp.dma_start(ident[:, :], ident_in).then_inc(ld_i, 16)
            sp.dma_start(craw[:, :, :], ctx_t.rearrange("(k p) t -> p k t", p=P)).then_inc(ld_c, 16)
            sp.dma_start(sraw[:, :], small_in).then_inc(ld_s, 16)
            sp.dma_start(cvec[:, :], coef_in.rearrange("(o c) -> o c", o=1).broadcast_to([P, 4])).then_inc(ld_m, 16)
            sp.dma_start(b2[:, :], b2_in).then_inc(ld_m, 16)
            sp.dma_start(gam[:, :], gamma_in.rearrange("(o c) -> o c", o=1).broadcast_to([P, D])).then_inc(ld_m, 16)
            sp.dma_start(bet[:, :], beta_in.rearrange("(o c) -> o c", o=1).broadcast_to([P, D])).then_inc(ld_m, 16)
            sp.dma_start(dec[:, :, :], decay_in).then_inc(ld_m, 16)
            sp.dma_start(masku[:, :, :], mask_in.rearrange("(o b) m -> o b m", o=1).broadcast_to([P, B, P])).then_inc(ld_m, 16)

            def load(n, c, i):
                f, g = FFN[n], FFN[n].base + c
                if g >= 2:
                    sp.wait_ge(t_ready, after(i, 2 * (g - 1), 4))
                if i is None:
                    src = w_in[n][c]
                else:
                    src = w_in[n][bass.ds(2 * i + c, 1), :, :].rearrange("o p c -> (o p) c")
                sp.dma_start(wraw[:, g % 2, 0:f.width + f.bias], src).then_inc(w_loaded[g % 2], 16)

            for n in LAYERS:
                every_chunk(sp, n, load)

            for p in range(PAIRS):
                sp.wait_ge(x_added, PAIRS * (blocks - 1) + p + 1)
                sp.dma_start(out[2 * p:2 * p + 2].rearrange("b p d -> p b d"),
                             x[:, 2 * p:2 * p + 2, :]).then_inc(stored, 16)
            sp.wait_ge(stored, 16 * PAIRS)

        @block_.gpsimd
        def _(pool):
            pool.memset(mhalf[:, :], -0.5).then_inc(const_ready, 1)
            pool.wait_ge(const_ready, 1)

            def power(block, p):
                r = PAIRS * block + p
                pool.wait_ge(mv_ready, r + 1)
                pool.tensor_tensor(rstd[:, r % 2, :], var_eps[:, r % 2, :], mhalf[:, 0:2],
                                   ALU.pow).then_inc(rstd_ready, 1)

            def norm(block):
                for p in range(PAIRS):
                    power(block, p)

            def third(b):
                heads = lambda a: a.rearrange("p (n d) -> p n d", d=HD1)
                pool.wait_ge(v2_ready, b + 1)
                pool.tensor_tensor(vp[:, b, :, 2 * HD1:3 * HD1], heads(vres[:, b % 2, 0, :]), vp[:, b, :, HD1:2 * HD1],
                                   ALU.subtract).then_inc(v3_ready, 1)

            def stack_low(z):
                pool.wait_ge(st_hi, z + 1)
                for r in (1, 3):
                    last = pool.tensor_tensor(stk[:, z % 2, :, r, :], qf[:, z % 4, :].rearrange("p (n d) -> p n d", d=HD1),
                                              stk[:, z % 2, :, 0, :], ALU.subtract)
                last.then_inc(st_lo, 1)

            def gate(n, c, i):
                f, g = FFN[n], FFN[n].base + c
                if c < f.plain or not f.up:
                    return
                slot = gated(n, c) % 2
                pool.wait_ge(g_loaded[slot], after(i, 16 * g_loads(n, c), 16 * len(segments(n, f.peeled))))
                for h in range(2):
                    pool.wait_ge(s_ready, after(i, 2 * g + h + 1, 4))
                    pool.wait_ge(t_ready, after(i, 2 * (g - 1) + h + 1, 4))
                    pool.tensor_tensor(sg[:, h, :], s_act[:, h, :], gb[:, slot, h * HALF:(h + 1) * HALF],
                                       ALU.mult).then_inc(sg_ready, 1)

            norm(0)
            pool.memset(vp[:, :, :, VW - 1:VW], 1.0).then_inc(const_ready, 1)
            pool.wait_ge(ld_i, 16)
            pool.tensor_copy(ident16[:, :], ident[:, :]).then_inc(const_ready, 1)
            for n in (3, 4):
                _, dst, src = SPLITS(ld_c, ld_s, craw, sraw, cl, sw_l)[n]
                hi = SPLITS(ld_c, ld_s, craw, sraw, ch, sw_h)[n][1]
                pool.wait_ge(split_hi, n + 1)
                pool.tensor_tensor(dst, src, hi.bitcast(F32), ALU.subtract).then_inc(small_lo, 1)
            for p in range(PAIRS):
                if p and blocks > 1:
                    power(1, p - 1)
                for b in (2 * p, 2 * p + 1):
                    third(b)
                if p == PAIRS - 1 and blocks > 1:
                    power(1, p)
                if p % 2:
                    for z in range(2 * p - 2, 2 * p + 2):
                        stack_low(z)
            if blocks > 2:
                norm(2)
                for u in range(8 * B):
                    pool.wait_ge(e1_ready, u + 1)
                    if u >= 4:
                        pool.wait_ge(o1_ps, u - 3)
                    pool.tensor_scalar(eh[:, u % 4, :], e1[:, u % 4, :], 1.0, 0.0,
                                       ALU.mult, ALU.add).then_inc(eh_ready, 1)
            if blocks > 3:
                norm(3)
                every_chunk(pool, 1, gate)
            if blocks > 4:
                norm(4)
            if blocks > 5:
                norm(5)
                every_chunk(pool, 2, gate)
            if blocks > 6:
                norm(6)
                pool.wait_ge(mv3_ready, 1)
                pool.tensor_tensor(rs3[:, :], ve3[:, :], mhalf[:, :], ALU.pow).then_inc(rs3_ready, 1)
                for b in range(B):
                    pool.wait_ge(ya_ready, b + 1)
                    if b >= 2:
                        pool.wait_ge(yc_ready, b - 1)
                    pool.tensor_tensor(yb[:, b % 2, :], ya[:, b % 2, :], gam[:, :], ALU.mult).then_inc(yb_ready, 1)
            if blocks > 7:
                norm(7)
                every_chunk(pool, 3, gate)

        @block_.tensor
        def _(pe):
            def product(dst, lhs, rhs, start=True, stop=True):
                last = None
                for k in range(K):
                    (ah, al), (bh, bl) = lhs(k), rhs(k)
                    for m, (a, b_) in enumerate(((ah, bh), (ah, bl), (al, bh))):
                        last = pe.matmul(dst, a, b_, start=start and k == 0 and m == 0,
                                         stop=stop and k == K - 1 and m == 2, skip_group_check=True)
                return last

            def x_tile(b):
                return lambda k: (xs[:, k, b, 0, :], xs[:, k, b, 1, :])

            def x_half(h):
                return lambda k: (xs[:, k, 4 * h:4 * h + 4, 0, :], xs[:, k, 4 * h:4 * h + 4, 1, :])

            def ctx_tile(b):
                return lambda k: (ch[:, k, b * P:(b + 1) * P], cl[:, k, b * P:(b + 1) * P])

            def ctx_cols(at_, size):
                return lambda k: (ch[:, k, at_:at_ + size], cl[:, k, at_:at_ + size])

            def weight(n, at_=0, size=D):
                def of(k):
                    a = (n * K + k) * D + at_
                    return sw_h[:, a:a + size], sw_l[:, a:a + size]
                return of

            def turn(q, bank):
                pe.wait_ge(xn_ready, q + 1)
                for k in range(K):
                    for t in range(2):
                        at_ = k * D + t * P
                        last = pe.transpose(ps[:, bank, at_:at_ + P], xn[:, (2 * q + t) % 4, k * P:(k + 1) * P], ident[:, :])
                last.then_inc(xt_ps, 1)

            def norm(block):
                for p in range(PAIRS):
                    turn(norms_before(block) + p, 4 + p)

            def keys0():
                for j in range(2):
                    for h in range(2):
                        pe.wait_ge(split_lo, 3)
                        product(ps[:, 2 * j + h, :], weight(0, j * P, P), ctx_cols(h * HALF, HALF)).then_inc(pre_ps, 1)

            def values0():
                pe.wait_ge(small_lo, 1)
                for p in range(PAIRS):
                    for t in range(2):
                        last = product(ps[:, 4 + p, t * D:(t + 1) * D], ctx_tile(2 * p + t), weight(1))
                    last.then_inc(pre_ps, 1)
                pe.wait_ge(pre_hi, 5)
                for h in range(2):
                    wt = sraw[:, WHT_AT + h * P:WHT_AT + (h + 1) * P]
                    last = pe.matmul(ps[:, 4, h * P:(h + 1) * P], wt, wt, start=True, stop=True)
                last.then_inc(pre_ps, 1)

            def rows(z, src, n):
                if z > B:
                    pe.wait_ge(qk_sq, z)
                product(ps[:, 6, 0:D], src, weight(n)).then_inc(qk_ps, 1)

            def stacks(z, bank):
                pe.wait_ge(st_lo, z + 1)
                for g in range(GROUPS1):
                    part = stk[:, z % 2, 4 * g:4 * g + 4, :, :].rearrange("p j r d -> p (j r d)")
                    last = pe.transpose(ps16[:, bank, g * P:(g + 1) * P], part, ident16[:, :])
                last.then_inc(qt_ps, 1)

            def keys_values(b):
                if b % 4 >= 2:
                    pe.wait_ge(qk_sq, b - 1)
                    pe.wait_ge(r1_ready, b - 1)
                elif b >= 4:
                    pe.wait_ge(qt_ready, b - 1)
                product(ps[:, 2 + b % 2, 0:D], ctx_tile(b), weight(2)).then_inc(qk_ps, 1)
                product(ps[:, 2 + b % 2, D:2 * D], ctx_tile(b), weight(3)).then_inc(v_ps, 1)

            def key_stacks(z):
                if z % 4 < 2:
                    pe.wait_ge(qk_sq, z + 3)
                    pe.wait_ge(r1_ready, z + 3)
                else:
                    pe.wait_ge(qt_ready, z - 1)
                stacks(z, key_bank(z))

            def prepare_last():
                for h in range(2):
                    for s in range(2):
                        parts = ((g_h, ch), (g_h, cl), (g_l, ch))
                        for m, (a, b_) in enumerate(parts):
                            last = pe.matmul(ps[:, 2 * h + s, :], a[:, h, :], b_[:, h, s * HALF:(s + 1) * HALF],
                                             start=m == 0, stop=m == 2)
                        last.then_inc(pre_ps, 1)
                for b in range(B):
                    if b < 4:
                        pe.wait_ge(pre_lo, 6 + b)
                    else:
                        pe.wait_ge(pre_hi, 14 + b - 4)
                    for h in range(2):
                        t = slice(b * P, (b + 1) * P)
                        wh = slice(WH_AT, WH_AT + D)
                        for m, (a, w) in enumerate(((ch, sw_h), (ch, sw_l), (cl, sw_h))):
                            last = pe.matmul(ps[:, b % 4, h * D:(h + 1) * D], a[:, h, t], w[:, wh],
                                             start=m == 0, stop=m == 2)
                    last.then_inc(pre_ps, 1)

            def attend0():
                norm(0)
                keys0()
                pe.wait_ge(pre_lo, 4)

                def scores(p):
                    for b in (2 * p, 2 * p + 1):
                        pe.wait_ge(xl_ready, p + 1)
                        if b >= 2:
                            pe.wait_ge(sc_read, b - 1)
                        product(ps[:, b % 2, 0:D], x_tile(b),
                                lambda k: (mk_h[:, k, p * D:(p + 1) * D], mk_l[:, k, p * D:(p + 1) * D])).then_inc(sc_ps, 1)

                scores(0)
                pe.wait_ge(xl_ready, PAIRS)
                values0()
                pe.wait_ge(small_lo, 2)
                keys_values(0)
                keys_values(1)
                pe.wait_ge(const_ready, 3)
                for p in range(PAIRS):
                    if p + 1 < PAIRS:
                        scores(p + 1)
                    if p:
                        keys_values(2 * p)
                        keys_values(2 * p + 1)
                    pe.wait_ge(pre_hi, 8)
                    if p == PAIRS - 1 and blocks > 1:
                        pe.wait_ge(xl_ready, norms_before(1) + 1)
                    for b in (2 * p, 2 * p + 1):
                        pe.wait_ge(ep_ready, b + 1)
                        pe.transpose(ps[:, 4 + (p + 1) % PAIRS, (b % 2) * P:(b % 2 + 1) * P], ep[:, b % 2, :],
                                     ident[:, :]).then_inc(ept_ps, 1)
                    if p == 0:
                        pe.wait_ge(pre_lo, 5)
                    for b in (2 * p, 2 * p + 1):
                        pe.wait_ge(ept_ready, b + 1)
                        pe.matmul(ps[:, 4 + p, (b % 2) * D:(b % 2 + 1) * D], ept[:, b % 2, :], vw0[:, b, :],
                                  start=True, stop=True).then_inc(av_ps, 1)
                    if p and blocks > 1:
                        turn(norms_before(1) + p - 1, 4 + p - 1)
                    if p == PAIRS - 1 and blocks > 1:
                        turn(norms_before(1) + p, 4 + p)
                    if p == 1:
                        for z in range(4):
                            key_stacks(z)

            def attend2():
                nb = norms_before(4)
                norm(4)
                for i in range(B + 2):
                    if i < B:
                        z = B + i
                        pe.wait_ge(xl_ready, nb + i // 2 + 1)
                        pe.wait_ge(sc_read, z - 1)
                        a = (i // 2) * D
                        product(ps[:, z % 2, 0:D], x_tile(i),
                                lambda k: (ch[:, k, a:a + D], cl[:, k, a:a + D])).then_inc(sc_ps, 1)
                    if 1 <= i <= B:
                        z = B + i - 1
                        pe.wait_ge(ex_ready, z + 1)
                        pe.wait_ge(ept_ready, z - 1)
                        pe.transpose(ps[:, 2 + z % 2, 0:P], ex[:, z % 2, :], ident[:, :]).then_inc(ept_ps, 1)
                    if i >= 2:
                        b, z = i - 2, B + i - 2
                        pe.wait_ge(ept_ready, z + 1)
                        pe.wait_ge(ld_n, 16)
                        if b == 0:
                            pe.wait_ge(xl_ready, nb + PAIRS)
                        pe.matmul(ps[:, 4 + b // 2, (b % 2) * D:(b % 2 + 1) * D], ept[:, z % 2, :], cn[:, b, :],
                                  start=True, stop=True).then_inc(av_ps, 1)

            def up(n, c, i, h):
                f, g = FFN[n], FFN[n].base + c
                pe.wait_ge(wup_lo, after(i, g + 1, 2))
                if g:
                    pe.wait_ge(s_ready, after(i, 2 * (g - 1) + h + 1, 4))
                    pe.wait_ge(t_ready, after(i, 2 * (g - 1) + h + 1, 4))
                for m in range(2 if f.up else 1):
                    def w(k):
                        a = m * D + k * P
                        return wup_h[:, g % 2, a:a + P], wup_l[:, g % 2, a:a + P]
                    last = product(ps[:, 2 * h + m, :], w, x_half(h))
                last.then_inc(up_ps, 1)

            def down(n, c, i):
                f, g = FFN[n], FFN[n].base + c
                pe.wait_ge(wdn_lo, after(i, g + 1, 2))
                if c == 0:
                    pe.wait_ge(gt_ready, 2 * n + 2)
                for b in range(B):
                    if b % 4 == 0:
                        pe.wait_ge(tl_ready, after(i, 2 * g + b // 4 + 1, 4))
                    dst = ps[:, 4 + b // 2, (b % 2) * D:(b % 2 + 1) * D]
                    t = slice(b * P, (b + 1) * P)
                    parts = ((th, wdn_h), (th, wdn_l), (tl, wdn_h))
                    for m, (a, w) in enumerate(parts):
                        last = pe.matmul(dst, a[:, g % 2, t], w[:, g % 2, :],
                                         start=c == 0 and i is None and b % 2 == 0 and m == 0,
                                         stop=c == f.chunks - 1 and m == 2, skip_group_check=True)
                    if c == f.chunks - 1 and b in (1, 3, 5):
                        last.then_inc(y_ps, 1)
                last.then_inc(dn_ps, 1)

            def experts(n):
                f, nb = FFN[n], norms_before(2 * n + 1)
                if n:
                    norm(2 * n + 1)

                def logits(h):
                    pe.wait_ge(xl_ready, nb + 2 * h + 2)
                    gate_w = lambda k: (sw_h[:, gate_cols(n, k)], sw_l[:, gate_cols(n, k)])
                    product(ps[0:f.gate_rows, 4 + 2 * h, :], gate_w, x_half(h)).then_inc(lt_ps, 1)

                def logit_rows(h):
                    pe.wait_ge(lt_ready, 2 * n + h + 1)
                    for t in range(4):
                        last = pe.transpose(ps[:, 5 + 2 * h, t * LP:t * LP + f.gate_rows],
                                            lgt[0:f.gate_rows, h, t * P:(t + 1) * P],
                                            ident[0:f.gate_rows, 0:f.gate_rows])
                    last.then_inc(lg_ps, 1)

                def gate_cols_(h):
                    pe.wait_ge(gw_ready, 2 * n + h + 1)
                    for t in range(4):
                        last = pe.transpose(ps[0:f.gate_rows, 4 + 2 * h, t * P:(t + 1) * P],
                                            lm[:, h, t, 0:f.gate_rows], ident[:, :])
                    last.then_inc(gt_ps, 1)

                logits(0)
                up(n, 0, None, 0)
                logits(1)
                logit_rows(0)
                up(n, 0, None, 1)
                logit_rows(1)
                if n == 0:
                    for z in (4, 5, 6):
                        key_stacks(z)
                gate_cols_(0)
                if n == 0:
                    key_stacks(7)
                gate_cols_(1)

                def chunk(n, c, i):
                    if c:
                        up(n, c, i, 0)
                        up(n, c, i, 1)
                        down(n, c - 1, i)
                every_chunk(pe, n, chunk)
                if n == 0:
                    for b in range(B):
                        pe.matmul(ps[:, 4 + b // 2, (b % 2) * D:(b % 2 + 1) * D], gt[0:f.experts + 1, b * P:(b + 1) * P],
                                  b2[:, :], start=False, stop=False, skip_group_check=True)
                down(n, f.chunks - 1, None)

            def scores1(u):
                b, s, j = u // 8, (u // 4) % 2, u % 4
                if j == 0:
                    pe.wait_ge(qt_ready, B + b + 1)
                if u >= 4:
                    pe.wait_ge(e1_ready, u - 3)
                r = slice(32 * j, 32 * j + 32)
                for g in range(4):
                    last = pe.matmul(ps[:, j, g * P:(g + 1) * P], kst[r, b, 4 * s + g, :], qst[r, b % 4, 4 * s + g, :],
                                     start=True, stop=True)
                last.then_inc(s1_ps, 1)

            def mix1(u):
                b, s, j = u // 8, (u // 4) % 2, u % 4
                pe.wait_ge(el_ready, u + 1)
                if j == 0 and b:
                    pe.wait_ge(o1_read, 2 * b + s - 1)
                for g in range(4):
                    head = 4 * (4 * s + g) + j
                    at_ = (head - 16 * s) * VW
                    for m, e in enumerate((eh, el)):
                        last = pe.matmul(ps[:, 4 + s, at_:at_ + VW], e[:, j, g * P:(g + 1) * P], vp[:, b, head, :],
                                         start=j == 0 and g == 0 and m == 0, stop=True, skip_group_check=True)
                last.then_inc(o1_ps, 1)

            def attend1():
                norm(2)
                prepare_last()
                pe.wait_ge(xl_ready, norms_before(2) + PAIRS)

                def raw(b):
                    rows(B + b, x_tile(b), 4)

                def stack(b):
                    if b:
                        pe.wait_ge(qt_ready, B + b)
                    stacks(B + b, 7)

                def tile(b):
                    for u in range(8 * b, 8 * b + 8):
                        if u + 4 < 8 * B:
                            scores1(u + 4)
                        mix1(u)
                for b in range(4):
                    raw(b)
                for b in range(4):
                    stack(b)
                pe.wait_ge(pre_hi, 21)
                for u in range(4):
                    scores1(u)
                for what, b in SCHEDULE1:
                    {"raw": raw, "tile": tile, "scale": lambda b: None, "stack": stack}[what](b)

            def retain():
                nb = norms_before(6)
                norm(6)
                for b in range(B):
                    pe.wait_ge(xl_ready, nb + b // 2 + 1)
                    for h in range(2):
                        for m, w in enumerate((mk_h, mk_l)):
                            last = pe.matmul(ps[:, h, 0:2 * P], w[:, h, b * P:(b + 1) * P],
                                             xs[:, h, b, :, :].rearrange("p r t -> p (r t)"),
                                             start=b == 0 and m == 0, stop=b == B - 1 and m == 1, skip_group_check=True)
                    if b == B - 1:
                        last.then_inc(a_ps, 1)
                for b in range(B):
                    if b >= 2:
                        pe.wait_ge(wr_ready, b - 1)
                    product(ps[:, 2 + b % 2, 0:D], x_tile(b), weight(5)).then_inc(wg_ps, 1)
                for s in range(2):
                    for h in range(2):
                        pe.wait_ge(a_ready, h + 1)
                        pe.matmul(ps[:, 4 + 2 * s + h, :], at[:, h, :],
                                  vw[:, h, 4 * s:4 * s + 4, :].rearrange("p b e -> p (b e)"),
                                  start=True, stop=True).then_inc(o_ps, 1)
                for p in range(PAIRS):
                    q = nb + PAIRS + p
                    if p >= 2:
                        pe.wait_ge(xl_ready, q - 1)
                    turn(q, p % 2)
                    pe.wait_ge(xl_ready, q + 1)
                    pe.wait_ge(ya_ready, 4 * (p // 2) + 4)
                    for t in range(2):
                        last = product(ps[:, 4 + p, t * D:(t + 1) * D], x_tile(2 * p + t), weight(6))
                    last.then_inc(y_ps, 1)

            pe.wait_ge(ld_i, 16)
            attend0()
            if blocks > 1:
                experts(0)
            if blocks > 2:
                attend1()
            if blocks > 3:
                experts(1)
            if blocks > 4:
                attend2()
            if blocks > 5:
                experts(2)
            if blocks > 6:
                retain()
            if blocks > 7:
                experts(3)

        @block_.scalar
        def _(act):
            def high(q, p, bank):
                act.wait_ge(xt_ps, q + 1)
                act.activation(xs[:, :, 2 * p:2 * p + 2, 0, :],
                               ps[:, bank, :].rearrange("p (k t c) -> p k t c", k=K, t=2), ACT.Copy).then_inc(xh_ready, 1)

            def norm(block):
                for p in range(PAIRS):
                    high(norms_before(block) + p, p, 4 + p)

            def split_up(n, c, i):
                f, g = FFN[n], FFN[n].base + c
                act.wait_ge(w_loaded[g % 2], after(i, 16 * (g // 2 + 1), 16))
                if g >= 2:
                    act.wait_ge(up_ps, after(i, 2 * (g - 1), 4))
                act.activation(wup_h[:, g % 2, 0:f.width - D], wraw[:, g % 2, 0:f.width - D], ACT.Copy).then_inc(wup_hi, 1)

            def split_down(n, c, i):
                f, g = FFN[n], FFN[n].base + c
                act.wait_ge(w_loaded[g % 2], after(i, 16 * (g // 2 + 1), 16))
                if g >= 2:
                    act.wait_ge(dn_ps, after(i, g - 1, 2))
                act.activation(wdn_h[:, g % 2, :], wraw[:, g % 2, f.width - D:f.width], ACT.Copy).then_inc(wdn_hi, 1)

            def gate_rows_load(n, c, i):
                f = FFN[n]
                if c < f.plain or c >= f.chunks:
                    return
                slot, j = gated(n, c) % 2, gated(n, c)
                if j >= 2:
                    g0 = f.base + c - 2 if c - 2 >= f.plain else FFN[n - 1].base + FFN[n - 1].chunks - (2 - (c - f.plain))
                    act.wait_ge(t_ready, after(i, 2 * g0 + 2, 4))
                for r, size, e in segments(n, c):
                    if i is None:
                        src = gates[n][e:e + 1, :]
                    else:
                        src = gates[n][bass.ds((4 if n == 2 else 2) * i + e, 1), :]
                    act.dma_start(gb[r:r + size, slot, :], src.broadcast_to([size, T])).then_inc(g_loaded[slot], 16)

            def activate(n, c, i):
                f, g = FFN[n], FFN[n].base + c
                for h in range(2):
                    act.wait_ge(up_ps, after(i, 2 * g + h + 1, 4))
                    if g:
                        act.wait_ge(t_ready, after(i, 2 * (g - 1) + h + 1, 4))
                    bias = 0.0
                    if f.bias:
                        bias = wraw[:, g % 2, f.width:f.width + 1]
                    act.activation(s_act[:, h, :], ps[:, 2 * h, :], f.act, bias=bias).then_inc(s_ready, 1)

            def chunk(n, c, i):
                f, g = FFN[n], FFN[n].base + c
                nxt = (n, c + 1) if c + 1 < f.chunks else (n + 1, 0)
                if c:
                    if g + 1 < CHUNKS:
                        split_up(*nxt, i)
                    activate(n, c, i)
                    if c + 1 == f.plain:
                        act.wait_ge(g_stored, 16 * (n + 1))
                    gate_rows_load(n, c + 1, i)
                if g + 1 < CHUNKS:
                    split_down(*nxt, i)
                for h in range(2):
                    act.wait_ge(t_ready, after(i, 2 * g + h + 1, 4))
                    act.activation(th[:, g % 2, h * HALF:(h + 1) * HALF], tt[:, h, :], ACT.Copy).then_inc(th_ready, 1)

            def experts(n):
                f = FFN[n]
                if n:
                    norm(2 * n + 1)
                for h in range(2):
                    act.wait_ge(lt_ps, 2 * n + h + 1)
                    act.activation(lgt[0:f.gate_rows, h, :], ps[0:f.gate_rows, 4 + 2 * h, :], ACT.Copy).then_inc(lt_ready, 1)
                if n == 0:
                    stack_high(4)
                    stack_high(5)
                split_up(n, 1, None)
                for h in range(2):
                    act.wait_ge(ld_ready, 2 * n + h + 1)
                    if f.gate_rows > f.experts:
                        act.activation(le[:, h, :, f.experts:f.gate_rows], lg[:, h, :, f.experts:f.gate_rows], ACT.Exp, scale=-1.0)
                    act.activation(le[:, h, :, 0:f.experts], le[:, h, :, 0:f.experts], ACT.Exp).then_inc(le_ready, 1)
                    if n == 0:
                        key_out(4 + h)
                        stack_high(6 + h)
                if n == 0:
                    key_out(6)
                activate(n, 0, None)
                for h in range(2):
                    act.wait_ge(gt_ps, 2 * n + h + 1)
                    act.activation(gt[0:f.gate_rows, h * HALF:(h + 1) * HALF], ps[0:f.gate_rows, 4 + 2 * h, :],
                                   ACT.Copy).then_inc(gt_ready, 1)
                if n == 0:
                    key_out(7)
                act.wait_ge(gt_ready, 2 * n + 2)
                act.dma_start(gates[n], gt[0:f.gate_rows, :]).then_inc(g_stored, 16)
                if f.plain == 0:
                    act.wait_ge(g_stored, 16 * (n + 1))
                    for c in (0, 1):
                        gate_rows_load(n, c, None)
                every_chunk(act, n, chunk)

            def key_out(z):
                stack_out(z, ps16[:, key_bank(z), :], kst[:, z, :, :])

            def exponentials0(p):
                for b in (2 * p, 2 * p + 1):
                    act.wait_ge(negm_ready, b + 1)
                    act.activation(ex[:, b % 2, :], sc[:, b % 2, :], ACT.Exp, bias=negm[:, b % 2:b % 2 + 1]).then_inc(ex_ready, 1)

            def attend0():
                heads = lambda a: a.rearrange("p (n d) -> p n d", d=HD1)
                for p in range(PAIRS):
                    for b in (2 * p, 2 * p + 1):
                        act.wait_ge(v_ps, b + 1)
                        raw(b, ps[:, 2 + b % 2, 0:D])
                        act.activation(vp[:, b, :, 0:HD1], heads(ps[:, 2 + b % 2, D:2 * D]), ACT.Copy).then_inc(v1_ready, 1)
                    act.wait_ge(ept_ps, 2 * p + 2)
                    if p:
                        act.wait_ge(av_ps, 2 * p)
                    act.activation(ept[:, :, :], ps[:, 4 + (p + 1) % PAIRS, 0:2 * P].rearrange("p (t c) -> p t c", t=2),
                                   ACT.Copy).then_inc(ept_ready, 2)
                    for b in (2 * p, 2 * p + 1):
                        act.wait_ge(r1_ready, b + 1)
                        act.activation(vp[:, b, :, HD1:2 * HD1], heads(vres[:, b % 2, 0, :]), ACT.Copy).then_inc(v2_ready, 1)
                    if p and blocks > 1:
                        high(norms_before(1) + p - 1, p - 1, 4 + p - 1)
                    if p + 1 < PAIRS:
                        exponentials0(p + 1)
                    elif blocks > 1:
                        high(norms_before(1) + p, p, 4 + p)
                    if p == 1:
                        stack_high(0)
                        for z in range(1, 4):
                            stack_high(z)
                            key_out(z - 1)
                        key_out(3)

            def attend2():
                norm(4)
                for i in range(B + 1):
                    if i < B:
                        z = B + i
                        act.wait_ge(negm_ready, z + 1)
                        act.wait_ge(ept_ps, z - 1)
                        act.activation(ex[:, z % 2, :], sc[:, z % 2, :], ACT.Exp, bias=negm[:, z % 2:z % 2 + 1],
                                       accum_out=esum[:, i:i + 1]).then_inc(ex_ready, 1)
                    if i >= 1:
                        z = B + i - 1
                        act.wait_ge(ept_ps, z + 1)
                        act.wait_ge(av_ps, z - 1)
                        act.activation(ept[:, z % 2, :], ps[:, 2 + z % 2, 0:P], ACT.Copy).then_inc(ept_ready, 1)

            def raw(z, src):
                act.wait_ge(qk_ps, z + 1)
                if z >= 4:
                    act.wait_ge(st_lo, z - 3)
                act.activation(qf[:, z % 4, :], src, ACT.Copy)
                if z >= 2:
                    act.wait_ge(ss_read, z - 1)
                act.activation(sq[:, z % 2, :], src, ACT.Square).then_inc(qk_sq, 1)

            def stack_high(z):
                act.wait_ge(qn_ready, z + 1)
                if z >= 2:
                    act.wait_ge(qt_ps, z - 1)
                for r in ((0, 2) if z < B else (0, 1)):
                    last = act.activation(stk[:, z % 2, :, r, :], qf[:, z % 4, :].rearrange("p (n d) -> p n d", d=HD1), ACT.Copy)
                last.then_inc(st_hi, 1)

            def stack_out(z, src, dst):
                act.wait_ge(qt_ps, z + 1)
                if z >= B + 4:
                    act.wait_ge(s1_ps, 8 * (z - B - 4) + 8)
                act.activation(dst.rearrange("p g t -> p (g t)"), src, ACT.Copy).then_inc(qt_ready, 1)

            def attend1():
                norm(2)
                for m in range(4):
                    act.wait_ge(pre_ps, 10 + m)
                    act.activation(mk_h[:, m // 2, (m % 2) * HALF:(m % 2 + 1) * HALF], ps[:, m, :], ACT.Copy).then_inc(pre_hi, 1)
                for b in range(B):
                    act.wait_ge(pre_ps, 14 + b)
                    for h in range(2):
                        last = act.activation(vw[:, h, b, :], ps[:, b % 4, h * D + h * P:h * D + (h + 1) * P], ACT.Copy)
                    last.then_inc(pre_hi, 1)

                def tile(b):
                    for u in range(8 * b, 8 * b + 8):
                        act.wait_ge(s1_ps, u + 1)
                        if u >= 4:
                            act.wait_ge(el_ready, u - 3)
                        act.activation(e1[:, u % 4, :], ps[:, u % 4, :], ACT.Exp, scale=HD1 ** -0.5).then_inc(e1_ready, 1)
                def stack(b):
                    stack_high(B + b)
                    stack_out(B + b, ps16[:, 7, :], qst[:, b % 4, :, :])
                for b in range(4):
                    raw(B + b, ps[:, 6, 0:D])
                for b in range(4):
                    stack(b)
                for what, b in SCHEDULE1:
                    {"raw": lambda b: raw(B + b, ps[:, 6, 0:D]), "tile": tile, "scale": lambda b: None,
                     "stack": stack}[what](b)

            def retain():
                nb = norms_before(6)
                norm(6)
                for b in range(B):
                    act.wait_ge(wg_ps, b + 1)
                    act.activation(wr[:, b, :], ps[:, 2 + b % 2, 0:D], ACT.Relu).then_inc(wr_ready, 1)
                for p in range(PAIRS):
                    high(nb + PAIRS + p, p, p % 2)

            def split_high(n):
                wait, dst, src = SPLITS(ld_c, ld_s, craw, sraw, ch, sw_h)[n]
                act.wait_ge(wait, 16)
                act.activation(dst, src, ACT.Copy).then_inc(split_hi, 1)

            norm(0)
            for n in range(3):
                split_high(n)
            act.wait_ge(ld_m, LD_M)
            act.activation(cwork[:, 0:1], cvec[:, 2:3], ACT.Exp, scale=-1.0)
            act.activation(cwork[:, 1:2], cvec[:, 3:4], ACT.Exp).then_inc(coef_exp, 1)
            split_high(3)
            for m in range(4):
                act.wait_ge(pre_ps, m + 1)
                act.activation(mk_h[:, m // 2, (m % 2) * HALF:(m % 2 + 1) * HALF], ps[:, m, :], ACT.Copy).then_inc(pre_hi, 1)
            exponentials0(0)
            split_high(4)
            for p in range(PAIRS):
                act.wait_ge(pre_ps, 5 + p)
                act.activation(vw0[:, 2 * p:2 * p + 2, :], ps[:, 4 + p, :].rearrange("p (t d) -> p t d", t=2), ACT.Copy).then_inc(pre_hi, 1)
            act.wait_ge(pre_ps, 9)
            act.activation(g_h[:, :, :], ps[:, 4, 0:2 * P].rearrange("p (h d) -> p h d", h=2), ACT.Copy).then_inc(pre_hi, 1)
            if blocks > 1:
                split_up(0, 0, None)
                split_down(0, 0, None)
            attend0()
            if blocks > 1:
                experts(0)
            if blocks > 2:
                attend1()
            if blocks > 3:
                act.wait_ge(o1_ps, 8 * B)
                act.dma_start(cn[:, :, :], ctx_n.rearrange("b p d -> p b d")).then_inc(ld_n, 16)
                experts(1)
            if blocks > 4:
                attend2()
            if blocks > 5:
                experts(2)
            if blocks > 6:
                retain()
            if blocks > 7:
                experts(3)

        @block_.vector
        def _(dve):
            steps = [0]

            def step(instruction):
                instruction.then_inc(dve_step, 1)
                steps[0] += 1
                return steps[0]

            def stats(block, p):
                r = PAIRS * block + p
                if block:
                    dve.wait_ge(x_added, r - PAIRS + 1)
                for t in range(2):
                    n = step(dve.bn_stats(stat[:, r % 2, t, :], x[:, 2 * p + t, :]))
                dve.wait_ge(dve_step, n)
                for t in range(2):
                    n = step(dve.bn_aggr(mv[:, r % 2, t, :], stat[:, r % 2, t, :]))
                dve.wait_ge(dve_step, n)
                dve.tensor_scalar(var_eps[:, r % 2, :], mv[:, r % 2, :, 1], LN_EPS, None, ALU.add).then_inc(mv_ready, 1)

            def normal(block, p):
                r, q = PAIRS * block + p, norms_before(block) + p
                dve.wait_ge(rstd_ready, r + 1)
                if q >= 2:
                    dve.wait_ge(xt_ps, q - 1)
                for t in range(2):
                    last = dve.tensor_scalar(xn[:, (2 * q + t) % 4, :], x[:, 2 * p + t, :], mv[:, r % 2, t, 0:1],
                                             rstd[:, r % 2, t:t + 1], ALU.subtract, ALU.mult)
                last.then_inc(xn_ready, 1)

            def low(q, p, bank):
                dve.wait_ge(xh_ready, q + 1)
                dve.tensor_tensor(xs[:, :, 2 * p:2 * p + 2, 1, :],
                                  ps[:, bank, :].rearrange("p (k t c) -> p k t c", k=K, t=2),
                                  xs[:, :, 2 * p:2 * p + 2, 0, :].bitcast(F32), ALU.subtract).then_inc(xl_ready, 1)

            def add_bank(block, p):
                if block in (1, 3, 5, 7) and p == PAIRS - 1:
                    f = FFN[block // 2]
                    dve.wait_ge(dn_ps, f.base + f.chunks)
                else:
                    dve.wait_ge(y_ps, {1: 0, 3: 3, 5: 6, 6: 9, 7: 13}[block] + p + 1)
                xp = x[:, 2 * p:2 * p + 2, :].rearrange("p t d -> p (t d)")
                dve.tensor_tensor(xp, ps[:, 4 + p, :], xp, ALU.add).then_inc(x_added, 1)

            def add_scaled(block, p):
                o = 0 if block == 0 else B
                dve.wait_ge(av_ps, o + 2 * p + 2)
                for t in range(2):
                    b = 2 * p + t
                    last = dve.scalar_tensor_tensor(x[:, b, :], ps[:, 4 + p, t * D:(t + 1) * D], rsum[:, b:b + 1],
                                                    x[:, b, :], ALU.mult, ALU.add)
                last.then_inc(x_added, 1)

            def boundary(block, add, done=0):
                nb = norms_before(block + 1)
                if block + 1 >= blocks:
                    for p in range(done, PAIRS):
                        add(block, p)
                    return
                for i in range(PAIRS + 2):
                    if i < PAIRS:
                        if i >= done:
                            add(block, i)
                        stats(block + 1, i)
                    if 1 <= i <= PAIRS:
                        normal(block + 1, i - 1)
                    if i >= 2:
                        low(nb + i - 2, i - 2, 4 + i - 2)

            def rsqrt(v, y, a, b_, minus_half):
                n = step(dve.tensor_scalar(a.bitcast(I32), v.bitcast(I32), 1, None, ALU.logical_shift_right))
                step(dve.tensor_scalar(minus_half, v, -0.5, None, ALU.mult))
                dve.wait_ge(dve_step, n)
                n = step(dve.tensor_scalar(y.bitcast(I32), a.bitcast(I32), -1.0, float(0x5F3759DF), ALU.mult, ALU.add))
                for _ in range(3):
                    dve.wait_ge(dve_step, n)
                    n = step(dve.tensor_tensor(a, y, y, ALU.mult))
                    dve.wait_ge(dve_step, n)
                    n = step(dve.tensor_tensor(b_, a, minus_half, ALU.mult))
                    dve.wait_ge(dve_step, n)
                    n = step(dve.scalar_tensor_tensor(y, b_, 1.5, y, ALU.add, ALU.mult))
                dve.wait_ge(dve_step, n)

            def front0(p):
                pair, n = (0, 1), [0, 0]
                s, w, m = sc, work, top
                for t in pair:
                    b = 2 * p + t
                    dve.wait_ge(sc_ps, b + 1)
                    if b >= 2:
                        dve.wait_ge(ex_ready, b - 1)
                    dve.tensor_scalar(s[:, t, :], ps[:, t, t * P:(t + 1) * P], cwork[:, 7:8], None, ALU.mult).then_inc(sc_read, 1)
                for t in pair:
                    dve.wait_ge(sc_read, 2 * p + t + 1)
                    n[t] = step(dve.max(m[:, t, 0:8], s[:, t, :]))
                for t in pair:
                    dve.wait_ge(dve_step, n[t])
                    dve.tensor_scalar(negm[:, t:t + 1], m[:, t, 0:1], -1.0, None, ALU.mult).then_inc(negm_ready, 1)
                for r in range(1, (CLIP + 7) // 8):
                    for t in pair:
                        dve.wait_ge(dve_step, n[t])
                        n[t] = step(dve.match_replace(w[:, t, :], m[:, t, 8 * r - 8:8 * r], (s if r == 1 else w)[:, t, :], NEG))
                    for t in pair:
                        dve.wait_ge(dve_step, n[t])
                        n[t] = step(dve.max(m[:, t, 8 * r:8 * r + 8], w[:, t, :]))
                for t in pair:
                    b = 2 * p + t
                    dve.wait_ge(dve_step, n[t])
                    dve.wait_ge(ex_ready, b + 1)
                    if b >= 2:
                        dve.wait_ge(ept_ps, b - 1)
                    n[t] = step(dve.scalar_tensor_tensor(ep[:, t, :], s[:, t, :], m[:, t, CLIP - 1:CLIP], ex[:, t, :],
                                                         ALU.is_ge, ALU.mult))
                for t in pair:
                    dve.wait_ge(dve_step, n[t])
                    n[t] = step(dve.tensor_reduce(esum[:, 2 * p + t:2 * p + t + 1], ep[:, t, :], AX.X, ALU.add))
                for t in pair:
                    b = 2 * p + t
                    dve.wait_ge(dve_step, n[t])
                    dve.reciprocal(rsum[:, b:b + 1], esum[:, b:b + 1]).then_inc(ep_ready, 1)

            def attend0():
                nb = norms_before(1)
                heads = lambda a: a.rearrange("p (n d) -> p n d", d=HD1)
                for p in range(PAIRS):
                    front0(p)
                    if p == 0:
                        dve.wait_ge(pre_hi, 9)
                        dve.tensor_tensor(g_l[:, :, :], ps[:, 4, 0:2 * P].rearrange("p (h d) -> p h d", h=2),
                                          g_h[:, :, :].bitcast(F32), ALU.subtract).then_inc(pre_lo, 1)
                        if blocks > 1:
                            low_up(0, 0, None)
                            low_down(0, 0, None)
                    if p:
                        add_scaled(0, p - 1)
                        if blocks > 1:
                            stats(1, p - 1)
                    for b in (2 * p, 2 * p + 1):
                        squares(b)
                        dve.wait_ge(v1_ready, b + 1)
                        if b >= 2:
                            dve.wait_ge(v3_ready, b - 1)
                        dve.tensor_tensor(heads(vres[:, b % 2, 0, :]), heads(ps[:, 2 + b % 2, D:2 * D]), vp[:, b, :, 0:HD1],
                                          ALU.subtract).then_inc(r1_ready, 1)
                    if p == 1:
                        scales(3)
                        for z in range(4):
                            scaled(z)
                    if p and blocks > 1:
                        normal(1, p - 1)
                    if p >= 2 and blocks > 1:
                        low(nb + p - 2, p - 2, 4 + p - 2)
                add_scaled(0, PAIRS - 1)
                if blocks > 1:
                    stats(1, PAIRS - 1)
                    low(nb + PAIRS - 2, PAIRS - 2, 4 + PAIRS - 2)
                    normal(1, PAIRS - 1)
                    low(nb + PAIRS - 1, PAIRS - 1, 4 + PAIRS - 1)
                    scales(7)
                    for z in range(4, 8):
                        scaled(z)

            def front2(b):
                z = B + b
                dve.wait_ge(sc_ps, z + 1)
                dve.wait_ge(ex_ready, z - 1)
                s, w = sc[:, z % 2, :], work[:, z % 2, :]
                dve.scalar_tensor_tensor(w, ps[:, z % 2, (b % 2) * P:(b % 2 + 1) * P], D ** -0.5,
                                         maskf[:, b, :], ALU.mult, ALU.mult).then_inc(sc_read, 1)
                dve.wait_ge(sc_read, z + 1)
                n = step(dve.tensor_tensor(s, w, maskb[:, b, :], ALU.add))
                dve.wait_ge(dve_step, n)
                dve.tensor_reduce(negm[:, z % 2:z % 2 + 1], s, AX.X, ALU.max, negate=True).then_inc(negm_ready, 1)

            def scale2(p):
                dve.wait_ge(ex_ready, B + 2 * p + 2)
                two = slice(2 * p, 2 * p + 2)
                n = step(dve.reciprocal(rsum[:, two], esum[:, two]))
                dve.wait_ge(dve_step, n)
                n = step(dve.tensor_tensor(rsum[:, two], rsum[:, two], valid[:, two], ALU.mult))
                dve.wait_ge(dve_step, n)

            def low_up(n, c, i):
                f, g = FFN[n], FFN[n].base + c
                dve.wait_ge(wup_hi, after(i, g + 1, 2))
                u = f.width - D
                dve.tensor_tensor(wup_l[:, g % 2, 0:u], wraw[:, g % 2, 0:u], wup_h[:, g % 2, 0:u].bitcast(F32),
                                  ALU.subtract).then_inc(wup_lo, 1)

            def low_down(n, c, i):
                f, g = FFN[n], FFN[n].base + c
                dve.wait_ge(wdn_hi, after(i, g + 1, 2))
                dve.tensor_tensor(wdn_l[:, g % 2, :], wraw[:, g % 2, f.width - D:f.width], wdn_h[:, g % 2, :].bitcast(F32),
                                  ALU.subtract).then_inc(wdn_lo, 1)

            def chunk(n, c, i):
                f, g = FFN[n], FFN[n].base + c
                nxt = (n, c + 1) if c + 1 < f.chunks else (n + 1, 0)
                if c and g + 1 < CHUNKS:
                    low_up(*nxt, i)
                slot = gated(n, c) % 2
                if not f.up and c >= f.plain:
                    dve.wait_ge(g_loaded[slot], after(i, 16 * g_loads(n, c), 16 * len(segments(n, f.peeled))))
                for h in range(2):
                    if g:
                        dve.wait_ge(tl_ready, after(i, 2 * (g - 1) + h + 1, 4))
                    if not f.up or c < f.plain:
                        dve.wait_ge(s_ready, after(i, 2 * g + h + 1, 4))
                    else:
                        before = sum(2 * (FFN[m].chunks - FFN[m].plain) for m in range(1, n))
                        dve.wait_ge(sg_ready, after(i, before + 2 * (c - f.plain) + h + 1, 4))
                    if not f.up and c < f.plain:
                        dve.tensor_copy(tt[:, h, :], s_act[:, h, :]).then_inc(t_ready, 1)
                    elif not f.up:
                        dve.tensor_tensor(tt[:, h, :], s_act[:, h, :], gb[:, slot, h * HALF:(h + 1) * HALF],
                                          ALU.mult).then_inc(t_ready, 1)
                    else:
                        a = s_act if c < f.plain else sg
                        dve.tensor_tensor(tt[:, h, :], a[:, h, :], ps[:, 2 * h + 1, :], ALU.mult).then_inc(t_ready, 1)
                if g + 1 < CHUNKS:
                    low_down(*nxt, i)
                for h in range(2):
                    dve.wait_ge(th_ready, after(i, 2 * g + h + 1, 4))
                    half = slice(h * HALF, (h + 1) * HALF)
                    dve.tensor_tensor(tl[:, g % 2, half], tt[:, h, :], th[:, g % 2, half].bitcast(F32),
                                      ALU.subtract).then_inc(tl_ready, 1)

            def route_max(n):
                f = FFN[n]
                e, rows_, k = f.experts, f.gate_rows, [0, 0]
                for h in range(2):
                    dve.wait_ge(lg_ps, 2 * n + h + 1)
                    src = ps[:, 5 + 2 * h, 0:4 * LP].rearrange("p (t e) -> p t e", e=LP)[:, :, 0:rows_]
                    k[h] = step(dve.tensor_copy(lg[:, h, :, 0:rows_], src))
                    dve.wait_ge(dve_step, k[h])
                    for t in range(4):
                        k[h] = step(dve.max(m8[:, h, t, :], lg[:, h, t, 0:e]))
                    dve.wait_ge(dve_step, k[h])
                    dve.tensor_tensor(le[:, h, :, 0:e], lg[:, h, :, 0:e], m8[:, h, :, 0:1].broadcast_to([P, 4, e]),
                                      ALU.subtract).then_inc(ld_ready, 1)
                    step(dve.tensor_tensor(lm[:, h, :, 0:e], lg[:, h, :, 0:e],
                                           m8[:, h, :, f.top - 1:f.top].broadcast_to([P, 4, e]), ALU.is_ge))

            def route_weights(n):
                f = FFN[n]
                e, rows_, k, both = f.experts, f.gate_rows, [0, 0], (0, 1)
                M, E, S = lm, le, gsum
                start = steps[0]
                for h in both:
                    dve.wait_ge(dve_step, start)
                    dve.wait_ge(le_ready, 2 * n + h + 1)
                    k[h] = step(dve.tensor_tensor(M[:, h, :, 0:e], M[:, h, :, 0:e], E[:, h, :, 0:e], ALU.mult))
                    if rows_ > e:
                        step(dve.tensor_scalar(S[:, h, 8:12], E[:, h, :, e], 1.0, None, ALU.add))
                for h in both:
                    dve.wait_ge(dve_step, k[h])
                    k[h] = step(dve.tensor_reduce(S[:, h, 0:4], M[:, h, :, 0:e], AX.X, ALU.add))
                for h in both:
                    dve.wait_ge(dve_step, k[h])
                    k[h] = step(dve.reciprocal(S[:, h, 4:8], S[:, h, 0:4]))
                    if rows_ > e:
                        k[h] = step(dve.reciprocal(M[:, h, :, e], S[:, h, 8:12]))
                for h in both:
                    dve.wait_ge(dve_step, k[h])
                    dve.tensor_tensor(M[:, h, :, 0:e], M[:, h, :, 0:e], S[:, h, 4:8].unsqueeze(2).broadcast_to([P, 4, e]),
                                      ALU.mult).then_inc(gw_ready, 1)

            def experts(n):
                if n == 0:
                    k = step(dve.memset(gt[0:FFN[0].experts + 1, :], 1.0))
                route_max(n)
                low_up(n, 1, None)
                route_weights(n)
                every_chunk(dve, n, chunk)
                boundary(2 * n + 1, add_bank)

            def squares(z):
                dve.wait_ge(qk_sq, z + 1)
                dve.tensor_reduce(ss[:, z % 4, :], sq[:, z % 2, :].rearrange("p (n d) -> p n d", d=HD1),
                                  AX.X, ALU.add).then_inc(ss_read, 1)

            def scales(z):
                dve.wait_ge(ss_read, z + 1)
                flat = lambda a: a[:, :, :].rearrange("p t n -> p (t n)")
                n = step(dve.tensor_scalar(flat(ss), flat(ss), 1.0 / HD1, RMS_EPS, ALU.mult, ALU.add))
                dve.wait_ge(dve_step, n)
                rsqrt(flat(ss), flat(nw_y), flat(nw_a), flat(nw_b), flat(nw_h))

            def scaled(z):
                heads = lambda a: a.rearrange("p (n d) -> p n d", d=HD1)
                dve.tensor_tensor(heads(qf[:, z % 4, :]), heads(qf[:, z % 4, :]),
                                  nw_y[:, z % 4, :].unsqueeze(2).broadcast_to([P, HEADS1, HD1]), ALU.mult).then_inc(qn_ready, 1)

            def stack(z):
                scaled(z)
                dve.wait_ge(st_hi, z + 1)
                for r in (2, 3):
                    last = dve.tensor_tensor(stk[:, z % 2, :, r, :], qf[:, z % 4, :].rearrange("p (n d) -> p n d", d=HD1),
                                             stk[:, z % 2, :, 0, :], ALU.subtract)
                last.then_inc(st_lo, 1)

            def mixed(w):
                b, s = w // 2, w % 2
                dve.wait_ge(o1_ps, 4 * w + 4)
                src = ps[:, 4 + s, 0:16 * VW].rearrange("p (n c) -> p n c", c=VW)
                parts = src[:, :, 0:3 * HD1].rearrange("p n (r d) -> p n d r", d=HD1)
                step(dve.tensor_reduce(o3[:, s, :, :], parts, AX.X, ALU.add))
                dve.reciprocal(r3[:, s, :], src[:, :, 3 * HD1]).then_inc(o1_read, 1)
                dve.wait_ge(o1_read, w + 1)
                n = step(dve.tensor_tensor(oy[:, s, :, :], o3[:, s, :, :], r3[:, s, :].unsqueeze(2).broadcast_to([P, 16, HD1]), ALU.mult))
                dve.wait_ge(dve_step, n)
                dst = x[:, b, s * P:(s + 1) * P]
                last = dve.tensor_tensor(dst, dst, oy[:, s, :, :].rearrange("p n d -> p (n d)"), ALU.add)
                if w % 4 == 3:
                    last.then_inc(x_added, 1)

            def attend1():
                nb = norms_before(2)
                for m in range(4):
                    dve.wait_ge(pre_hi, 10 + m)
                    half = slice((m % 2) * HALF, (m % 2 + 1) * HALF)
                    dve.tensor_tensor(mk_l[:, m // 2, half], ps[:, m, :], mk_h[:, m // 2, half].bitcast(F32),
                                      ALU.subtract).then_inc(pre_lo, 1)

                def tile(b):
                    for u in range(8 * b, 8 * b + 8):
                        dve.wait_ge(eh_ready, u + 1)
                        dve.tensor_tensor(el[:, u % 4, :], e1[:, u % 4, :], eh[:, u % 4, :], ALU.subtract).then_inc(el_ready, 1)
                        if u % 4 == 1 and u > 4:
                            mixed(u // 4 - 1)
                for b in range(4):
                    squares(B + b)
                scales(B + 3)
                for b in range(4):
                    stack(B + b)
                for what, b in SCHEDULE1:
                    {"raw": lambda b: squares(B + b), "tile": tile, "scale": lambda b: scales(B + b),
                     "stack": lambda b: stack(B + b)}[what](b)
                mixed(2 * B - 1)
                boundary(2, None, done=PAIRS)

            def retain():
                nb = norms_before(6)
                dve.wait_ge(a_ps, 1)
                for h in range(2):
                    n = step(dve.tensor_copy(a1[:, h, :], ps[:, h, 0:P]))
                    dve.wait_ge(dve_step, n)
                    n = step(dve.tensor_tensor(a1[:, h, :], ps[:, h, P:2 * P], a1[:, h, :], ALU.add))
                    dve.wait_ge(dve_step, n)
                    n = step(dve.tensor_tensor(a1[:, h, :], a1[:, h, :], dec[:, h, :], ALU.mult))
                    dve.wait_ge(dve_step, n)
                    n = step(dve.scalar_tensor_tensor(at[:, h, :], a1[:, h, :], -1.0, a1[:, h, :], ALU.mult, ALU.max))
                    dve.wait_ge(dve_step, n)
                    dve.tensor_scalar(at[:, h, :], at[:, h, :], 1.0, None, ALU.max).then_inc(a_ready, 1)
                for b in range(B):
                    dve.wait_ge(o_ps, 2 * (b // 4) + 2)
                    for h in range(2):
                        n = step(dve.bn_stats(st3[:, b, h, :], ps[:, 4 + 2 * (b // 4) + h, (b % 4) * P:(b % 4 + 1) * P]))
                dve.wait_ge(dve_step, n)
                for b in range(B):
                    n = step(dve.bn_aggr(mv3[:, b, :], st3[:, b, :, :].rearrange("p h s -> p (h s)")))
                dve.wait_ge(dve_step, n)
                dve.tensor_scalar(ve3[:, :], mv3[:, :, 1], GN_EPS, None, ALU.add).then_inc(mv3_ready, 1)
                dve.wait_ge(rs3_ready, 1)

                def finish(b):
                    p, q = b // 2, nb + PAIRS + b // 2
                    dve.wait_ge(yb_ready, b + 1)
                    dve.tensor_tensor(yc[:, b % 2, :], yb[:, b % 2, :], bet[:, :], ALU.add).then_inc(yc_ready, 1)
                    dve.wait_ge(yc_ready, b + 1)
                    dve.wait_ge(wr_ready, b + 1)
                    dve.wait_ge(xt_ps, q - 1)
                    last = dve.tensor_tensor(xn[:, (2 * q + b % 2) % 4, :], yc[:, b % 2, :], wr[:, b, :], ALU.mult)
                    if b % 2:
                        last.then_inc(xn_ready, 1)
                    if b in (5, 7):
                        low(q - 2, p - 2, p % 2)

                for b in range(B):
                    if b >= 2:
                        dve.wait_ge(yb_ready, b - 1)
                    for h in range(2):
                        last = dve.tensor_scalar(ya[:, b % 2, h * P:(h + 1) * P],
                                                 ps[:, 4 + 2 * (b // 4) + h, (b % 4) * P:(b % 4 + 1) * P],
                                                 mv3[:, b, 0:1], rs3[:, b:b + 1], ALU.subtract, ALU.mult)
                    last.then_inc(ya_ready, 1)
                    if b:
                        finish(b - 1)
                finish(B - 1)
                for p in (2, 3):
                    low(nb + PAIRS + p, p, p % 2)
                boundary(6, add_bank)

            dve.wait_ge(ld_x, 16)
            for i in range(PAIRS + 2):
                if i < PAIRS:
                    stats(0, i)
                if 1 <= i <= PAIRS:
                    normal(0, i - 1)
                if i >= 2:
                    low(i - 2, i - 2, 4 + i - 2)
            for n, (_, dst, src) in enumerate(SPLITS(ld_c, ld_s, craw, sraw, cl, sw_l)[0:3]):
                hi = SPLITS(ld_c, ld_s, craw, sraw, ch, sw_h)[n][1]
                dve.wait_ge(split_hi, n + 1)
                dve.tensor_tensor(dst, src, hi.bitcast(F32), ALU.subtract).then_inc(split_lo, 1)
            dve.wait_ge(coef_exp, 1)
            n = step(dve.tensor_scalar(cwork[:, 2:3], cwork[:, 0:1], 1.0, None, ALU.add))
            dve.wait_ge(dve_step, n)
            n = step(dve.reciprocal(cwork[:, 3:4], cwork[:, 2:3]))
            n = step(dve.tensor_tensor(cwork[:, 4:5], cvec[:, 0:1], cvec[:, 1:2], ALU.subtract))
            dve.wait_ge(dve_step, n)
            n = step(dve.scalar_tensor_tensor(cwork[:, 5:6], cwork[:, 4:5], cwork[:, 3:4], cvec[:, 1:2], ALU.mult, ALU.add))
            dve.wait_ge(dve_step, n)
            n = step(dve.tensor_scalar(cwork[:, 7:8], cwork[:, 5:6], cwork[:, 1:2], D ** -0.5, ALU.mult, ALU.mult))
            dve.wait_ge(dve_step, n)
            for m in range(4):
                dve.wait_ge(pre_hi, m + 1)
                half = slice((m % 2) * HALF, (m % 2 + 1) * HALF)
                dve.tensor_tensor(mk_l[:, m // 2, half], ps[:, m, :], mk_h[:, m // 2, half].bitcast(F32),
                                  ALU.subtract).then_inc(pre_lo, 1)
            attend0()
            if blocks > 1:
                experts(0)
            if blocks > 2:
                attend1()
            if blocks > 3:
                experts(1)
            if blocks > 4:
                dve.tensor_copy(maskf[:, :, :], masku[:, :, :]).then_inc(mask_ready, 1)
                dve.wait_ge(mask_ready, 1)
                dve.tensor_scalar(maskb[:, :, :], maskf[:, :, :], -1.0, 1e30, ALU.add, ALU.mult).then_inc(mask_ready, 1)
                dve.tensor_reduce(valid[:, :], maskf[:, :, :], AX.X, ALU.max).then_inc(mask_ready, 1)
                dve.wait_ge(mask_ready, 3)
                for b in range(B):
                    front2(b)
                for p in range(PAIRS):
                    scale2(p)
                boundary(4, add_scaled)
            if blocks > 5:
                experts(2)
            if blocks > 6:
                retain()
            if blocks > 7:
                experts(3)

def pack_small(mats, gates, wh):
    import numpy as np
    cols = [m[k * P:(k + 1) * P] for m in mats for k in range(K)]
    cols += [g[k * P:(k + 1) * P] for g in gates for k in range(K)]
    cols += [wh[h] for h in range(2)] + [wh[h].T for h in range(2)]
    return np.ascontiguousarray(np.concatenate(cols, axis=1))


def pack_experts(first, second, bias=None):
    import numpy as np
    chunks = second.shape[0] // P
    out = []
    for c in range(chunks):
        u = slice(c * P, (c + 1) * P)
        cols = [m[k * P:(k + 1) * P, u] for m in first for k in range(K)] + [second[u]]
        if bias is not None:
            cols.append(bias[u, None])
        out.append(np.concatenate(cols, axis=1))
    return np.ascontiguousarray(np.stack(out))


def decay_table():
    import numpy as np
    gam = 1.0 - 2.0 ** (-5.0 - np.arange(2, dtype=np.float64))
    s, t = np.arange(P)[:, None], np.arange(P)[None, :]
    d = np.where(t <= s, gam[:, None, None] ** (t - s), 0.0)
    d = d / np.sqrt(d.sum(axis=-1))[:, None, :] / np.sqrt(float(P))
    return np.ascontiguousarray(d.transpose(2, 0, 1).astype(np.float32))


def kernel(**inputs):
    import numpy as np
    import concourse.bacc as bacc
    from concourse.bass_utils import run_bass_kernel_spmd as run

    a = {k: np.asarray(v) for k, v in inputs.items()}
    cat = np.concatenate

    def units(w):
        return w.transpose(1, 0, 2).reshape(w.shape[1], -1)

    wkv = cat([a["L1_xattn_Wk"], a["L1_xattn_Wv"]], axis=0)
    small = pack_small(
        [a["L0_xattn_W_qkv"][:D], a["L0_xattn_W_o"].T, wkv[0::2].T, wkv[1::2].T, a["L1_xattn_Wq"].T,
         a["L3_xattn_wg_w"], a["L3_xattn_wo_w"]],
        [a["L0_ffn_gate_w"], a["L1_ffn_gate_w"].T,
         cat([a["L2_ffn_router_w"], a["L2_ffn_shared_expert_gate_w"]], axis=0).T, a["L3_ffn_w_gate"]],
        a["L3_xattn_Wh"])

    w0 = pack_experts([cat([a["L0_ffn_shared_w1"], units(a["L0_ffn_w1"])], axis=1)],
                      cat([a["L0_ffn_shared_w2"], a["L0_ffn_w2"].reshape(-1, D)], axis=0),
                      cat([a["L0_ffn_shared_b1"], a["L0_ffn_b1"].reshape(-1)]))
    b2 = cat([a["L0_ffn_b2"], a["L0_ffn_shared_b2"][None]], axis=0)

    def first1(shared, w):
        zero = np.zeros((D, 3 * P - shared.shape[1]), np.float32)
        return cat([shared, zero, units(w[:, :, P:]), units(w[:, :, :P])], axis=1)

    zero = np.zeros((3 * P - 2 * I1, D), np.float32)
    w1 = pack_experts([first1(a["L1_ffn_sw1"], a["L1_ffn_w1"]), first1(a["L1_ffn_sw3"], a["L1_ffn_w3"])],
                      cat([a["L1_ffn_sw2"], zero, a["L1_ffn_w2"][:, P:].reshape(-1, D), a["L1_ffn_w2"][:, :P].reshape(-1, D)], axis=0))

    gu, zero = a["L2_ffn_gate_up_proj"], np.zeros((64, D), np.float32)
    w2 = pack_experts([cat([a["L2_ffn_shared_gate_w"], zero, gu[:, :64].reshape(-1, D)], axis=0).T,
                       cat([a["L2_ffn_shared_up_w"], zero, gu[:, 64:].reshape(-1, D)], axis=0).T],
                      cat([a["L2_ffn_shared_down_w"].T, zero, a["L2_ffn_down_proj"].transpose(0, 2, 1).reshape(-1, D)], axis=0))

    gu, sh = a["L3_ffn_w_gate_up"], a["L3_ffn_w_sh_gate_up"]
    w3 = pack_experts([cat([sh[:, :512], units(gu[:, :, :P])], axis=1), cat([sh[:, 512:], units(gu[:, :, P:])], axis=1)],
                      cat([a["L3_ffn_w_sh_down"], a["L3_ffn_w_down"].reshape(-1, D)], axis=0))

    arrays = {
        "x_in": a["x"], "ctx_t": np.ascontiguousarray(a["ctx_2048"].reshape(T, D).T), "ctx_n": a["ctx_2048"],
        "mask_in": a["mask_BxS2_bk0"], "small_in": small,
        "coef_in": np.stack([a["L0_xattn_beta_q"], a["L0_xattn_beta_k"], a["L0_xattn_gate"], a["L0_xattn_log_tau"]]),
        "b2_in": b2, "gamma_in": a["L3_xattn_gn_gamma"], "beta_in": a["L3_xattn_gn_beta"],
        "decay_in": decay_table(), "ident_in": np.eye(P, dtype=np.float32),
        "w0_in": w0, "w1_in": w1, "w2_in": w2, "w3_in": w3,
    }
    arrays = {k: np.ascontiguousarray(v) for k, v in arrays.items()}
    nc = bacc.Bacc("TRN2", target_bir_lowering=False, num_devices=1)
    ap = {k: nc.dram_tensor(k, v.shape, mybir.dt.from_np(v.dtype), kind="ExternalInput").ap() for k, v in arrays.items()}
    ws = [ap.pop(f"w{n}_in") for n in range(4)]
    gates = [nc.dram_tensor(f"gates{n}", (FFN[n].gate_rows, T), F32, kind="Internal").ap() for n in range(4)]
    out = nc.dram_tensor("y_out", (B, P, D), F32, kind="ExternalOutput").ap()
    program(nc, **ap, w_in=ws, gates=gates, out=out, blocks=BLOCKS)
    r = run(nc, [arrays], core_ids=[0])
    return r.results[0]["y_out"]
```

```python
from contextlib import ExitStack

import concourse.bass as bass
from concourse import mybir

F32 = mybir.dt.float32
F32R = mybir.dt.float32r
F16 = mybir.dt.float16
BF16 = mybir.dt.bfloat16
I32 = mybir.dt.int32
U8 = mybir.dt.uint8
ALU = mybir.AluOpType
ACT = mybir.ActivationFunctionType
AX = mybir.AxisListType

P = 128
D = 256
K = D // P
B = 8
T = B * P
PAIRS = B // 2
HALF = T // 2
BLOCKS = 8
LN_EPS = 1e-5
RMS_EPS = 1e-6
GN_EPS = 1e-3
HEADS1 = 32
HD1 = D // HEADS1
GROUPS1 = HEADS1 // 4
VW = 3 * HD1 + 1
CLIP = 54
NEG = -3.0e38


TAIL = 2


class Ffn:

    def __init__(self, base, chunks, peeled, plain, experts, gate_rows, top, up, act):
        self.base, self.chunks, self.peeled, self.plain = base, chunks, peeled, plain
        self.experts, self.gate_rows, self.top, self.up, self.act = experts, gate_rows, top, up, act
        self.steps = (chunks - peeled - TAIL) // 2
        self.width = (K * P * (2 if up else 1)) + D
        self.bias = not up
        assert (chunks - peeled - TAIL) % 2 == 0


FFN = [
    Ffn(0, 10, 2, 2, 8, 8, 2, False, ACT.Gelu),
    Ffn(10, 14, 6, 3, 8, 8, 2, True, ACT.Silu),
    Ffn(24, 33, 3, 0, 64, 65, 8, True, ACT.Silu),
    Ffn(57, 12, 4, 4, 8, 8, 2, True, ACT.Silu),
]
I1 = 176
R1 = I1 - P
GATED = [sum(f.chunks - f.plain for f in FFN[:n]) for n in range(len(FFN))]

SMALL = ["wq0", "wo0", "wk1", "wv1", "wq1", "wg3", "wo3"]
GATE_AT = []
_at = len(SMALL) * K * D
for _f in FFN:
    GATE_AT.append(_at)
    _at += K * _f.gate_rows
WH_AT = _at
LP = 66
LD_M = 16 * 6
SCHEDULE1 = {
    "raw": {2: 8, 3: 10}, "raw_copy": {2: 12, 3: 14}, "squares": {2: 10, 3: 12},
    "scale": {1: 13}, "rows": {4: 14, 5: 14, 6: 14, 7: 15},
    "high": {2: 0, 3: 5, 4: 18, 5: 19, 6: 21, 7: 24},
    "low": {1: 0, 2: 1, 3: 4, 4: 16, 5: 17, 6: 19, 7: 22},
    "turn": {1: 0, 2: 3, 3: 5, 4: 16, 5: 18, 6: 20, 7: 23},
    "out": {1: 4, 2: 7, 3: 10, 4: 20, 5: 22, 6: 24, 7: 32},
}
for _step, _unit in (("stats", 22), ("power", 24), ("xnormal", 26), ("xturn", 24), ("xhigh", 29), ("xlow", 28)):
    SCHEDULE1[_step] = {p: _unit + 16 * p for p in range(PAIRS - 1)}


def between(u, mine):
    for what, do in mine.items():
        for k, unit in SCHEDULE1[what].items():
            if unit == u:
                do(k)


WHT_AT = WH_AT + D
SMALL_W = WHT_AT + D


def SPLITS(ld_w, ld_c, ld_s, craw, sraw, c_part, s_part):
    first, second = K * D, 4 * K * D
    return [(ld_w, s_part[:, 0:first], sraw[:, 0:first]),
            (ld_c, c_part[:, :, 0:HALF], craw[:, :, 0:HALF]), (ld_c, c_part[:, :, HALF:T], craw[:, :, HALF:T]),
            (ld_s, s_part[:, first:second], sraw[:, first:second]),
            (ld_s, s_part[:, second:WHT_AT], sraw[:, second:WHT_AT])]


def program(nc, x_in, ctx_t, ctx_n, mask_in, small_in, coef_in, b2_in, gamma_in, beta_in,
            decay_in, ident_in, w_in, gates, out, blocks=8):
    with ExitStack() as ctx:
        def sb(name, shape, dt=F32):
            return ctx.enter_context(nc.sbuf_tensor(name, shape, dt))

        def sem(name):
            return ctx.enter_context(nc.semaphore(name))

        x = sb("x", [P, B, D])
        xs = sb("xs", [P, K, B, 2, P], F32R)
        xn = sb("xn", [P, 4, D])
        ch = sb("ch", [P, K, T], F32R)
        cl = sb("cl", [P, K, T], F32R)
        mk_h = sb("mk_h", [P, 2, T], F32R)
        mk_l = sb("mk_l", [P, 2, T], F32R)
        vw = sb("vw", [P, 2, B, P])
        vw0 = vw[:, :, :, :].rearrange("p h b e -> p (h b e)").rearrange("p (b d) -> p b d", b=B)
        two = ExitStack()
        cn = two.enter_context(nc.sbuf_tensor("cn", [P, B, D], F32))
        two.close()
        kst = sb("kst", [P, B, GROUPS1, P], F16)
        vp = sb("vp", [P, B, HEADS1, VW], BF16)
        sw_h = sb("sw_h", [P, WHT_AT], F32R)
        sw_l = sb("sw_l", [P, WHT_AT], F32R)
        g_h = sb("g_h", [P, 2, P], F32R)
        g_l = sb("g_l", [P, 2, P], F32R)
        ident = sb("ident", [P, P])
        ident16 = sb("ident16", [P, P], F16)
        wraw = sb("wraw", [P, 2, 3 * D])
        wup_h = sb("wup_h", [P, 2, 2 * D], F32R)
        wup_l = sb("wup_l", [P, 2, 2 * D], F32R)
        wdn_h = sb("wdn_h", [P, 2, D], F32R)
        wdn_l = sb("wdn_l", [P, 2, D], F32R)
        b2 = sb("b2", [FFN[0].experts + 1, D])
        gam = sb("gam", [P, D])
        bet = sb("bet", [P, D])
        dec = sb("dec", [P, 2, P])
        masku = sb("masku", [P, B, P], U8)
        stat = sb("stat", [P, 2, 2, 6])
        mv = sb("mv", [P, 2, 2, 2])
        var_eps = sb("var_eps", [P, 2, 2])
        rstd = sb("rstd", [P, 2, 2])
        nmean = sb("nmean", [P, 2, 2])
        shift = sb("shift", [P, 2, 2])
        mhalf = sb("mhalf", [P, 8])
        cvec = sb("cvec", [P, 4])
        cwork = sb("cwork", [P, 8])
        negm = sb("negm", [P, 2])
        esum = sb("esum", [P, B])
        rsum = sb("rsum", [P, B])
        valid = sb("valid", [P, B])
        sc = sb("sc", [P, 2, P])
        work = sb("work", [P, 2, P])
        ex = sb("ex", [P, 2, P])
        ep = sb("ep", [P, 2, P])
        ept = sb("ept", [P, 2, P])
        top = sb("top", [P, 2, 56])

        early = ExitStack()
        craw = early.enter_context(nc.sbuf_tensor("craw", [P, K, T], F32))
        sraw = early.enter_context(nc.sbuf_tensor("sraw", [P, SMALL_W], F32))
        early.close()

        mid = ExitStack()

        def sbm(name, shape, dt=F32):
            return mid.enter_context(nc.sbuf_tensor(name, shape, dt))
        s_act = sbm("s_act", [P, 2, HALF])
        sg = sbm("sg", [P, 2, HALF])
        tt = sbm("tt", [P, 2, HALF])
        gb = sbm("gb", [P, 2, T])
        gt = sbm("gt", [P, T])
        routing = ExitStack()

        def sbr(name, shape, dt=F32):
            return routing.enter_context(nc.sbuf_tensor(name, shape, dt))
        lgt = sbr("lgt", [P, 2, HALF])
        lg = sbr("lg", [P, 2, 4, 65])
        le = sbr("le", [P, 2, 4, 65])
        lm = sbr("lm", [P, 2, 4, 65])
        m8 = sbr("m8", [P, 2, 4, 8])
        gsum = sbr("gsum", [P, 2, 16])
        routing.close()
        th = sbm("th", [P, 2, T], F32R)
        tl = sbm("tl", [P, 2, T], F32R)
        mid.close()

        att = ExitStack()

        def sba(name, shape, dt=F32):
            return att.enter_context(nc.sbuf_tensor(name, shape, dt))
        maskf = sba("maskf", [P, B, P])
        maskb = sba("maskb", [P, B, P])
        at = sba("at", [P, 2, P])
        a1 = sba("a1", [P, 2, P])
        wr = sba("wr", [P, B, D])
        wb = sba("wb", [P, B, D])
        ya = sba("ya", [P, B, D])
        st3 = sba("st3", [P, B, 2, 6])
        mv3 = sba("mv3", [P, B, 2])
        ve3 = sba("ve3", [P, B])
        rs3 = sba("rs3", [P, B])
        nm3 = sba("nm3", [P, B])
        att.close()

        one = ExitStack()

        def sb1(name, shape, dt=F32):
            return one.enter_context(nc.sbuf_tensor(name, shape, dt))
        sq = sb1("sq", [P, 2, D])
        ss = sb1("ss", [P, 4, HEADS1])
        nw_a = sb1("nw_a", [P, 4, HEADS1])
        nw_b = sb1("nw_b", [P, 4, HEADS1])
        nw_h = sb1("nw_h", [P, 4, HEADS1])
        qf = sb1("qf", [P, 4, D])
        vres = sb1("vres", [P, 2, 2, D])
        stk = sb1("stk", [P, 2, HEADS1, 4, HD1], F16)
        nw_y = sb1("nw_y", [P, 4, HEADS1])
        qst = sb1("qst", [P, 4, GROUPS1, P], F16)
        e1 = sb1("e1", [P, 4, HALF])
        eh = sb1("eh", [P, 4, HALF], F16)
        el = sb1("el", [P, 4, HALF], F16)
        o3 = sb1("o3", [P, 2, 16, HD1])
        oy = sb1("oy", [P, 2, 16, HD1])
        r3 = sb1("r3", [P, 2, 16])
        one.close()

        ps = ctx.enter_context(nc.psum_tensor("ps", [P, 8, 512], F32))
        ps16 = ps[:, :, :].bitcast(F16)

        ld_x, ld_c, ld_s, ld_m, ld_n = sem("ld_x"), sem("ld_c"), sem("ld_s"), sem("ld_m"), sem("ld_n")
        w_loaded = [sem("w_loaded0"), sem("w_loaded1")]
        g_loaded = [sem("g_loaded0"), sem("g_loaded1")]
        g_stored, stored = sem("g_stored"), sem("stored")
        const_ready = sem("const_ready")
        dve_step = sem("dve_step")
        ld_i, ld_w = sem("ld_i"), sem("ld_w")
        split_hi, split_lo, small_lo = sem("split_hi"), sem("split_lo"), sem("small_lo")
        pre_ps, pre_hi, pre_lo = sem("pre_ps"), sem("pre_hi"), sem("pre_lo")
        mv_ready, rstd_ready, shift_ready = sem("mv_ready"), sem("rstd_ready"), sem("shift_ready")
        nx_ready = sem("nx_ready")
        xn_ready, xt_ps, xh_ready, xl_ready = sem("xn_ready"), sem("xt_ps"), sem("xh_ready"), sem("xl_ready")
        coef_exp = sem("coef_exp")
        sc_ps, sc_read, negm_ready, ex_ready = sem("sc_ps"), sem("sc_read"), sem("negm_ready"), sem("ex_ready")
        ep_ready, ept_ps, ept_ready = sem("ep_ready"), sem("ept_ps"), sem("ept_ready")
        y_ps, x_added = sem("y_ps"), sem("x_added")
        up_ps, s_ready, sg_ready, t_ready = sem("up_ps"), sem("s_ready"), sem("sg_ready"), sem("t_ready")
        th_ready, tl_ready, dn_ps = sem("th_ready"), sem("tl_ready"), sem("dn_ps")
        wup_hi, wup_lo, wdn_hi, wdn_lo = sem("wup_hi"), sem("wup_lo"), sem("wdn_hi"), sem("wdn_lo")
        lt_ps, lt_ready, lg_ps = sem("lt_ps"), sem("lt_ready"), sem("lg_ps")
        ld_ready, le_ready, gw_ready = sem("ld_ready"), sem("le_ready"), sem("gw_ready")
        gt_ps, gt_ready = sem("gt_ps"), sem("gt_ready")
        qk_ps, qk_sq, ss_read = sem("qk_ps"), sem("qk_sq"), sem("ss_read")
        qn_ready, st_hi, st_lo = sem("qn_ready"), sem("st_hi"), sem("st_lo")
        qt_ps, qt_ready = sem("qt_ps"), sem("qt_ready")
        v_ps, v1_ready, v2_ready, v3_ready, r1_ready = (
            sem("v_ps"), sem("v1_ready"), sem("v2_ready"), sem("v3_ready"), sem("r1_ready"))
        s1_ps, e1_ready, eh_ready, el_ready = sem("s1_ps"), sem("e1_ready"), sem("eh_ready"), sem("el_ready")
        o1_ps, o1_read, oy_ready = sem("o1_ps"), sem("o1_read"), sem("oy_ready")
        a_ps, a_ready, o_ps, wg_ps, wr_ready = sem("a_ps"), sem("a_ready"), sem("o_ps"), sem("wg_ps"), sem("wr_ready")
        mv3_ready, rs3_ready, nm3_ready, ya_ready = sem("mv3_ready"), sem("rs3_ready"), sem("nm3_ready"), sem("ya_ready")
        wb_ready, wg_ready, mask_ready, av_ps = sem("wb_ready"), sem("wg_ready"), sem("mask_ready"), sem("av_ps")

        def small(n, k):
            return slice((n * K + k) * D, (n * K + k + 1) * D)

        def key_bank(z):
            return 7 if z < 4 else (1, 3)[z % 2]

        def gate_cols(n, k):
            return slice(GATE_AT[n] + k * FFN[n].gate_rows, GATE_AT[n] + (k + 1) * FFN[n].gate_rows)

        LAYERS = [n for n in range(4) if 2 * n + 1 < blocks]
        CHUNKS = sum(FFN[n].chunks for n in LAYERS)

        def norms_before(block):
            return PAIRS * (block + (1 if block > 6 else 0))

        def after(i, count, rate):
            return count if i is None else rate * i + count

        def every_chunk(eng, n, do):
            f = FFN[n]
            for c in range(f.peeled):
                do(n, c, None)
            with eng.Fori(0, f.steps) as i:
                for u in range(2):
                    do(n, f.peeled + u, i)
            for c in range(f.chunks - TAIL, f.chunks):
                do(n, c, None)

        def gated_late(n, c):
            return n == 2 and c == 0

        def sg_count(n, c, h):
            return sum(2 * (FFN[m].chunks - FFN[m].plain) for m in range(1, n)) + 2 * (c - FFN[n].plain) + h + 1

        def gated(n, c):
            return GATED[n] + c - FFN[n].plain

        def segments(n, c):
            f = FFN[n]
            if n == 2:
                return [(0, P, 64)] if c == 0 else [(0, 64, 2 * (c - 1)), (64, 64, 2 * (c - 1) + 1)]
            if n == 1 and c < f.peeled:
                found, r = [], 0
                while r < P:
                    unit = (c - f.plain) * P + r
                    e = unit // R1
                    size = min(P - r, (e + 1) * R1 - unit)
                    found.append((r, size, e))
                    r += size
                return found
            return [(0, P, c - (f.peeled if n == 1 else f.plain))]

        def g_loads(n, c):
            return sum(len(segments(m, d)) for m in range(n + 1) for d in range(FFN[m].plain, FFN[m].chunks)
                       if gated(m, d) % 2 == gated(n, c) % 2 and (m < n or d <= c))

        block_ = ctx.enter_context(nc.Block())

        @block_.sync
        def _(sp):
            sp.dma_start(x[:, :, :], x_in.rearrange("b p d -> p b d")).then_inc(ld_x, 16)
            sp.dma_start(ident[:, :], ident_in).then_inc(ld_i, 16)
            sp.dma_start(sraw[:, 0:K * D], small_in[:, 0:K * D]).then_inc(ld_w, 16)
            sp.dma_start(craw[:, :, :], ctx_t.rearrange("(k p) t -> p k t", p=P)).then_inc(ld_c, 16)
            sp.dma_start(sraw[:, K * D:], small_in[:, K * D:]).then_inc(ld_s, 16)
            sp.dma_start(cvec[:, :], coef_in.rearrange("(o c) -> o c", o=1).broadcast_to([P, 4])).then_inc(ld_m, 16)
            sp.dma_start(b2[:, :], b2_in).then_inc(ld_m, 16)
            sp.dma_start(gam[:, :], gamma_in.rearrange("(o c) -> o c", o=1).broadcast_to([P, D])).then_inc(ld_m, 16)
            sp.dma_start(bet[:, :], beta_in.rearrange("(o c) -> o c", o=1).broadcast_to([P, D])).then_inc(ld_m, 16)
            sp.dma_start(dec[:, :, :], decay_in).then_inc(ld_m, 16)
            sp.dma_start(masku[:, :, :], mask_in.rearrange("(o b) m -> o b m", o=1).broadcast_to([P, B, P])).then_inc(ld_m, 16)

            def load(n, c, i):
                f, g = FFN[n], FFN[n].base + c
                if g >= 2:
                    sp.wait_ge(t_ready, after(i, 2 * (g - 1), 4))
                if i is None:
                    src = w_in[n][c]
                else:
                    src = w_in[n][bass.ds(2 * i + c, 1), :, :].rearrange("o p c -> (o p) c")
                sp.dma_start(wraw[:, g % 2, 0:f.width + f.bias], src).then_inc(w_loaded[g % 2], 16)

            for n in LAYERS:
                every_chunk(sp, n, load)

            for p in range(PAIRS):
                sp.wait_ge(x_added, PAIRS * (blocks - 1) + p + 1)
                sp.dma_start(out[2 * p:2 * p + 2].rearrange("b p d -> p b d"),
                             x[:, 2 * p:2 * p + 2, :]).then_inc(stored, 16)
            sp.wait_ge(stored, 16 * PAIRS)

        @block_.gpsimd
        def _(pool):
            pool.memset(mhalf[:, :], -0.5).then_inc(const_ready, 1)
            pool.wait_ge(const_ready, 1)

            def power(block, p):
                r = PAIRS * block + p
                pool.wait_ge(mv_ready, r + 1)
                if r >= 2:
                    pool.wait_ge(nx_ready, r - 1)
                pool.tensor_tensor(rstd[:, r % 2, :], var_eps[:, r % 2, :], mhalf[:, 0:2],
                                   ALU.pow).then_inc(rstd_ready, 1)
                pool.wait_ge(rstd_ready, r + 1)
                pool.tensor_tensor(shift[:, r % 2, :], nmean[:, r % 2, :], rstd[:, r % 2, :],
                                   ALU.mult).then_inc(shift_ready, 1)

            def norm(block):
                for p in range(PAIRS):
                    power(block, p)

            def third(b):
                heads = lambda a: a.rearrange("p (n d) -> p n d", d=HD1)
                pool.wait_ge(v2_ready, b + 1)
                pool.tensor_tensor(vp[:, b, :, 2 * HD1:3 * HD1], heads(vres[:, b % 2, 0, :]), vp[:, b, :, HD1:2 * HD1],
                                   ALU.subtract).then_inc(v3_ready, 1)

            def stack_low(z):
                pool.wait_ge(st_hi, z + 1)
                for r in (1, 3):
                    last = pool.tensor_tensor(stk[:, z % 2, :, r, :], qf[:, z % 4, :].rearrange("p (n d) -> p n d", d=HD1),
                                              stk[:, z % 2, :, 0, :], ALU.subtract)
                last.then_inc(st_lo, 1)

            def gate(n, c, i):
                f, g = FFN[n], FFN[n].base + c
                if c < f.plain or not f.up:
                    return
                slot = gated(n, c) % 2
                pool.wait_ge(g_loaded[slot], after(i, 16 * g_loads(n, c), 16 * len(segments(n, f.peeled))))
                for h in range(2):
                    a = s_act
                    if gated_late(n, c):
                        a = tt
                        pool.wait_ge(t_ready, 2 * g + h + 1)
                    else:
                        pool.wait_ge(s_ready, after(i, 2 * g + h + 1, 4))
                        if c and gated_late(n, c - 1):
                            pool.wait_ge(tl_ready, 2 * (g - 1) + h + 1)
                        else:
                            pool.wait_ge(t_ready, after(i, 2 * (g - 1) + h + 1, 4))
                    pool.tensor_tensor(sg[:, h, :], a[:, h, :], gb[:, slot, h * HALF:(h + 1) * HALF],
                                       ALU.mult).then_inc(sg_ready, 1)

            norm(0)
            pool.memset(vp[:, :, :, VW - 1:VW], 1.0).then_inc(const_ready, 1)
            pool.wait_ge(ld_i, 16)
            pool.tensor_copy(ident16[:, :], ident[:, :]).then_inc(const_ready, 1)
            for n in (3, 4):
                _, dst, src = SPLITS(ld_w, ld_c, ld_s, craw, sraw, cl, sw_l)[n]
                hi = SPLITS(ld_w, ld_c, ld_s, craw, sraw, ch, sw_h)[n][1]
                pool.wait_ge(split_hi, n + 1)
                pool.tensor_tensor(dst, src, hi.bitcast(F32), ALU.subtract).then_inc(small_lo, 1)
            for p in range(PAIRS):
                if p and blocks > 1:
                    power(1, p - 1)
                for b in (2 * p, 2 * p + 1):
                    third(b)
                if p == PAIRS - 1 and blocks > 1:
                    power(1, p)
                if p % 2:
                    for z in range(2 * p - 2, 2 * p + 2):
                        stack_low(z)
            if blocks > 2:
                norm(2)

                def mixed(w):
                    b, s = w // 2, w % 2
                    pool.wait_ge(o1_read, w + 1)
                    pool.tensor_tensor(oy[:, s, :, :], o3[:, s, :, :], r3[:, s, :].unsqueeze(2).broadcast_to([P, 16, HD1]),
                                       ALU.mult).then_inc(oy_ready, 1)
                    pool.wait_ge(oy_ready, w + 1)
                    dst = x[:, b, s * P:(s + 1) * P]
                    last = pool.tensor_tensor(dst, dst, oy[:, s, :, :].rearrange("p n d -> p (n d)"), ALU.add)
                    if w % 4 == 3:
                        last.then_inc(x_added, 1)

                for u in range(8 * B):
                    pool.wait_ge(e1_ready, u + 1)
                    if u >= 4:
                        pool.wait_ge(o1_ps, u - 3)
                    pool.tensor_scalar(eh[:, u % 4, :], e1[:, u % 4, :], 1.0, 0.0,
                                       ALU.mult, ALU.add).then_inc(eh_ready, 1)
                    if u % 4 == 0 and u >= 8:
                        mixed(u // 4 - 2)
                    if blocks > 3:
                        between(u, {"power": lambda p: power(3, p)})
                mixed(2 * B - 2)
                mixed(2 * B - 1)
            if blocks > 3:
                power(3, PAIRS - 1)
                every_chunk(pool, 1, gate)
            if blocks > 4:
                norm(4)
            if blocks > 5:
                norm(5)
                every_chunk(pool, 2, gate)
            if blocks > 6:
                norm(6)
                for b in range(B):
                    pool.wait_ge(wr_ready, b + 1)
                    pool.tensor_tensor(wb[:, b, :], wr[:, b, :], bet[:, :], ALU.mult).then_inc(wb_ready, 1)
                    pool.wait_ge(wb_ready, b + 1)
                    pool.tensor_tensor(wr[:, b, :], wr[:, b, :], gam[:, :], ALU.mult).then_inc(wg_ready, 1)
                for s in range(2):
                    four = slice(4 * s, 4 * s + 4)
                    pool.wait_ge(mv3_ready, s + 1)
                    pool.tensor_tensor(rs3[:, four], ve3[:, four], mhalf[:, four], ALU.pow).then_inc(rs3_ready, 1)
            if blocks > 7:
                norm(7)
                every_chunk(pool, 3, gate)

        @block_.tensor
        def _(pe):
            def product(dst, lhs, rhs, start=True, stop=True):
                last = None
                for k in range(K):
                    (ah, al), (bh, bl) = lhs(k), rhs(k)
                    for m, (a, b_) in enumerate(((ah, bh), (ah, bl), (al, bh))):
                        last = pe.matmul(dst, a, b_, start=start and k == 0 and m == 0,
                                         stop=stop and k == K - 1 and m == 2, skip_group_check=True)
                return last

            def x_tile(b):
                return lambda k: (xs[:, k, b, 0, :], xs[:, k, b, 1, :])

            def x_half(h):
                return lambda k: (xs[:, k, 4 * h:4 * h + 4, 0, :], xs[:, k, 4 * h:4 * h + 4, 1, :])

            def ctx_tile(b):
                return lambda k: (ch[:, k, b * P:(b + 1) * P], cl[:, k, b * P:(b + 1) * P])

            def ctx_cols(at_, size):
                return lambda k: (ch[:, k, at_:at_ + size], cl[:, k, at_:at_ + size])

            def weight(n, at_=0, size=D):
                def of(k):
                    a = (n * K + k) * D + at_
                    return sw_h[:, a:a + size], sw_l[:, a:a + size]
                return of

            def turn(q, bank, gated=False):
                if gated:
                    pe.wait_ge(xn_ready, q - norms_before(6) - PAIRS + 1)
                else:
                    pe.wait_ge(nx_ready, q + 1 - (PAIRS if q >= norms_before(7) else 0))
                for k in range(K):
                    for t in range(2):
                        at_ = k * D + t * P
                        last = pe.transpose(ps[:, bank, at_:at_ + P], xn[:, (2 * q + t) % 4, k * P:(k + 1) * P], ident[:, :])
                last.then_inc(xt_ps, 1)

            def norm(block):
                for p in range(PAIRS):
                    turn(norms_before(block) + p, 4 + p)

            def keys0(h):
                pe.wait_ge(split_lo, 2 + h)
                for j in range(2):
                    product(ps[:, 2 * h + j, :], weight(0, j * P, P), ctx_cols(h * HALF, HALF)).then_inc(pre_ps, 1)

            def values0():
                pe.wait_ge(small_lo, 1)
                for p in range(PAIRS):
                    for t in range(2):
                        last = product(ps[:, 4 + p, t * D:(t + 1) * D], ctx_tile(2 * p + t), weight(1))
                    last.then_inc(pre_ps, 1)
                pe.wait_ge(pre_hi, 5)
                for h in range(2):
                    wt = sraw[:, WHT_AT + h * P:WHT_AT + (h + 1) * P]
                    last = pe.matmul(ps[:, 4, h * P:(h + 1) * P], wt, wt, start=True, stop=True)
                last.then_inc(pre_ps, 1)

            def queries(r):
                pe.wait_ge(xl_ready, norms_before(2) + (r + 1 if r < 2 else PAIRS))
                if r == 3:
                    pe.wait_ge(qk_sq, B + r)
                for t in range(2):
                    last = product(ps[:, 4 + min(r, 2), t * D:(t + 1) * D], x_tile(2 * r + t), weight(4))
                last.then_inc(qk_ps, 1)

            def stacks(z, bank):
                pe.wait_ge(st_lo, z + 1)
                for g in range(GROUPS1):
                    part = stk[:, z % 2, 4 * g:4 * g + 4, :, :].rearrange("p j r d -> p (j r d)")
                    last = pe.transpose(ps16[:, bank, g * P:(g + 1) * P], part, ident16[:, :])
                last.then_inc(qt_ps, 1)

            def keys_values(b):
                if b >= 2:
                    pe.wait_ge(qk_sq, b - 1)
                    pe.wait_ge(r1_ready, b - 1)
                product(ps[:, 2 + b % 2, 0:D], ctx_tile(b), weight(2)).then_inc(qk_ps, 1)
                product(ps[:, 2 + b % 2, D:2 * D], ctx_tile(b), weight(3)).then_inc(v_ps, 1)

            def key_stacks(z):
                if z == 4:
                    pe.wait_ge(qk_sq, B)
                    pe.wait_ge(r1_ready, B)
                elif z:
                    pe.wait_ge(qt_ready, z if z < 4 else z - 1)
                stacks(z, key_bank(z))

            def last_keys(h):
                for s in range(2):
                    for m, (a, b_) in enumerate(((g_h, ch), (g_h, cl), (g_l, ch))):
                        last = pe.matmul(ps[:, 2 * h + s, :], a[:, h, :], b_[:, h, s * HALF:(s + 1) * HALF],
                                         start=m == 0, stop=m == 2)
                    last.then_inc(pre_ps, 1)

            def last_values(b):
                if b < 4:
                    pe.wait_ge(pre_lo, 6 + b)
                else:
                    pe.wait_ge(pre_hi, 14 + b - 4)
                for h in range(2):
                    t = slice(b * P, (b + 1) * P)
                    wh = slice(WH_AT + (h - 1) * P, WH_AT + (h + 1) * P)
                    for m, (a, w) in enumerate(((ch, sw_h), (ch, sw_l), (cl, sw_h))):
                        last = pe.matmul(ps[:, b % 4, h * D:(h + 1) * D], a[:, h, t], w[:, wh],
                                         start=m == 0, stop=m == 2)
                last.then_inc(pre_ps, 1)

            def attend0():
                turn(0, 4)
                keys0(0)
                turn(1, 5)
                keys0(1)
                turn(2, 6)
                turn(3, 7)
                pe.wait_ge(pre_lo, 2)

                def scores(p):
                    for b in (2 * p, 2 * p + 1):
                        pe.wait_ge(xl_ready, p + 1)
                        if b >= 2:
                            pe.wait_ge(sc_read, b - 1)
                        product(ps[:, b % 2, 0:D], x_tile(b),
                                lambda k: (mk_h[:, k, p * D:(p + 1) * D], mk_l[:, k, p * D:(p + 1) * D])).then_inc(sc_ps, 1)

                scores(0)
                pe.wait_ge(xl_ready, PAIRS)
                values0()
                pe.wait_ge(small_lo, 2)
                pe.wait_ge(pre_lo, 4)
                keys_values(0)
                keys_values(1)
                pe.wait_ge(const_ready, 3)
                for p in range(PAIRS):
                    if p + 1 < PAIRS:
                        scores(p + 1)
                    if p in (1, 3):
                        keys_values(2 * p)
                        keys_values(2 * p + 1)
                    if p == 2:
                        pe.wait_ge(qt_ready, 4)
                    pe.wait_ge(pre_hi, 8)
                    if p == PAIRS - 1 and blocks > 1:
                        pe.wait_ge(xl_ready, norms_before(1) + 1)
                    for b in (2 * p, 2 * p + 1):
                        pe.wait_ge(ep_ready, b + 1)
                        pe.transpose(ps[:, 4 + (p + 1) % PAIRS, (b % 2) * P:(b % 2 + 1) * P], ep[:, b % 2, :],
                                     ident[:, :]).then_inc(ept_ps, 1)
                    if p == 0:
                        pe.wait_ge(pre_lo, 5)
                    for b in (2 * p, 2 * p + 1):
                        pe.wait_ge(ept_ready, b + 1)
                        pe.matmul(ps[:, 4 + p, (b % 2) * D:(b % 2 + 1) * D], ept[:, b % 2, :], vw0[:, b, :],
                                  start=True, stop=True).then_inc(av_ps, 1)
                    if p and blocks > 1:
                        turn(norms_before(1) + p - 1, 4 + p - 1)
                    if p == 1:
                        keys_values(4)
                        keys_values(5)
                        for z in range(4):
                            key_stacks(z)

            def attend2():
                nb = norms_before(4)
                norm(4)

                def scores(p):
                    pe.wait_ge(xl_ready, nb + p + 1)
                    pe.wait_ge(sc_read, B + p)
                    for t in range(2):
                        last = product(ps[:, t, 0:D], x_tile(2 * p + t),
                                       lambda k: (ch[:, k, p * D:(p + 1) * D], cl[:, k, p * D:(p + 1) * D]))
                    last.then_inc(sc_ps, 1)

                scores(0)
                for p in range(PAIRS):
                    if p + 1 < PAIRS:
                        scores(p + 1)
                    if p == 0:
                        pe.wait_ge(ld_n, 16)
                    pe.wait_ge(ex_ready, B + 2 * p + 2)
                    if p >= 2:
                        pe.wait_ge(ept_ready, B + 2 * p - 2)
                    for t in range(2):
                        last = pe.transpose(ps[:, 2 + p % 2, t * P:(t + 1) * P], ex[:, t, :], ident[:, :])
                    last.then_inc(ept_ps, 2)
                    pe.wait_ge(ept_ready, B + 2 * p + 2)
                    for t in range(2):
                        last = pe.matmul(ps[:, 4 + p, t * D:(t + 1) * D], ept[:, t, :], cn[:, 2 * p + t, :],
                                         start=True, stop=True)
                    last.then_inc(av_ps, 2)
                    if p and blocks > 5:
                        turn(norms_before(5) + p - 1, 4 + p - 1)

            def up(n, c, i, h):
                f, g = FFN[n], FFN[n].base + c
                pe.wait_ge(wup_lo, after(i, g + 1, 2))
                if g:
                    pe.wait_ge(s_ready, after(i, 2 * (g - 1) + h + 1, 4))
                    pe.wait_ge(t_ready, after(i, 2 * (g - 1) + h + 1, 4))
                for m in range(2 if f.up else 1):
                    def w(k):
                        a = m * D + k * P
                        return wup_h[:, g % 2, a:a + P], wup_l[:, g % 2, a:a + P]
                    last = product(ps[:, 2 * h + m, :], w, x_half(h))
                last.then_inc(up_ps, 1)

            def down(n, c, i):
                f, g = FFN[n], FFN[n].base + c
                pe.wait_ge(wdn_lo, after(i, g + 1, 2))
                if c == 0:
                    pe.wait_ge(gt_ready, 2 * n + 2)
                for b in range(B):
                    if b % 4 == 0:
                        pe.wait_ge(tl_ready, after(i, 2 * g + b // 4 + 1, 4))
                    dst = ps[:, 4 + b // 2, (b % 2) * D:(b % 2 + 1) * D]
                    t = slice(b * P, (b + 1) * P)
                    parts = ((th, wdn_h), (th, wdn_l), (tl, wdn_h))
                    for m, (a, w) in enumerate(parts):
                        last = pe.matmul(dst, a[:, g % 2, t], w[:, g % 2, :],
                                         start=c == 0 and i is None and b % 2 == 0 and m == 0,
                                         stop=c == f.chunks - 1 and m == 2, skip_group_check=True)
                    if c == f.chunks - 1 and b in (1, 3, 5):
                        last.then_inc(y_ps, 1)
                last.then_inc(dn_ps, 1)

            def experts(n):
                f, nb = FFN[n], norms_before(2 * n + 1)
                def logits(h):
                    pe.wait_ge(xl_ready, nb + 2 * h + 2)
                    if n == 1:
                        pe.wait_ge(o1_read, 2 * B)
                    gate_w = lambda k: (sw_h[:, gate_cols(n, k)], sw_l[:, gate_cols(n, k)])
                    product(ps[0:f.gate_rows, 4 + 2 * h, :], gate_w, x_half(h)).then_inc(lt_ps, 1)

                def logit_rows(h):
                    pe.wait_ge(lt_ready, 2 * n + h + 1)
                    for t in range(4):
                        last = pe.transpose(ps[:, 5 + 2 * h, t * LP:t * LP + f.gate_rows],
                                            lgt[0:f.gate_rows, h, t * P:(t + 1) * P],
                                            ident[0:f.gate_rows, 0:f.gate_rows])
                    last.then_inc(lg_ps, 1)

                def gate_cols_(h):
                    pe.wait_ge(gw_ready, 2 * n + h + 1)
                    for t in range(4):
                        last = pe.transpose(ps[0:f.gate_rows, 4 + 2 * h, t * P:(t + 1) * P],
                                            lm[:, h, t, 0:f.gate_rows], ident[:, :])
                    last.then_inc(gt_ps, 1)

                logits(0)
                turn(nb + PAIRS - 1, 7)
                up(n, 0, None, 0)
                logits(1)
                logit_rows(0)
                logit_rows(1)
                up(n, 0, None, 1)
                if n == 0:
                    for z in (4, 5, 6):
                        key_stacks(z)
                gate_cols_(0)
                if n == 0:
                    key_stacks(7)
                gate_cols_(1)

                def chunk(n, c, i):
                    if c:
                        up(n, c, i, 0)
                        up(n, c, i, 1)
                        down(n, c - 1, i)
                every_chunk(pe, n, chunk)
                if n == 0:
                    for b in range(B):
                        pe.matmul(ps[:, 4 + b // 2, (b % 2) * D:(b % 2 + 1) * D], gt[0:f.experts + 1, b * P:(b + 1) * P],
                                  b2[:, :], start=False, stop=False, skip_group_check=True)
                down(n, f.chunks - 1, None)

            def scores1(u):
                b, s, j = u // 8, (u // 4) % 2, u % 4
                if j == 0:
                    pe.wait_ge(qt_ready, B + b + 1)
                if u >= 4:
                    pe.wait_ge(e1_ready, u - 3)
                r = slice(32 * j, 32 * j + 32)
                for g in range(4):
                    last = pe.matmul(ps[:, j, g * P:(g + 1) * P], kst[r, b, 4 * s + g, :], qst[r, b % 4, 4 * s + g, :],
                                     start=True, stop=True)
                last.then_inc(s1_ps, 1)

            def mix1(u):
                b, s, j = u // 8, (u // 4) % 2, u % 4
                pe.wait_ge(el_ready, u + 1)
                if j == 0 and b:
                    pe.wait_ge(o1_read, 2 * b + s - 1)
                for g in range(4):
                    head = 4 * (4 * s + g) + j
                    at_ = (head - 16 * s) * VW
                    for m, e in enumerate((eh, el)):
                        last = pe.matmul(ps[:, 4 + s, at_:at_ + VW], e[:, j, g * P:(g + 1) * P], vp[:, b, head, :],
                                         start=j == 0 and g == 0 and m == 0, stop=True, skip_group_check=True)
                last.then_inc(o1_ps, 1)

            def attend1():
                nb = norms_before(2)
                last_keys(0)
                turn(nb, 4)
                last_keys(1)
                turn(nb + 1, 5)
                queries(0)
                turn(nb + 2, 6)
                last_values(0)
                last_values(1)
                queries(1)
                turn(nb + 3, 7)
                for b in range(2, B):
                    last_values(b)

                def turn_stack(b):
                    if b:
                        pe.wait_ge(qt_ready, B + b)
                    stacks(B + b, 7)

                pe.wait_ge(xl_ready, nb + PAIRS)
                turn_stack(0)
                pe.wait_ge(pre_hi, 21)
                for u in range(4):
                    scores1(u)
                mine = {"raw": queries, "turn": turn_stack}
                if blocks > 3:
                    mine["xturn"] = lambda p: turn(norms_before(3) + p, 6)
                for u in range(8 * B):
                    if u + 4 < 8 * B:
                        scores1(u + 4)
                    mix1(u)
                    between(u, mine)

            def retain():
                nb = norms_before(6)
                turn(nb, 4)
                for b in range(B):
                    if b % 2 == 0 and b < B - 2:
                        turn(nb + b // 2 + 1, 5 + b // 2)
                    pe.wait_ge(xl_ready, nb + b // 2 + 1)
                    for h in range(2):
                        for m, w in enumerate((mk_h, mk_l)):
                            last = pe.matmul(ps[:, h, 0:2 * P], w[:, h, b * P:(b + 1) * P],
                                             xs[:, h, b, :, :].rearrange("p r t -> p (r t)"),
                                             start=b == 0 and m == 0, stop=b == B - 1 and m == 1, skip_group_check=True)
                    if b == B - 1:
                        last.then_inc(a_ps, 1)
                    if b >= 2:
                        pe.wait_ge(wr_ready, b - 1)
                    product(ps[:, 2 + b % 2, 0:D], x_tile(b), weight(5)).then_inc(wg_ps, 1)
                for s in range(2):
                    for h in range(2):
                        pe.wait_ge(a_ready, h + 1)
                        pe.matmul(ps[:, 4 + 2 * s + h, :], at[:, h, :],
                                  vw[:, h, 4 * s:4 * s + 4, :].rearrange("p b e -> p (b e)"),
                                  start=True, stop=True).then_inc(o_ps, 1)
                for i in range(PAIRS + 3):
                    if i < PAIRS:
                        q = nb + PAIRS + i
                        if i >= 2:
                            pe.wait_ge(xl_ready, q - 1)
                        turn(q, i % 2, gated=True)
                    if 1 <= i <= PAIRS:
                        p = i - 1
                        pe.wait_ge(xl_ready, nb + PAIRS + p + 1)
                        pe.wait_ge(ya_ready, 4 * (p // 2) + 4)
                        for t in range(2):
                            last = product(ps[:, 4 + p, t * D:(t + 1) * D], x_tile(2 * p + t), weight(6))
                        last.then_inc(y_ps, 1)
                    if 3 <= i < PAIRS + 2 and blocks > 7:
                        turn(norms_before(7) + i - 3, 4 + i - 3)

            pe.wait_ge(ld_i, 16)
            attend0()
            if blocks > 1:
                experts(0)
            if blocks > 2:
                attend1()
            if blocks > 3:
                experts(1)
            if blocks > 4:
                attend2()
            if blocks > 5:
                experts(2)
            if blocks > 6:
                retain()
            if blocks > 7:
                experts(3)

        @block_.scalar
        def _(act):
            def high(q, p, bank):
                act.wait_ge(xt_ps, q + 1)
                act.activation(xs[:, :, 2 * p:2 * p + 2, 0, :],
                               ps[:, bank, :].rearrange("p (k t c) -> p k t c", k=K, t=2), ACT.Copy).then_inc(xh_ready, 1)

            def normal(block, p):
                r, q = PAIRS * block + p, norms_before(block) + p
                act.wait_ge(shift_ready, r + 1)
                if q >= 2:
                    act.wait_ge(xt_ps, q - 1)
                for t in range(2):
                    last = act.activation(xn[:, (2 * q + t) % 4, :], x[:, 2 * p + t, :], ACT.Identity,
                                          bias=shift[:, r % 2, t:t + 1], scale=rstd[:, r % 2, t:t + 1])
                last.then_inc(nx_ready, 1)

            def norm(block):
                normal(block, 0)
                for p in range(PAIRS):
                    if p + 1 < PAIRS:
                        normal(block, p + 1)
                    high(norms_before(block) + p, p, 4 + p)

            def split_up(n, c, i):
                f, g = FFN[n], FFN[n].base + c
                act.wait_ge(w_loaded[g % 2], after(i, 16 * (g // 2 + 1), 16))
                if g >= 2:
                    act.wait_ge(up_ps, after(i, 2 * (g - 1), 4))
                act.activation(wup_h[:, g % 2, 0:f.width - D], wraw[:, g % 2, 0:f.width - D], ACT.Copy).then_inc(wup_hi, 1)

            def split_down(n, c, i):
                f, g = FFN[n], FFN[n].base + c
                act.wait_ge(w_loaded[g % 2], after(i, 16 * (g // 2 + 1), 16))
                if g >= 2:
                    act.wait_ge(dn_ps, after(i, g - 1, 2))
                act.activation(wdn_h[:, g % 2, :], wraw[:, g % 2, f.width - D:f.width], ACT.Copy).then_inc(wdn_hi, 1)

            def gate_rows_load(n, c, i):
                f = FFN[n]
                if c < f.plain or c >= f.chunks:
                    return
                slot, j = gated(n, c) % 2, gated(n, c)
                if j >= 2:
                    g0 = f.base + c - 2 if c - 2 >= f.plain else FFN[n - 1].base + FFN[n - 1].chunks - (2 - (c - f.plain))
                    act.wait_ge(t_ready, after(i, 2 * g0 + 2, 4))
                for r, size, e in segments(n, c):
                    if i is None:
                        src = gates[n][e:e + 1, :]
                    else:
                        src = gates[n][bass.ds((4 if n == 2 else 2) * i + e, 1), :]
                    act.dma_start(gb[r:r + size, slot, :], src.broadcast_to([size, T])).then_inc(g_loaded[slot], 16)

            def activate(n, c, i):
                f, g = FFN[n], FFN[n].base + c
                for h in range(2):
                    act.wait_ge(up_ps, after(i, 2 * g + h + 1, 4))
                    if g:
                        act.wait_ge(t_ready, after(i, 2 * (g - 1) + h + 1, 4))
                    bias = 0.0
                    if f.bias:
                        bias = wraw[:, g % 2, f.width:f.width + 1]
                    act.activation(s_act[:, h, :], ps[:, 2 * h, :], f.act, bias=bias).then_inc(s_ready, 1)

            def chunk(n, c, i):
                f, g = FFN[n], FFN[n].base + c
                nxt = (n, c + 1) if c + 1 < f.chunks else (n + 1, 0)
                if c:
                    if g + 1 < CHUNKS:
                        split_up(*nxt, i)
                    activate(n, c, i)
                    if c + 1 == f.plain:
                        act.wait_ge(g_stored, 16 * (n + 1))
                    gate_rows_load(n, c + 1, i)
                last = c == f.chunks - 1
                if g + 1 < CHUNKS and not last:
                    split_down(*nxt, i)
                for h in range(2):
                    hidden = tt
                    if gated_late(n, c):
                        hidden = sg
                        act.wait_ge(sg_ready, sg_count(n, c, h))
                    else:
                        act.wait_ge(t_ready, after(i, 2 * g + h + 1, 4))
                    act.activation(th[:, g % 2, h * HALF:(h + 1) * HALF], hidden[:, h, :], ACT.Copy).then_inc(th_ready, 1)
                if g + 1 < CHUNKS and last:
                    split_down(*nxt, i)

            def experts(n):
                f = FFN[n]
                normal(2 * n + 1, PAIRS - 1)
                for h in range(2):
                    if h:
                        high(norms_before(2 * n + 1) + PAIRS - 1, PAIRS - 1, 7)
                    act.wait_ge(lt_ps, 2 * n + h + 1)
                    act.activation(lgt[0:f.gate_rows, h, :], ps[0:f.gate_rows, 4 + 2 * h, :], ACT.Copy).then_inc(lt_ready, 1)
                if n == 0:
                    stack_high(4)
                    stack_high(5)
                split_up(n, 1, None)
                for h in range(2):
                    act.wait_ge(ld_ready, 2 * n + h + 1)
                    if f.gate_rows > f.experts:
                        act.activation(le[:, h, :, f.experts:f.gate_rows], lg[:, h, :, f.experts:f.gate_rows], ACT.Exp, scale=-1.0)
                    act.activation(le[:, h, :, 0:f.experts], le[:, h, :, 0:f.experts], ACT.Exp).then_inc(le_ready, 1)
                    if n == 0:
                        key_out(4 + h)
                        stack_high(6 + h)
                if n == 0:
                    key_out(6)
                activate(n, 0, None)
                for h in range(2):
                    act.wait_ge(gt_ps, 2 * n + h + 1)
                    act.activation(gt[0:f.gate_rows, h * HALF:(h + 1) * HALF], ps[0:f.gate_rows, 4 + 2 * h, :],
                                   ACT.Copy).then_inc(gt_ready, 1)
                if n == 0:
                    key_out(7)
                act.wait_ge(gt_ready, 2 * n + 2)
                act.dma_start(gates[n], gt[0:f.gate_rows, :]).then_inc(g_stored, 16)
                if f.plain == 0:
                    act.wait_ge(g_stored, 16 * (n + 1))
                    for c in (0, 1):
                        gate_rows_load(n, c, None)
                every_chunk(act, n, chunk)

            def key_out(z):
                stack_out(z, ps16[:, key_bank(z), :], kst[:, z, :, :])

            def exponentials0(p):
                for b in (2 * p, 2 * p + 1):
                    act.wait_ge(negm_ready, b + 1)
                    act.activation(ex[:, b % 2, :], sc[:, b % 2, :], ACT.Exp, bias=negm[:, b % 2:b % 2 + 1]).then_inc(ex_ready, 1)

            def attend0():
                heads = lambda a: a.rearrange("p (n d) -> p n d", d=HD1)

                def keys_values(b):
                    act.wait_ge(v_ps, b + 1)
                    raw(b, ps[:, 2 + b % 2, 0:D])
                    act.activation(vp[:, b, :, 0:HD1], heads(ps[:, 2 + b % 2, D:2 * D]), ACT.Copy).then_inc(v1_ready, 1)

                for p in range(PAIRS):
                    if p != 2:
                        keys_values(2 * p)
                        keys_values(2 * p + 1)
                    act.wait_ge(ept_ps, 2 * p + 2)
                    if p:
                        act.wait_ge(av_ps, 2 * p)
                    act.activation(ept[:, :, :], ps[:, 4 + (p + 1) % PAIRS, 0:2 * P].rearrange("p (t c) -> p t c", t=2),
                                   ACT.Copy).then_inc(ept_ready, 2)
                    if p and blocks > 1:
                        normal(1, p - 1)
                    for b in (2 * p, 2 * p + 1):
                        act.wait_ge(r1_ready, b + 1)
                        act.activation(vp[:, b, :, HD1:2 * HD1], heads(vres[:, b % 2, 0, :]), ACT.Copy).then_inc(v2_ready, 1)
                    if p and blocks > 1:
                        high(norms_before(1) + p - 1, p - 1, 4 + p - 1)
                    if p + 1 < PAIRS:
                        exponentials0(p + 1)
                    if p == 1:
                        stack_high(0)
                        for z in range(1, 4):
                            stack_high(z)
                            key_out(z - 1)
                            if z < 3:
                                keys_values(3 + z)
                        key_out(3)

            def attend2():
                norm(4)
                for p in range(PAIRS):
                    act.wait_ge(negm_ready, B + p + 1)
                    act.wait_ge(ept_ps, B + 2 * p)
                    for t in range(2):
                        b = 2 * p + t
                        act.activation(ex[:, t, :], sc[:, t, :], ACT.Exp, bias=negm[:, t:t + 1],
                                       accum_out=esum[:, b:b + 1]).then_inc(ex_ready, 1)
                    act.wait_ge(ept_ps, B + 2 * p + 2)
                    act.wait_ge(av_ps, B + 2 * p)
                    act.activation(ept[:, :, :], ps[:, 2 + p % 2, 0:2 * P].rearrange("p (t c) -> p t c", t=2),
                                   ACT.Copy).then_inc(ept_ready, 2)
                    if p and blocks > 5:
                        normal(5, p - 1)
                        high(norms_before(5) + p - 1, p - 1, 4 + p - 1)

            def raw(z, src):
                act.wait_ge(qk_ps, z + 1)
                if z >= 4:
                    act.wait_ge(st_lo, z - 3)
                act.activation(qf[:, z % 4, :], src, ACT.Copy)
                if z >= 2:
                    act.wait_ge(ss_read, z - 1)
                act.activation(sq[:, z % 2, :], src, ACT.Square).then_inc(qk_sq, 1)

            def stack_high(z):
                act.wait_ge(qn_ready, z + 1)
                if z >= 2:
                    act.wait_ge(qt_ps, z - 1)
                for r in ((0, 2) if z < B else (0, 1)):
                    last = act.activation(stk[:, z % 2, :, r, :], qf[:, z % 4, :].rearrange("p (n d) -> p n d", d=HD1), ACT.Copy)
                last.then_inc(st_hi, 1)

            def stack_out(z, src, dst):
                act.wait_ge(qt_ps, z + 1)
                if z >= B + 4:
                    act.wait_ge(s1_ps, 8 * (z - B - 4) + 8)
                act.activation(dst.rearrange("p g t -> p (g t)"), src, ACT.Copy).then_inc(qt_ready, 1)

            def attend1():
                nb = norms_before(2)
                normal(2, 0)
                for m in range(4):
                    act.wait_ge(pre_ps, 10 + m)
                    act.activation(mk_h[:, m // 2, (m % 2) * HALF:(m % 2 + 1) * HALF], ps[:, m, :], ACT.Copy).then_inc(pre_hi, 1)
                    if m == 1:
                        normal(2, 1)
                        high(nb, 0, 4)
                        normal(2, 2)

                def last_values(b):
                    act.wait_ge(pre_ps, 14 + b)
                    act.activation(vw[:, :, b, :], ps[:, b % 4, :].rearrange("p (h e) -> p h e", h=2)[:, :, P:2 * P],
                                   ACT.Copy).then_inc(pre_hi, 1)

                def queries(r):
                    act.wait_ge(qk_ps, B + r + 1)
                    act.wait_ge(st_lo, B if r < 2 else B + 2 * r - 2)
                    src = ps[:, 4 + min(r, 2), :].rearrange("p (t d) -> p t d", t=2)
                    act.activation(qf[:, 2 * (r % 2):2 * (r % 2) + 2, :], src, ACT.Copy)
                    act.wait_ge(ss_read, B + r)
                    act.activation(sq[:, :, :], src, ACT.Square).then_inc(qk_sq, 1)

                high(nb + 1, 1, 5)
                normal(2, 3)
                queries(0)
                high(nb + 2, 2, 6)
                last_values(0)
                last_values(1)
                queries(1)
                high(nb + 3, 3, 7)
                for b in range(2, B):
                    last_values(b)
                out = lambda b: stack_out(B + b, ps16[:, 7, :], qst[:, b % 4, :, :])
                stack_high(B)
                stack_high(B + 1)
                out(0)
                mine = {"raw_copy": queries, "high": lambda b: stack_high(B + b), "out": out}
                if blocks > 3:
                    mine["xnormal"] = lambda p: normal(3, p)
                    mine["xhigh"] = lambda p: high(norms_before(3) + p, p, 6)
                for u in range(8 * B):
                    act.wait_ge(s1_ps, u + 1)
                    if u >= 4:
                        act.wait_ge(el_ready, u - 3)
                    act.activation(e1[:, u % 4, :], ps[:, u % 4, :], ACT.Exp, scale=HD1 ** -0.5).then_inc(e1_ready, 1)
                    between(u, mine)

            def retain():
                nb = norms_before(6)
                normal(6, 0)
                normal(6, 1)
                high(nb, 0, 4)
                for b in range(B):
                    if b % 2 == 0 and b < B - 4:
                        normal(6, b // 2 + 2)
                    if b % 2 == 0 and b < B - 2:
                        high(nb + b // 2 + 1, b // 2 + 1, 5 + b // 2)
                    act.wait_ge(wg_ps, b + 1)
                    act.activation(wr[:, b, :], ps[:, 2 + b % 2, 0:D], ACT.Relu).then_inc(wr_ready, 1)
                for b in range(B):
                    act.wait_ge(nm3_ready, b // 4 + 1)
                    src = ps[:, 4 + 2 * (b // 4):6 + 2 * (b // 4), (b % 4) * P:(b % 4 + 1) * P]
                    act.activation(ya[:, b, :].rearrange("p (h e) -> p h e", h=2), src, ACT.Identity,
                                   bias=nm3[:, b:b + 1], scale=rs3[:, b:b + 1]).then_inc(ya_ready, 1)
                for i in range(PAIRS + 3):
                    if i < PAIRS:
                        high(nb + PAIRS + i, i, i % 2)
                    if 2 <= i < PAIRS + 1 and blocks > 7:
                        normal(7, i - 2)
                    if 3 <= i < PAIRS + 2 and blocks > 7:
                        high(norms_before(7) + i - 3, i - 3, 4 + i - 3)

            def split_high(n):
                wait, dst, src = SPLITS(ld_w, ld_c, ld_s, craw, sraw, ch, sw_h)[n]
                act.wait_ge(wait, 16)
                act.activation(dst, src, ACT.Copy).then_inc(split_hi, 1)

            def keys0(m):
                act.wait_ge(pre_ps, m + 1)
                act.activation(mk_h[:, m % 2, (m // 2) * HALF:(m // 2 + 1) * HALF], ps[:, m, :], ACT.Copy).then_inc(pre_hi, 1)

            normal(0, 0)
            normal(0, 1)
            high(0, 0, 4)
            normal(0, 2)
            for n in range(3):
                split_high(n)
            high(1, 1, 5)
            normal(0, 3)
            act.wait_ge(ld_m, LD_M)
            act.activation(cwork[:, 0:1], cvec[:, 2:3], ACT.Exp, scale=-1.0)
            act.activation(cwork[:, 1:2], cvec[:, 3:4], ACT.Exp).then_inc(coef_exp, 1)
            split_high(3)
            keys0(0)
            keys0(1)
            high(2, 2, 6)
            high(3, 3, 7)
            keys0(2)
            keys0(3)
            exponentials0(0)
            split_high(4)
            for p in range(PAIRS):
                act.wait_ge(pre_ps, 5 + p)
                act.activation(vw0[:, 2 * p:2 * p + 2, :], ps[:, 4 + p, :].rearrange("p (t d) -> p t d", t=2), ACT.Copy).then_inc(pre_hi, 1)
            act.wait_ge(pre_ps, 9)
            act.activation(g_h[:, :, :], ps[:, 4, 0:2 * P].rearrange("p (h d) -> p h d", h=2), ACT.Copy).then_inc(pre_hi, 1)
            if blocks > 1:
                split_up(0, 0, None)
                split_down(0, 0, None)
            attend0()
            if blocks > 1:
                experts(0)
            if blocks > 2:
                attend1()
            if blocks > 3:
                act.wait_ge(o1_ps, 8 * B)
                act.dma_start(cn[:, :, :], ctx_n.rearrange("b p d -> p b d")).then_inc(ld_n, 16)
                experts(1)
            if blocks > 4:
                attend2()
            if blocks > 5:
                experts(2)
            if blocks > 6:
                retain()
            if blocks > 7:
                experts(3)

        @block_.vector
        def _(dve):
            steps = [0]

            def step(instruction):
                instruction.then_inc(dve_step, 1)
                steps[0] += 1
                return steps[0]

            def stats(block, p):
                r = PAIRS * block + p
                if block:
                    dve.wait_ge(x_added, r - PAIRS + 1)
                if r >= 2:
                    dve.wait_ge(shift_ready, r - 1)
                for t in range(2):
                    n = step(dve.bn_stats(stat[:, r % 2, t, :], x[:, 2 * p + t, :]))
                dve.wait_ge(dve_step, n)
                for t in range(2):
                    n = step(dve.bn_aggr(mv[:, r % 2, t, :], stat[:, r % 2, t, :]))
                dve.wait_ge(dve_step, n)
                dve.tensor_scalar(nmean[:, r % 2, :], mv[:, r % 2, :, 0], -1.0, None, ALU.mult)
                dve.tensor_scalar(var_eps[:, r % 2, :], mv[:, r % 2, :, 1], LN_EPS, None, ALU.add).then_inc(mv_ready, 1)

            def low(q, p, bank):
                dve.wait_ge(xh_ready, q + 1)
                dve.tensor_tensor(xs[:, :, 2 * p:2 * p + 2, 1, :],
                                  ps[:, bank, :].rearrange("p (k t c) -> p k t c", k=K, t=2),
                                  xs[:, :, 2 * p:2 * p + 2, 0, :].bitcast(F32), ALU.subtract).then_inc(xl_ready, 1)

            def add_bank(block, p):
                if block in (1, 3, 5, 7) and p == PAIRS - 1:
                    f = FFN[block // 2]
                    dve.wait_ge(dn_ps, f.base + f.chunks)
                else:
                    dve.wait_ge(y_ps, {1: 0, 3: 3, 5: 6, 6: 9, 7: 13}[block] + p + 1)
                xp = x[:, 2 * p:2 * p + 2, :].rearrange("p t d -> p (t d)")
                dve.tensor_tensor(xp, ps[:, 4 + p, :], xp, ALU.add).then_inc(x_added, 1)

            def add_scaled(block, p):
                o = 0 if block == 0 else B
                dve.wait_ge(av_ps, o + 2 * p + 2)
                for t in range(2):
                    b = 2 * p + t
                    last = dve.scalar_tensor_tensor(x[:, b, :], ps[:, 4 + p, t * D:(t + 1) * D], rsum[:, b:b + 1],
                                                    x[:, b, :], ALU.mult, ALU.add)
                last.then_inc(x_added, 1)

            def boundary(block, add, also=None):
                nb = norms_before(block + 1)
                if block + 1 >= blocks:
                    for p in range(PAIRS):
                        add(block, p)
                    return
                for i in range(PAIRS + 2):
                    if i < PAIRS:
                        add(block, i)
                        stats(block + 1, i)
                    if i >= 2:
                        low(nb + i - 2, i - 2, 4 + i - 2)
                    if also:
                        also(i)

            def rsqrt(v, y, a, b_, minus_half):
                n = step(dve.tensor_scalar(a.bitcast(I32), v.bitcast(I32), 1, None, ALU.logical_shift_right))
                step(dve.tensor_scalar(minus_half, v, -0.5, None, ALU.mult))
                dve.wait_ge(dve_step, n)
                n = step(dve.tensor_scalar(y.bitcast(I32), a.bitcast(I32), -1.0, float(0x5F3759DF), ALU.mult, ALU.add))
                for _ in range(3):
                    dve.wait_ge(dve_step, n)
                    n = step(dve.tensor_tensor(a, y, y, ALU.mult))
                    dve.wait_ge(dve_step, n)
                    n = step(dve.tensor_tensor(b_, a, minus_half, ALU.mult))
                    dve.wait_ge(dve_step, n)
                    n = step(dve.scalar_tensor_tensor(y, b_, 1.5, y, ALU.add, ALU.mult))
                dve.wait_ge(dve_step, n)

            def front0(p):
                pair, n = (0, 1), [0, 0]
                s, w, m = sc, work, top
                for t in pair:
                    b = 2 * p + t
                    dve.wait_ge(sc_ps, b + 1)
                    if b >= 2:
                        dve.wait_ge(ex_ready, b - 1)
                    dve.tensor_scalar(s[:, t, :], ps[:, t, t * P:(t + 1) * P], cwork[:, 7:8], None, ALU.mult).then_inc(sc_read, 1)
                for t in pair:
                    dve.wait_ge(sc_read, 2 * p + t + 1)
                    n[t] = step(dve.max(m[:, t, 0:8], s[:, t, :]))
                for t in pair:
                    dve.wait_ge(dve_step, n[t])
                    dve.tensor_scalar(negm[:, t:t + 1], m[:, t, 0:1], -1.0, None, ALU.mult).then_inc(negm_ready, 1)
                for r in range(1, (CLIP + 7) // 8):
                    for t in pair:
                        dve.wait_ge(dve_step, n[t])
                        n[t] = step(dve.match_replace(w[:, t, :], m[:, t, 8 * r - 8:8 * r], (s if r == 1 else w)[:, t, :], NEG))
                    for t in pair:
                        dve.wait_ge(dve_step, n[t])
                        n[t] = step(dve.max(m[:, t, 8 * r:8 * r + 8], w[:, t, :]))
                for t in pair:
                    b = 2 * p + t
                    dve.wait_ge(dve_step, n[t])
                    dve.wait_ge(ex_ready, b + 1)
                    if b >= 2:
                        dve.wait_ge(ept_ps, b - 1)
                    n[t] = step(dve.scalar_tensor_tensor(ep[:, t, :], s[:, t, :], m[:, t, CLIP - 1:CLIP], ex[:, t, :],
                                                         ALU.is_ge, ALU.mult))
                for t in pair:
                    dve.wait_ge(dve_step, n[t])
                    n[t] = step(dve.tensor_reduce(esum[:, 2 * p + t:2 * p + t + 1], ep[:, t, :], AX.X, ALU.add))
                for t in pair:
                    b = 2 * p + t
                    dve.wait_ge(dve_step, n[t])
                    dve.reciprocal(rsum[:, b:b + 1], esum[:, b:b + 1]).then_inc(ep_ready, 1)

            def attend0():
                nb = norms_before(1)
                heads = lambda a: a.rearrange("p (n d) -> p n d", d=HD1)
                for p in range(PAIRS):
                    front0(p)
                    if p == 0:
                        dve.wait_ge(pre_hi, 9)
                        dve.tensor_tensor(g_l[:, :, :], ps[:, 4, 0:2 * P].rearrange("p (h d) -> p h d", h=2),
                                          g_h[:, :, :].bitcast(F32), ALU.subtract).then_inc(pre_lo, 1)
                        if blocks > 1:
                            low_up(0, 0, None)
                            low_down(0, 0, None)
                    if p:
                        add_scaled(0, p - 1)
                        if blocks > 1:
                            stats(1, p - 1)
                    for b in (2 * p, 2 * p + 1):
                        squares(b)
                        dve.wait_ge(v1_ready, b + 1)
                        if b >= 2:
                            dve.wait_ge(v3_ready, b - 1)
                        dve.tensor_tensor(heads(vres[:, b % 2, 0, :]), heads(ps[:, 2 + b % 2, D:2 * D]), vp[:, b, :, 0:HD1],
                                          ALU.subtract).then_inc(r1_ready, 1)
                    if p == 1:
                        scales(4)
                        for z in range(4):
                            scaled(z)
                    if p >= 2 and blocks > 1:
                        low(nb + p - 2, p - 2, 4 + p - 2)
                add_scaled(0, PAIRS - 1)
                if blocks > 1:
                    stats(1, PAIRS - 1)
                    low(nb + PAIRS - 2, PAIRS - 2, 4 + PAIRS - 2)
                    low(nb + PAIRS - 1, PAIRS - 1, 4 + PAIRS - 1)
                    scales(B)
                    for z in range(4, 8):
                        scaled(z)

            def front2(p):
                dve.wait_ge(sc_ps, B + p + 1)
                dve.wait_ge(ex_ready, B + 2 * p)
                src = ps[:, 0:3, :].rearrange("p b c -> p (b c)")[:, 0:2 * (2 * D + P)].rearrange(
                    "p (t c) -> p t c", t=2)[:, :, 0:P]
                two = slice(2 * p, 2 * p + 2)
                dve.scalar_tensor_tensor(work[:, :, :], src, D ** -0.5, maskf[:, two, :], ALU.mult, ALU.mult).then_inc(sc_read, 1)
                dve.wait_ge(sc_read, B + p + 1)
                n = step(dve.tensor_tensor(sc[:, :, :], work[:, :, :], maskb[:, two, :], ALU.add))
                dve.wait_ge(dve_step, n)
                dve.tensor_reduce(negm[:, :], sc[:, :, :], AX.X, ALU.max, negate=True).then_inc(negm_ready, 1)

            def scale2(p):
                dve.wait_ge(ex_ready, B + 2 * p + 2)
                two = slice(2 * p, 2 * p + 2)
                n = step(dve.reciprocal(rsum[:, two], esum[:, two]))
                dve.wait_ge(dve_step, n)
                n = step(dve.tensor_tensor(rsum[:, two], rsum[:, two], valid[:, two], ALU.mult))
                dve.wait_ge(dve_step, n)

            def low_up(n, c, i):
                f, g = FFN[n], FFN[n].base + c
                dve.wait_ge(wup_hi, after(i, g + 1, 2))
                u = f.width - D
                dve.tensor_tensor(wup_l[:, g % 2, 0:u], wraw[:, g % 2, 0:u], wup_h[:, g % 2, 0:u].bitcast(F32),
                                  ALU.subtract).then_inc(wup_lo, 1)

            def low_down(n, c, i):
                f, g = FFN[n], FFN[n].base + c
                dve.wait_ge(wdn_hi, after(i, g + 1, 2))
                dve.tensor_tensor(wdn_l[:, g % 2, :], wraw[:, g % 2, f.width - D:f.width], wdn_h[:, g % 2, :].bitcast(F32),
                                  ALU.subtract).then_inc(wdn_lo, 1)

            def chunk(n, c, i):
                f, g = FFN[n], FFN[n].base + c
                nxt = (n, c + 1) if c + 1 < f.chunks else (n + 1, 0)
                if c and g + 1 < CHUNKS:
                    low_up(*nxt, i)
                slot = gated(n, c) % 2
                if not f.up and c >= f.plain:
                    dve.wait_ge(g_loaded[slot], after(i, 16 * g_loads(n, c), 16 * len(segments(n, f.peeled))))
                for h in range(2):
                    if g:
                        dve.wait_ge(tl_ready, after(i, 2 * (g - 1) + h + 1, 4))
                    ungated = c < f.plain or gated_late(n, c)
                    if not f.up or ungated:
                        dve.wait_ge(s_ready, after(i, 2 * g + h + 1, 4))
                    else:
                        dve.wait_ge(sg_ready, after(i, sg_count(n, c, h), 4))
                    if not f.up and c < f.plain:
                        dve.tensor_copy(tt[:, h, :], s_act[:, h, :]).then_inc(t_ready, 1)
                    elif not f.up:
                        dve.tensor_tensor(tt[:, h, :], s_act[:, h, :], gb[:, slot, h * HALF:(h + 1) * HALF],
                                          ALU.mult).then_inc(t_ready, 1)
                    else:
                        a = s_act if ungated else sg
                        dve.tensor_tensor(tt[:, h, :], a[:, h, :], ps[:, 2 * h + 1, :], ALU.mult).then_inc(t_ready, 1)
                last = c == f.chunks - 1
                if g + 1 < CHUNKS and not last:
                    low_down(*nxt, i)
                for h in range(2):
                    dve.wait_ge(th_ready, after(i, 2 * g + h + 1, 4))
                    half = slice(h * HALF, (h + 1) * HALF)
                    hidden = sg if gated_late(n, c) else tt
                    dve.tensor_tensor(tl[:, g % 2, half], hidden[:, h, :], th[:, g % 2, half].bitcast(F32),
                                      ALU.subtract).then_inc(tl_ready, 1)
                if g + 1 < CHUNKS and last:
                    low_down(*nxt, i)

            def route_max(n):
                f = FFN[n]
                e, rows_, k = f.experts, f.gate_rows, [0, 0]
                for h in range(2):
                    dve.wait_ge(lg_ps, 2 * n + h + 1)
                    src = ps[:, 5 + 2 * h, 0:4 * LP].rearrange("p (t e) -> p t e", e=LP)[:, :, 0:rows_]
                    k[h] = step(dve.tensor_copy(lg[:, h, :, 0:rows_], src))
                    dve.wait_ge(dve_step, k[h])
                    for t in range(4):
                        k[h] = step(dve.max(m8[:, h, t, :], lg[:, h, t, 0:e]))
                    dve.wait_ge(dve_step, k[h])
                    dve.tensor_tensor(le[:, h, :, 0:e], lg[:, h, :, 0:e], m8[:, h, :, 0:1].broadcast_to([P, 4, e]),
                                      ALU.subtract).then_inc(ld_ready, 1)
                    step(dve.tensor_tensor(lm[:, h, :, 0:e], lg[:, h, :, 0:e],
                                           m8[:, h, :, f.top - 1:f.top].broadcast_to([P, 4, e]), ALU.is_ge))

            def route_weights(n):
                f = FFN[n]
                e, rows_, k, both = f.experts, f.gate_rows, [0, 0], (0, 1)
                M, E, S = lm, le, gsum
                start = steps[0]
                for h in both:
                    dve.wait_ge(dve_step, start)
                    dve.wait_ge(le_ready, 2 * n + h + 1)
                    k[h] = step(dve.tensor_tensor(M[:, h, :, 0:e], M[:, h, :, 0:e], E[:, h, :, 0:e], ALU.mult))
                    if rows_ > e:
                        step(dve.tensor_scalar(S[:, h, 8:12], E[:, h, :, e], 1.0, None, ALU.add))
                for h in both:
                    dve.wait_ge(dve_step, k[h])
                    k[h] = step(dve.tensor_reduce(S[:, h, 0:4], M[:, h, :, 0:e], AX.X, ALU.add))
                for h in both:
                    dve.wait_ge(dve_step, k[h])
                    k[h] = step(dve.reciprocal(S[:, h, 4:8], S[:, h, 0:4]))
                    if rows_ > e:
                        k[h] = step(dve.reciprocal(M[:, h, :, e], S[:, h, 8:12]))
                for h in both:
                    dve.wait_ge(dve_step, k[h])
                    dve.tensor_tensor(M[:, h, :, 0:e], M[:, h, :, 0:e], S[:, h, 4:8].unsqueeze(2).broadcast_to([P, 4, e]),
                                      ALU.mult).then_inc(gw_ready, 1)

            def experts(n):
                if n == 0:
                    k = step(dve.memset(gt[0:FFN[0].experts + 1, :], 1.0))
                route_max(n)
                low_up(n, 1, None)
                route_weights(n)
                every_chunk(dve, n, chunk)
                boundary(2 * n + 1, add_bank, prepare1 if n == 0 else None)

            def squares(z):
                dve.wait_ge(qk_sq, z + 1)
                dve.tensor_reduce(ss[:, z % 4, :], sq[:, z % 2, :].rearrange("p (n d) -> p n d", d=HD1),
                                  AX.X, ALU.add).then_inc(ss_read, 1)

            def scales(count):
                dve.wait_ge(ss_read, count)
                flat = lambda a: a[:, :, :].rearrange("p t n -> p (t n)")
                n = step(dve.tensor_scalar(flat(ss), flat(ss), 1.0 / HD1, RMS_EPS, ALU.mult, ALU.add))
                dve.wait_ge(dve_step, n)
                rsqrt(flat(ss), flat(nw_y), flat(nw_a), flat(nw_b), flat(nw_h))

            def scaled(z):
                heads = lambda a: a.rearrange("p (n d) -> p n d", d=HD1)
                dve.tensor_tensor(heads(qf[:, z % 4, :]), heads(qf[:, z % 4, :]),
                                  nw_y[:, z % 4, :].unsqueeze(2).broadcast_to([P, HEADS1, HD1]), ALU.mult).then_inc(qn_ready, 1)

            def squares2(r):
                dve.wait_ge(qk_sq, B + r + 1)
                dve.tensor_reduce(ss[:, 2 * (r % 2):2 * (r % 2) + 2, :], sq[:, :, :].rearrange("p t (n d) -> p t n d", d=HD1),
                                  AX.X, ALU.add).then_inc(ss_read, 1)

            def stack_low(z):
                dve.wait_ge(st_hi, z + 1)
                for r in (2, 3):
                    last = dve.tensor_tensor(stk[:, z % 2, :, r, :], qf[:, z % 4, :].rearrange("p (n d) -> p n d", d=HD1),
                                             stk[:, z % 2, :, 0, :], ALU.subtract)
                last.then_inc(st_lo, 1)

            def mixed(w):
                s = w % 2
                dve.wait_ge(o1_ps, 4 * w + 4)
                if w >= 2:
                    dve.wait_ge(oy_ready, w - 1)
                src = ps[:, 4 + s, 0:16 * VW].rearrange("p (n c) -> p n c", c=VW)
                parts = src[:, :, 0:3 * HD1].rearrange("p n (r d) -> p n d r", d=HD1)
                dve.tensor_reduce(o3[:, s, :, :], parts, AX.X, ALU.add)
                dve.reciprocal(r3[:, s, :], src[:, :, 3 * HD1]).then_inc(o1_read, 1)

            def last_keys(m):
                dve.wait_ge(pre_hi, 10 + m)
                half = slice((m % 2) * HALF, (m % 2 + 1) * HALF)
                dve.tensor_tensor(mk_l[:, m // 2, half], ps[:, m, :], mk_h[:, m // 2, half].bitcast(F32),
                                  ALU.subtract).then_inc(pre_lo, 1)

            def prepare1(i):
                if 1 <= i <= 4:
                    last_keys(i - 1)
                if i == 4:
                    squares2(0)

            def attend1():
                nb = norms_before(3)
                squares2(1)
                scales(B + 2)
                for b in range(4):
                    scaled(B + b)
                stack_low(B)
                mine = {"squares": squares2, "scale": lambda g: scales(B + 4), "rows": lambda b: scaled(B + b),
                        "low": lambda b: stack_low(B + b)}
                if blocks > 3:
                    mine.update(stats=lambda p: stats(3, p), xlow=lambda p: low(nb + p, p, 6))
                for u in range(8 * B):
                    dve.wait_ge(eh_ready, u + 1)
                    dve.tensor_tensor(el[:, u % 4, :], e1[:, u % 4, :], eh[:, u % 4, :], ALU.subtract).then_inc(el_ready, 1)
                    if u % 4 == 1 and u > 4:
                        mixed(u // 4 - 1)
                    between(u, mine)
                mixed(2 * B - 1)
                if blocks > 3:
                    stats(3, PAIRS - 1)
                    low(nb + PAIRS - 1, PAIRS - 1, 7)

            def retain():
                nb = norms_before(6)
                dve.wait_ge(a_ps, 1)
                for h in range(2):
                    n = step(dve.tensor_copy(a1[:, h, :], ps[:, h, 0:P]))
                    dve.wait_ge(dve_step, n)
                    n = step(dve.tensor_tensor(a1[:, h, :], ps[:, h, P:2 * P], a1[:, h, :], ALU.add))
                    dve.wait_ge(dve_step, n)
                    n = step(dve.tensor_tensor(a1[:, h, :], a1[:, h, :], dec[:, h, :], ALU.mult))
                    dve.wait_ge(dve_step, n)
                    n = step(dve.scalar_tensor_tensor(at[:, h, :], a1[:, h, :], -1.0, a1[:, h, :], ALU.mult, ALU.max))
                    dve.wait_ge(dve_step, n)
                    dve.tensor_scalar(at[:, h, :], at[:, h, :], 1.0, None, ALU.max).then_inc(a_ready, 1)
                for s in range(2):
                    four = slice(4 * s, 4 * s + 4)
                    dve.wait_ge(o_ps, 2 * s + 2)
                    for b in range(4 * s, 4 * s + 4):
                        for h in range(2):
                            n = step(dve.bn_stats(st3[:, b, h, :], ps[:, 4 + 2 * s + h, (b % 4) * P:(b % 4 + 1) * P]))
                    dve.wait_ge(dve_step, n)
                    for b in range(4 * s, 4 * s + 4):
                        n = step(dve.bn_aggr(mv3[:, b, :], st3[:, b, :, :].rearrange("p h s -> p (h s)")))
                    dve.wait_ge(dve_step, n)
                    dve.tensor_scalar(ve3[:, four], mv3[:, four, 1], GN_EPS, None, ALU.add).then_inc(mv3_ready, 1)
                for s in range(2):
                    four = slice(4 * s, 4 * s + 4)
                    dve.wait_ge(rs3_ready, s + 1)
                    dve.scalar_tensor_tensor(nm3[:, four], mv3[:, four, 0], -1.0, rs3[:, four],
                                             ALU.mult, ALU.mult).then_inc(nm3_ready, 1)

                def finish(p):
                    q = nb + PAIRS + p
                    two = slice(2 * p, 2 * p + 2)
                    dve.wait_ge(ya_ready, 2 * p + 2)
                    dve.wait_ge(wg_ready, 2 * p + 2)
                    n = step(dve.tensor_tensor(ya[:, two, :], ya[:, two, :], wr[:, two, :], ALU.mult))
                    dve.wait_ge(dve_step, n)
                    dve.wait_ge(xt_ps, q - 1)
                    xp = 2 * (q % 2)
                    dve.tensor_tensor(xn[:, xp:xp + 2, :], ya[:, two, :], wb[:, two, :], ALU.add).then_inc(xn_ready, 1)

                for i in range(PAIRS + 4):
                    if i < PAIRS:
                        finish(i)
                    if 1 <= i <= PAIRS:
                        low(nb + PAIRS + i - 1, i - 1, (i - 1) % 2)
                    if 2 <= i <= PAIRS + 1:
                        add_bank(6, i - 2)
                        if blocks > 7:
                            stats(7, i - 2)
                    if i >= 4 and blocks > 7:
                        low(norms_before(7) + i - 4, i - 4, 4 + i - 4)

            def split_low(n):
                _, dst, src = SPLITS(ld_w, ld_c, ld_s, craw, sraw, cl, sw_l)[n]
                hi = SPLITS(ld_w, ld_c, ld_s, craw, sraw, ch, sw_h)[n][1]
                dve.wait_ge(split_hi, n + 1)
                dve.tensor_tensor(dst, src, hi.bitcast(F32), ALU.subtract).then_inc(split_lo, 1)

            def keys0(m):
                dve.wait_ge(pre_hi, m + 1)
                half = slice((m // 2) * HALF, (m // 2 + 1) * HALF)
                dve.tensor_tensor(mk_l[:, m % 2, half], ps[:, m, :], mk_h[:, m % 2, half].bitcast(F32),
                                  ALU.subtract).then_inc(pre_lo, 1)

            dve.wait_ge(ld_x, 16)
            for p in range(3):
                stats(0, p)
            low(0, 0, 4)
            stats(0, 3)
            for n in range(3):
                split_low(n)
            low(1, 1, 5)
            dve.wait_ge(coef_exp, 1)
            n = step(dve.tensor_scalar(cwork[:, 2:3], cwork[:, 0:1], 1.0, None, ALU.add))
            dve.wait_ge(dve_step, n)
            n = step(dve.reciprocal(cwork[:, 3:4], cwork[:, 2:3]))
            n = step(dve.tensor_tensor(cwork[:, 4:5], cvec[:, 0:1], cvec[:, 1:2], ALU.subtract))
            dve.wait_ge(dve_step, n)
            n = step(dve.scalar_tensor_tensor(cwork[:, 5:6], cwork[:, 4:5], cwork[:, 3:4], cvec[:, 1:2], ALU.mult, ALU.add))
            dve.wait_ge(dve_step, n)
            n = step(dve.tensor_scalar(cwork[:, 7:8], cwork[:, 5:6], cwork[:, 1:2], D ** -0.5, ALU.mult, ALU.mult))
            dve.wait_ge(dve_step, n)
            keys0(0)
            keys0(1)
            low(2, 2, 6)
            low(3, 3, 7)
            keys0(2)
            keys0(3)
            attend0()
            if blocks > 1:
                experts(0)
            if blocks > 2:
                attend1()
            if blocks > 3:
                experts(1)
            if blocks > 4:
                dve.tensor_copy(maskf[:, :, :], masku[:, :, :]).then_inc(mask_ready, 1)
                dve.wait_ge(mask_ready, 1)
                dve.tensor_scalar(maskb[:, :, :], maskf[:, :, :], -1.0, 1e30, ALU.add, ALU.mult).then_inc(mask_ready, 1)
                dve.tensor_reduce(valid[:, :], maskf[:, :, :], AX.X, ALU.max).then_inc(mask_ready, 1)
                dve.wait_ge(mask_ready, 3)
                nb = norms_before(5)
                front2(0)
                front2(1)
                for p in range(PAIRS):
                    scale2(p)
                    add_scaled(4, p)
                    if blocks > 5:
                        stats(5, p)
                    if p + 2 < PAIRS:
                        front2(p + 2)
                    if p and blocks > 5:
                        low(nb + p - 1, p - 1, 4 + p - 1)
                if blocks > 5:
                    low(nb + PAIRS - 1, PAIRS - 1, 4 + PAIRS - 1)
            if blocks > 5:
                experts(2)
            if blocks > 6:
                retain()
            if blocks > 7:
                experts(3)

def pack_small(mats, gates, wh):
    import numpy as np
    cols = [m[k * P:(k + 1) * P] for m in mats for k in range(K)]
    cols += [g[k * P:(k + 1) * P] for g in gates for k in range(K)]
    cols += [wh[h] for h in range(2)] + [wh[h].T for h in range(2)]
    return np.ascontiguousarray(np.concatenate(cols, axis=1))


def pack_experts(first, second, bias=None):
    import numpy as np
    chunks = second.shape[0] // P
    out = []
    for c in range(chunks):
        u = slice(c * P, (c + 1) * P)
        cols = [m[k * P:(k + 1) * P, u] for m in first for k in range(K)] + [second[u]]
        if bias is not None:
            cols.append(bias[u, None])
        out.append(np.concatenate(cols, axis=1))
    return np.ascontiguousarray(np.stack(out))


def decay_table():
    import numpy as np
    gam = 1.0 - 2.0 ** (-5.0 - np.arange(2, dtype=np.float64))
    s, t = np.arange(P)[:, None], np.arange(P)[None, :]
    d = np.where(t <= s, gam[:, None, None] ** (t - s), 0.0)
    d = d / np.sqrt(d.sum(axis=-1))[:, None, :] / np.sqrt(float(P))
    return np.ascontiguousarray(d.transpose(2, 0, 1).astype(np.float32))


def kernel(**inputs):
    import numpy as np
    import concourse.bacc as bacc
    from concourse.bass_utils import run_bass_kernel_spmd as run

    a = {k: np.asarray(v) for k, v in inputs.items()}
    cat = np.concatenate

    def units(w):
        return w.transpose(1, 0, 2).reshape(w.shape[1], -1)

    wkv = cat([a["L1_xattn_Wk"], a["L1_xattn_Wv"]], axis=0)
    small = pack_small(
        [a["L0_xattn_W_qkv"][:D], a["L0_xattn_W_o"].T, wkv[0::2].T, wkv[1::2].T, a["L1_xattn_Wq"].T,
         a["L3_xattn_wg_w"], a["L3_xattn_wo_w"]],
        [a["L0_ffn_gate_w"], a["L1_ffn_gate_w"].T,
         cat([a["L2_ffn_router_w"], a["L2_ffn_shared_expert_gate_w"]], axis=0).T, a["L3_ffn_w_gate"]],
        a["L3_xattn_Wh"])

    w0 = pack_experts([cat([a["L0_ffn_shared_w1"], units(a["L0_ffn_w1"])], axis=1)],
                      cat([a["L0_ffn_shared_w2"], a["L0_ffn_w2"].reshape(-1, D)], axis=0),
                      cat([a["L0_ffn_shared_b1"], a["L0_ffn_b1"].reshape(-1)]))
    b2 = cat([a["L0_ffn_b2"], a["L0_ffn_shared_b2"][None]], axis=0)

    def first1(shared, w):
        zero = np.zeros((D, 3 * P - shared.shape[1]), np.float32)
        return cat([shared, zero, units(w[:, :, P:]), units(w[:, :, :P])], axis=1)

    zero = np.zeros((3 * P - 2 * I1, D), np.float32)
    w1 = pack_experts([first1(a["L1_ffn_sw1"], a["L1_ffn_w1"]), first1(a["L1_ffn_sw3"], a["L1_ffn_w3"])],
                      cat([a["L1_ffn_sw2"], zero, a["L1_ffn_w2"][:, P:].reshape(-1, D), a["L1_ffn_w2"][:, :P].reshape(-1, D)], axis=0))

    gu, zero = a["L2_ffn_gate_up_proj"], np.zeros((64, D), np.float32)
    w2 = pack_experts([cat([a["L2_ffn_shared_gate_w"], zero, gu[:, :64].reshape(-1, D)], axis=0).T,
                       cat([a["L2_ffn_shared_up_w"], zero, gu[:, 64:].reshape(-1, D)], axis=0).T],
                      cat([a["L2_ffn_shared_down_w"].T, zero, a["L2_ffn_down_proj"].transpose(0, 2, 1).reshape(-1, D)], axis=0))

    gu, sh = a["L3_ffn_w_gate_up"], a["L3_ffn_w_sh_gate_up"]
    w3 = pack_experts([cat([sh[:, :512], units(gu[:, :, :P])], axis=1), cat([sh[:, 512:], units(gu[:, :, P:])], axis=1)],
                      cat([a["L3_ffn_w_sh_down"], a["L3_ffn_w_down"].reshape(-1, D)], axis=0))

    arrays = {
        "x_in": a["x"], "ctx_t": np.ascontiguousarray(a["ctx_2048"].reshape(T, D).T), "ctx_n": a["ctx_2048"],
        "mask_in": a["mask_BxS2_bk0"], "small_in": small,
        "coef_in": np.stack([a["L0_xattn_beta_q"], a["L0_xattn_beta_k"], a["L0_xattn_gate"], a["L0_xattn_log_tau"]]),
        "b2_in": b2, "gamma_in": a["L3_xattn_gn_gamma"], "beta_in": a["L3_xattn_gn_beta"],
        "decay_in": decay_table(), "ident_in": np.eye(P, dtype=np.float32),
        "w0_in": w0, "w1_in": w1, "w2_in": w2, "w3_in": w3,
    }
    arrays = {k: np.ascontiguousarray(v) for k, v in arrays.items()}
    nc = bacc.Bacc("TRN2", target_bir_lowering=False, num_devices=1)
    ap = {k: nc.dram_tensor(k, v.shape, mybir.dt.from_np(v.dtype), kind="ExternalInput").ap() for k, v in arrays.items()}
    ws = [ap.pop(f"w{n}_in") for n in range(4)]
    gates = [nc.dram_tensor(f"gates{n}", (FFN[n].gate_rows, T), F32, kind="Internal").ap() for n in range(4)]
    out = nc.dram_tensor("y_out", (B, P, D), F32, kind="ExternalOutput").ap()
    program(nc, **ap, w_in=ws, gates=gates, out=out, blocks=BLOCKS)
    r = run(nc, [arrays], core_ids=[0])
    return r.results[0]["y_out"]
```
